# Optimizing a Trainium2 kernel written in Bass

```python
import numpy as np
import jax
import jax.numpy as jnp

def _softmax(x, axis=-1):
    return jax.nn.softmax(x, axis=axis)

def _gelu(x):
    return jax.nn.gelu(x, approximate=True)

def _silu(x):
    return jax.nn.silu(x)

def _sigmoid(x):
    return jax.nn.sigmoid(x)

def _layernorm(x, axis=-1, eps=1e-05):
    m = jnp.mean(x, axis=axis, keepdims=True)
    v = jnp.var(x, axis=axis, keepdims=True)
    return (x - m) / jnp.sqrt(v + eps)

def _scatter_add(tgt, idx, src, axis=0):
    return tgt.at[idx].add(src)

def _segment_sum(src, seg, n):
    return jax.ops.segment_sum(src, seg, n)
kernel_name = 'mk_perceiver_d1_seqx_r2_68bc5c'

def setup_inputs(seed: int=0):
    np.random.seed(seed)
    _w = jnp.asarray

    def _rec_inputs():
        import jax
        import jax.numpy as jnp
        _rk = jax.random.key(seed)
        x = -0.000125 + 0.9999 * jax.random.normal(jax.random.fold_in(_rk, 1), (8, 64, 512), jnp.float32)
        _lenS = 64 - jax.random.randint(jax.random.fold_in(_rk, 7), (8,), 0, max(1, 64 // 4) + 1, jnp.int32)
        _lenS2 = 1601 - jax.random.randint(jax.random.fold_in(_rk, 8), (8,), 0, max(1, 1601 // 4) + 1, jnp.int32)
        _ctx_1024P = jax.random.normal(jax.random.fold_in(_rk, 11), (8, 16, 512), jnp.float32)
        _ctx_1024c = jax.random.dirichlet(jax.random.fold_in(_rk, 511), 0.3 * jnp.ones((16,), jnp.float32), (8, 1601))
        _ctx_1024t = jnp.einsum('bsk,bkd->bsd', _ctx_1024c, _ctx_1024P)
        _ctx_1024t = _ctx_1024t * jax.lax.rsqrt(jnp.mean(jnp.square(_ctx_1024t)) + 1e-12) * 0.953939
        ctx_1024 = -1.52775e-05 + 0.999936 * (_ctx_1024t + 0.3 * jax.random.normal(jax.random.fold_in(_rk, 611), (8, 1601, 512), jnp.float32))
        return (x, ctx_1024)
    x, ctx_1024 = _rec_inputs()

    def _L0_xattn_setup():
        import jax, jax.numpy as jnp
        import numpy as np
        B, LP, LQ, H = (16, 1024, 1024, 512)
        key = jax.random.key(seed)
        k1, k2, k3 = jax.random.split(key, 3)
        proj_p = jax.random.normal(k1, (B, LP, H), dtype=jnp.float32)
        proj_q = jax.random.normal(k2, (B, LQ, H), dtype=jnp.float32)
        W = jax.random.normal(k3, (H, H), dtype=jnp.float32) * (1.0 / np.sqrt(H))
        b = jnp.zeros((H,), dtype=jnp.float32)
        return {'proj_p': proj_p, 'proj_q': proj_q, 'W': W, 'b': b}
    _L0_xattn_all = _L0_xattn_setup()
    _L0_xattn_in = {k: v for k, v in _L0_xattn_all.items() if k in ('W', 'b')}
    del _L0_xattn_all

    def _L0_attn_setup():
        import jax, jax.numpy as jnp
        import numpy as np
        B, S, D, H, DH, FF = (2, 2048, 512, 16, 64, 2048)

        def _ln(x, g, b):
            m = x.mean(-1, keepdims=True)
            v = ((x - m) ** 2).mean(-1, keepdims=True)
            return (x - m) * jax.lax.rsqrt(v + 1e-05) * g + b

        def _phi(x, proj):
            return jax.nn.elu(x @ proj) + 1.0
        key = jax.random.key(seed)
        ks = jax.random.split(key, 10)
        s = 0.02
        return {'x': jax.random.normal(ks[0], (B, S, D), jnp.float32), 'wq': jax.random.normal(ks[1], (D, H * DH), jnp.float32) * s, 'wk': jax.random.normal(ks[2], (D, H * DH), jnp.float32) * s, 'wv': jax.random.normal(ks[3], (D, H * DH), jnp.float32) * s, 'wo': jax.random.normal(ks[4], (H * DH, D), jnp.float32) * s, 'proj': jax.random.normal(ks[5], (DH, DH), jnp.float32) / np.sqrt(DH).astype(np.float32), 'w1': jax.random.normal(ks[6], (D, FF), jnp.float32) * s, 'b1': jnp.zeros((FF,), jnp.float32), 'w2': jax.random.normal(ks[7], (FF, D), jnp.float32) * s, 'b2': jnp.zeros((D,), jnp.float32), 'g1': jnp.ones((D,), jnp.float32), 'beta1': jnp.zeros((D,), jnp.float32), 'g2': jnp.ones((D,), jnp.float32), 'beta2': jnp.zeros((D,), jnp.float32)}
    _L0_attn_all = _L0_attn_setup()
    _L0_attn_in = {k: v for k, v in _L0_attn_all.items() if k in ('wq', 'wk', 'wv', 'wo', 'proj', 'w1', 'b1', 'w2', 'b2', 'g1', 'beta1', 'g2', 'beta2')}
    del _L0_attn_all

    def _L0_ffn_setup():
        import jax, jax.numpy as jnp
        import numpy as np
        B, S, H, F, E, K = (4, 1024, 512, 1024, 8, 2)
        key = jax.random.key(seed)
        k0, k1, k2, k3, k4 = jax.random.split(key, 5)
        return {'hidden_states': jax.random.normal(k0, (B, S, H), dtype=jnp.float32), 'w_router': jax.random.normal(k1, (H, E), dtype=jnp.float32) * 0.02, 'w0': jax.random.normal(k2, (E, H, F), dtype=jnp.float32) * 0.02, 'w1': jax.random.normal(k3, (E, H, F), dtype=jnp.float32) * 0.02, 'wo': jax.random.normal(k4, (E, F, H), dtype=jnp.float32) * 0.02}
    _L0_ffn_all = _L0_ffn_setup()
    _L0_ffn_in = {k: v for k, v in _L0_ffn_all.items() if k in ('w_router', 'w0', 'w1', 'wo')}
    del _L0_ffn_all
    return {'x': x, 'ctx_1024': ctx_1024, 'L0_xattn_W': _L0_xattn_in['W'], 'L0_xattn_b': _L0_xattn_in['b'], 'L0_attn_wq': _L0_attn_in['wq'], 'L0_attn_wk': _L0_attn_in['wk'], 'L0_attn_wv': _L0_attn_in['wv'], 'L0_attn_wo': _L0_attn_in['wo'], 'L0_attn_proj': _L0_attn_in['proj'], 'L0_attn_w1': _L0_attn_in['w1'], 'L0_attn_b1': _L0_attn_in['b1'], 'L0_attn_w2': _L0_attn_in['w2'], 'L0_attn_b2': _L0_attn_in['b2'], 'L0_attn_g1': _L0_attn_in['g1'], 'L0_attn_beta1': _L0_attn_in['beta1'], 'L0_attn_g2': _L0_attn_in['g2'], 'L0_attn_beta2': _L0_attn_in['beta2'], 'L0_ffn_w_router': _L0_ffn_in['w_router'], 'L0_ffn_w0': _L0_ffn_in['w0'], 'L0_ffn_w1': _L0_ffn_in['w1'], 'L0_ffn_wo': _L0_ffn_in['wo']}

def reference(x, ctx_1024, L0_xattn_W, L0_xattn_b, L0_attn_wq, L0_attn_wk, L0_attn_wv, L0_attn_wo, L0_attn_proj, L0_attn_w1, L0_attn_b1, L0_attn_w2, L0_attn_b2, L0_attn_g1, L0_attn_beta1, L0_attn_g2, L0_attn_beta2, L0_ffn_w_router, L0_ffn_w0, L0_ffn_w1, L0_ffn_wo):
    import jax
    import jax.numpy as jnp

    def _L0_xattn_ref(proj_p, proj_q, W, b):
        import jax, jax.numpy as jnp
        import numpy as np
        B, LP, LQ, H = (16, 1024, 1024, 512)
        trans_q = jnp.einsum('bqh,oh->bqo', proj_q, W) + b
        att_weights = jnp.einsum('bph,bqh->bpq', proj_p, trans_q)
        att_norm = jax.nn.softmax(att_weights, axis=-1)
        att_vec = jnp.einsum('bpq,bqh->bph', att_norm, proj_q)
        out = jax.nn.relu(jnp.einsum('bph,oh->bpo', att_vec, W) + b)
        return out

    def _L0_attn_ref(x, wq, wk, wv, wo, proj, w1, b1, w2, b2, g1, beta1, g2, beta2):
        import jax, jax.numpy as jnp
        import numpy as np
        B, S, D, H, DH, FF = (2, 2048, 512, 16, 64, 2048)

        def _ln(x, g, b):
            m = x.mean(-1, keepdims=True)
            v = ((x - m) ** 2).mean(-1, keepdims=True)
            return (x - m) * jax.lax.rsqrt(v + 1e-05) * g + b

        def _phi(x, proj):
            return jax.nn.elu(x @ proj) + 1.0
        b, s, d = x.shape
        h = _ln(x, g1, beta1)
        q = _phi((h @ wq).reshape(b, s, H, DH), proj)
        k = _phi((h @ wk).reshape(b, s, H, DH), proj)
        v = (h @ wv).reshape(b, s, H, DH)
        qs = jnp.moveaxis(q, 1, 0)
        ks_ = jnp.moveaxis(k, 1, 0)
        vs = jnp.moveaxis(v, 1, 0)

        def step(carry, qkv_t):
            kv, ksum = carry
            q_t, k_t, v_t = qkv_t
            kv = kv + k_t[..., :, None] * v_t[..., None, :]
            ksum = ksum + k_t
            num = jnp.einsum('bhd,bhde->bhe', q_t, kv)
            den = jnp.einsum('bhd,bhd->bh', q_t, ksum) + 1e-06
            return ((kv, ksum), num / den[..., None])
        kv0 = jnp.zeros((b, H, DH, DH), x.dtype)
        ks0 = jnp.zeros((b, H, DH), x.dtype)
        _, outs = jax.lax.scan(step, (kv0, ks0), (qs, ks_, vs))
        attn = jnp.moveaxis(outs, 0, 1).reshape(b, s, H * DH) @ wo
        x = x + attn
        h2 = _ln(x, g2, beta2)
        x = x + (jax.nn.gelu(h2 @ w1 + b1, approximate=False) @ w2 + b2)
        return x

    def _L0_ffn_ref(hidden_states, w_router, w0, w1, wo):
        import jax, jax.numpy as jnp
        import numpy as np
        B, S, H, F, E, K = (4, 1024, 512, 1024, 8, 2)
        'MoE: router top-k + softmax over selected logits, gated-FFN experts, weighted combine.'
        b, s, h = hidden_states.shape
        e = w_router.shape[1]
        x = hidden_states.reshape(-1, h)
        t = x.shape[0]
        router_logits = x @ w_router
        top_w, top_i = jax.lax.top_k(router_logits, K)
        top_w = jax.nn.softmax(top_w.astype(jnp.float32), axis=-1).astype(x.dtype)
        gating = jnp.zeros((t, e), dtype=x.dtype).at[jnp.arange(t)[:, None], top_i].add(top_w)
        out = jnp.zeros_like(x)
        for ei in range(e):
            hmid = jax.nn.silu(x @ w0[ei]) * (x @ w1[ei])
            out = out + gating[:, ei:ei + 1] * (hmid @ wo[ei])
        return out.reshape(b, s, h)
    x = x + _L0_xattn_ref(_layernorm(x, axis=-1), ctx_1024, L0_xattn_W, L0_xattn_b)
    x = x + _L0_attn_ref(_layernorm(x, axis=-1), L0_attn_wq, L0_attn_wk, L0_attn_wv, L0_attn_wo, L0_attn_proj, L0_attn_w1, L0_attn_b1, L0_attn_w2, L0_attn_b2, L0_attn_g1, L0_attn_beta1, L0_attn_g2, L0_attn_beta2)
    x = x + _L0_ffn_ref(_layernorm(x, axis=-1), L0_ffn_w_router, L0_ffn_w0, L0_ffn_w1, L0_ffn_wo)
    return x

_drawn_inputs = setup_inputs


def setup_inputs(seed=0):
    import zlib

    import numpy as np

    out = dict(_drawn_inputs(seed))
    spreads = {'L0_xattn_b': (0.0, 0.1),
     'L0_attn_b1': (0.0, 0.349),
     'L0_attn_b2': (0.0, 0.1),
     'L0_attn_g1': (1.0, 0.6),
     'L0_attn_beta1': (0.0, 0.685),
     'L0_attn_g2': (1.0, 0.6),
     'L0_attn_beta2': (0.0, 0.771)}
    factors = {'L0_attn_wq': 8.0,
     'L0_attn_wk': 8.0,
     'L0_attn_proj': 8.0,
     'L0_ffn_w_router': 3.094,
     'L0_ffn_w0': 2.766,
     'L0_ffn_w1': 2.708,
     'L0_ffn_wo': 2.71}
    for name, (base, spread) in spreads.items():
        noise = np.random.default_rng([zlib.crc32(name.encode()), seed]).standard_normal(out[name].shape)
        drawn = base * np.exp(spread * noise) if base else spread * noise
        out[name] = jnp.asarray(drawn.astype(out[name].dtype))
    for name, factor in factors.items():
        out[name] = (out[name] * factor).astype(out[name].dtype)
    return out
```

```python
import concourse.bass as bass
from concourse import mybir
from contextlib import ExitStack


def perceiver_block(nc, ins, out):
    f32, f32r = mybir.dt.float32, mybir.dt.float32r
    ACT = mybir.ActivationFunctionType
    ALU = mybir.AluOpType
    AX = mybir.AxisListType

    P = 128
    B, S, D = ins["x"].shape
    KEYS = ins["ctx_1024"].shape[1]
    NT = B * S // P
    KD = D // P
    CH = 4
    FULL = KEYS // P
    NC = FULL // CH + 1
    REM = KEYS - FULL * P
    REMP = REM + REM % 2
    NKT = FULL + 1
    assert FULL % CH == 0 and REM > 0
    EPS = 1e-5

    H, DH = 16, 64
    HD = H * DH
    FF = ins["L0_attn_w1"].shape[1]
    E, _, FE = ins["L0_ffn_w0"].shape
    OV = 7
    NB = E + OV
    RING = 3
    assert HD == 2 * 512 and FE == 2 * 512 and D == 512 and FF == 4 * 512
    assert 2 * B * S <= (OV + 1) * P and E <= OV + 1

    x_v = ins["x"].rearrange("b s d -> (b s) d").rearrange("(t p) d -> p t d", p=P)
    out_v = out.rearrange("b s d -> (b s) d").rearrange("(t p) d -> p t d", p=P)

    with ExitStack() as ctx:
        def sb(name, shape, dt=f32, scope=ctx):
            return scope.enter_context(nc.sbuf_tensor(name, shape, dt))

        def sem(name):
            return ctx.enter_context(nc.semaphore(name))

        bank = [ctx.enter_context(nc.psum_tensor(f"bank{i}", [P, 512], f32)) for i in range(8)]

        ident = sb("ident", [P, P])
        xt = sb("xt", [P, NT, D])
        stats = sb("stats", [P, NT, 6])
        mv = sb("mv", [P, NT, 2])
        rstd = sb("rstd", [P, NT])
        mhalf = sb("mhalf", [P, NT])

        xscope = ExitStack()
        b_col = sb("b_col", [P, KD], f32, xscope)
        avT = sb("avT", [P, KD, B * S], f32, xscope)
        pw_all = sb("pw_all", [P, KD, B, P], f32r, xscope)
        pw = [sb(f"pw{i}", [P, KD, P], f32r, xscope) for i in range(2)]
        pb = sb("pb", [S, B], f32, xscope)
        sc = [sb(f"sc{i}", [S, NKT * P], f32, xscope) for i in range(2)]
        sc_low = [sb(f"sc_low{i}", [S, 512], f32, xscope) for i in range(2)]
        pv_low = sb("pv_low", [S, D], f32, xscope)
        av = sb("av", [S, D], f32, xscope)
        mx4 = sb("mx4", [S, NC], f32, xscope)
        mx = sb("mx", [S, 2], f32, xscope)
        nbias = [sb(f"nbias{i}", [S, 1], f32, xscope) for i in range(2)]
        rsum = [sb(f"rsum{i}", [S, 1], f32, xscope) for i in range(2)]
        rinv = sb("rinv", [S, 1], f32, xscope)
        raw_scope = ExitStack()
        raw = [sb(f"raw{i}", [P, NKT, D], f32, raw_scope) for i in range(2)]
        loop_scope = ExitStack()
        nat_hi = sb("nat_hi", [P, NKT, D], f32r, loop_scope)
        nat_lo = sb("nat_lo", [P, NKT, D], f32r, loop_scope)
        ct_hi = [sb(f"ct_hi{i}", [P, KD, 512], f32r, loop_scope) for i in range(2)]
        ct_lo = [sb(f"ct_lo{i}", [P, KD, 512], f32r, loop_scope) for i in range(2)]
        pT = sb("pT", [P, NKT, P], f32r, loop_scope)
        loop_scope.close()
        pro_scope = ExitStack()
        Wn = sb("Wn", [P, KD, D], f32, pro_scope)
        pn = sb("pn", [P, NT, D], f32, pro_scope)
        pnT = sb("pnT", [P, KD, B * S], f32, pro_scope)
        pnT_hi = sb("pnT_hi", [P, KD, B * S], f32r, pro_scope)
        pnT_lo = sb("pnT_lo", [P, KD, B * S], f32r, pro_scope)
        W_hi = sb("W_hi", [P, KD, D], f32r, pro_scope)
        W_lo = sb("W_lo", [P, KD, D], f32r, pro_scope)
        pro_scope.close()
        raw_scope.close()
        epi_scope = ExitStack()
        We = sb("We", [P, KD, D], f32, epi_scope)
        b_bc = sb("b_bc", [P, D], f32, epi_scope)
        WT_hi = sb("WT_hi", [P, KD, D], f32r, epi_scope)
        WT_lo = sb("WT_lo", [P, KD, D], f32r, epi_scope)
        avT_hi = sb("avT_hi", [P, KD, B * S], f32r, epi_scope)
        avT_lo = sb("avT_lo", [P, KD, B * S], f32r, epi_scope)
        xo = sb("xo", [P, NT, D], f32, epi_scope)
        epi_scope.close()
        xscope.close()

        x1n = sb("x1n", [P, NT, D])
        xn = sb("xn", [P, NT, D])
        heads = xn[:, :, :].rearrange("p (r a) d -> p r (a d)", r=2)
        xT_hi = sb("xT_hi", [P, KD, B * S], f32r)
        xT_lo = sb("xT_lo", [P, KD, B * S], f32r)
        w_raw = [sb(f"w_raw{i}", [P, KD, 512]) for i in range(RING)]
        w_hi = [sb(f"w_hi{i}", [P, KD, 512], f32r) for i in range(RING)]
        w_lo = [sb(f"w_lo{i}", [P, KD, 512], f32r) for i in range(RING)]
        gain = sb("gain", [P, D])
        shift = sb("shift", [P, D])
        b2_bc = sb("b2_bc", [P, D])
        b1_col = sb("b1_col", [P, FF // P])
        zeros = sb("zeros", [P, D])
        ones = sb("ones", [P, P])
        before = sb("before", [P, P])
        e_int = sb("e_int", [P, E], mybir.dt.int32)
        e_idx = sb("e_idx", [P, E])
        upto = sb("upto", [P, E, E])
        w_router = sb("w_router", [P, KD, E])
        late = ExitStack()
        proj2 = sb("proj2", [P, P], f32, late)
        proj2_hi = sb("proj2_hi", [P, P], f32r, late)
        proj2_lo = sb("proj2_lo", [P, P], f32r, late)
        mask = sb("mask", [P, P], f32, late)
        z_hi = [sb(f"z_hi{i}", [P, B * S], f32r, late) for i in range(2)]
        z_lo = [sb(f"z_lo{i}", [P, B * S], f32r, late) for i in range(2)]
        neg = [sb(f"neg{i}", [P, B * S], f32, late) for i in range(2)]
        phi = [sb(f"phi_{n}", [P, H // 2, B * S], f32, late) for n in "qk"]
        v1 = sb("v1", [P, NT, H, DH + 1], f32, late)
        at = [sb(f"at{i}", [P, 4, P], f32, late) for i in range(2)]
        oT_hi = sb("oT_hi", [P, HD // P, P], f32r, late)
        oT_lo = sb("oT_lo", [P, HD // P, P], f32r, late)
        den = sb("den", [P, 2, 4], f32, late)
        late.close()
        ffn = ExitStack()
        gl = [sb(f"gl{i}", [P, B * S], f32, ffn) for i in range(2)]
        gl_hi = [sb(f"gl_hi{i}", [P, B * S], f32r, ffn) for i in range(2)]
        gl_lo = [sb(f"gl_lo{i}", [P, B * S], f32r, ffn) for i in range(2)]
        ffn.close()

        moe = ExitStack()
        xT32 = sb("xT32", [P, KD, B * S], f32, moe)
        logits = sb("logits", [P, NT, E], f32, moe)
        pref = sb("pref", [P, E], f32, moe)
        low_slot = sb("low_slot", [P, E], f32, moe)
        pick = [sb(f"pick{k}", [P, NT, E], f32, moe) for k in range(2)]
        scr = sb("scr", [P, NT, E], f32, moe)
        scr8 = sb("scr8", [P, E, E], f32, moe)
        best = [sb(f"best{k}", [P, NT], f32, moe) for k in range(2)]
        top = sb("top", [P, NT], f32, moe)
        chosen = sb("chosen", [P, NT, E], f32, moe)
        rank = sb("rank", [P, NT, E], f32, moe)
        count = sb("count", [P, E], f32, moe)
        extra = sb("extra", [P, E], f32, moe)
        upto_extra = sb("upto_extra", [P, E], f32, moe)
        shift8 = sb("shift8", [P, E], f32, moe)
        slotf = [sb(f"slotf{k}", [P, NT], f32, moe) for k in range(2)]
        slot_of = [sb(f"slot_of{k}", [P, NT], mybir.dt.uint32, moe) for k in range(2)]
        ovf = sb("ovf", [P, OV], f32, moe)
        block_expert = sb("block_expert", [P, OV], mybir.dt.int32, moe)
        gate = [sb(f"gate{k}", [P, NT], f32, moe) for k in range(2)]
        gap = sb("gap", [P, NT], f32, moe)
        gsum = sb("gsum", [P, NT], f32, moe)
        xg = sb("xg", [P, D], f32, moe)
        xgT_hi = sb("xgT_hi", [P, KD, P], f32r, moe)
        xgT_lo = sb("xgT_lo", [P, KD, P], f32r, moe)
        sg = [sb(f"sg{i}", [P, 512], f32, moe) for i in range(2)]
        hm = [sb(f"hm{i}", [P, 512], f32, moe) for i in range(2)]
        hmT_hi = [sb(f"hmT_hi{i}", [P, 4, P], f32r, moe) for i in range(2)]
        hmT_lo = [sb(f"hmT_lo{i}", [P, 4, P], f32r, moe) for i in range(2)]
        yb = sb("yb", [P, D], f32, moe)
        yt = [sb(f"yt{k}", [P, NT, D], f32, moe) for k in range(2)]
        moe.close()
        xs = nc.dram_tensor("slots_x", [NB * P, D], f32).ap()
        ys = nc.dram_tensor("slots_y", [NB * P, D], f32).ap()

        x_loaded, W_loaded, b_loaded = sem("x_loaded"), sem("W_loaded"), sem("b_loaded")
        ctx_loaded = [[sem(f"ctx_loaded{p}_{c}") for c in range(NC)] for p in range(2)]
        raw_zeroed, sc_zeroed = sem("raw_zeroed"), sem("sc_zeroed")
        const_ready = sem("const_ready")
        dve_step, pool_step = sem("dve_step"), sem("pool_step")
        var_ready, rstd_ready, pn_ready = sem("var_ready"), sem("rstd_ready"), sem("pn_ready")
        pnT_done, pnT_hi_ready, pnT_ready, pnT_lo_ready = sem("pnT_done"), sem("pnT_hi_ready"), sem("pnT_ready"), sem("pnT_lo_ready")
        W_hi_ready, W_lo_ready = sem("W_hi_ready"), sem("W_lo_ready")
        pwT_done, pw_hi_ready, pw_lo_ready, pw_ready = sem("pwT_done"), sem("pw_hi_ready"), sem("pw_lo_ready"), sem("pw_ready")
        pb_done, pb_ready = sem("pb_done"), sem("pb_ready")
        t_done, t_hi, t_lo = sem("t_done"), sem("t_hi"), sem("t_lo")
        qk_done, s_low, s_ready = sem("qk_done"), sem("s_low"), sem("s_ready")
        max_ready, exp_done, rinv_ready = sem("max_ready"), sem("exp_done"), sem("rinv_ready")
        pt_done, pt_hi, pt_lo = sem("pt_done"), sem("pt_hi"), sem("pt_lo")
        nat_hi_ready, nat_lo_ready = sem("nat_hi_ready"), sem("nat_lo_ready")
        pv_done, pv_low_ready, av_sum, av_ready = sem("pv_done"), sem("pv_low_ready"), sem("av_sum"), sem("av_ready")
        avt_done, avt_ready = sem("avt_done"), sem("avt_ready")
        WT_done, WT_hi_ready, WT_lo_ready = sem("WT_done"), sem("WT_hi_ready"), sem("WT_lo_ready")
        avT_hi_ready, avT_lo_ready, xo_done, x1_ready = sem("avT_hi_ready"), sem("avT_lo_ready"), sem("xo_done"), sem("x1_ready")
        stored = sem("stored")
        zeros_ready, slots_zeroed, router_loaded, index_ready, order_ready = sem("zeros_ready"), sem("slots_zeroed"), sem("router_loaded"), sem("index_ready"), sem("order_ready")
        xT32_ready, logits_done, chosen_ready, rank_done = sem("xT32_ready"), sem("logits_done"), sem("chosen_ready"), sem("rank_done")
        gap_ready, gap_exp, slots_ready, scattered = sem("gap_ready"), sem("gap_exp"), sem("slots_ready"), sem("scattered")
        xo_ready = sem("xo_ready")
        xg_loaded, xgT_done, xgT_hi_ready, xgT_lo_ready = sem("xg_loaded"), sem("xgT_done"), sem("xgT_hi_ready"), sem("xgT_lo_ready")
        unit_done, silu_ready, hm_ready, hmT_done = sem("unit_done"), sem("silu_ready"), sem("hm_ready"), sem("hmT_done")
        hmT_hi_ready, hmT_lo_ready, y_ready, y_stored = sem("hmT_hi_ready"), sem("hmT_lo_ready"), sem("y_ready"), sem("y_stored")
        gathered = [sem(f"gathered{t}") for t in range(NT)]
        w_loaded = [sem(f"w_loaded{i}") for i in range(RING)]
        w_hi_ready = [sem(f"w_hi_ready{i}") for i in range(RING)]
        w_lo_ready = [sem(f"w_lo_ready{i}") for i in range(RING)]
        b1_loaded = sem("b1_loaded")
        vec_loaded, vec2_loaded = sem("vec_loaded"), sem("vec2_loaded")
        proj_loaded, proj_zero, proj_hi_ready, proj_lo_ready, mask_ready = sem("proj_loaded"), sem("proj_zero"), sem("proj_hi_ready"), sem("proj_lo_ready"), sem("mask_ready")
        xn_ready, xT_done, xT_hi_ready, xT_lo_ready = sem("xn_ready"), sem("xT_done"), sem("xT_hi_ready"), sem("xT_lo_ready")
        z_done, z_hi_ready, z_lo_ready = sem("z_done"), sem("z_hi_ready"), sem("z_lo_ready")
        f_done, neg_ready, e_ready, phi_ready = sem("f_done"), sem("neg_ready"), sem("e_ready"), sem("phi_ready")
        v_done, v_ready, v_one = sem("v_done"), sem("v_ready"), sem("v_one")
        a_done, a_ready, o_done, o_ready = sem("a_done"), sem("a_ready"), sem("o_done"), sem("o_ready")
        oT_done, oT_hi_ready, oT_lo_ready = sem("oT_done"), sem("oT_hi_ready"), sem("oT_lo_ready")
        ao_done, xa_ready = sem("ao_done"), sem("xa_ready")
        up_done, gelu_ready, gl_hi_ready, gl_lo_ready, dn_done, x2_ready = sem("up_done"), sem("gelu_ready"), sem("gl_hi_ready"), sem("gl_lo_ready"), sem("dn_done"), sem("x2_ready")

        def unit(name, half, rows=False):
            w = ins[name].rearrange("(k p) n -> p k n", p=P)
            return w[:, KD * half:KD * (half + 1), :] if rows else w[:, :, 512 * half:512 * (half + 1)]

        UNITS = [unit(f"L0_attn_{n}", half) for n in ("wq", "wk", "wv") for half in range(2)]
        UNITS += [unit("L0_attn_wo", half, rows=True) for half in range(2)]
        for i in range(FF // 512):
            UNITS += [unit("L0_attn_w1", i), unit("L0_attn_w2", i, rows=True)]
        NU = len(UNITS)
        USED = [(z_done, 4 * (u + 1)) for u in range(4)] + [(v_done, NT), (v_done, 2 * NT), (ao_done, NT), (ao_done, NT)]
        for i in range(FF // 512):
            USED += [(up_done, 4 * (i + 1)), (dn_done, 4 * (i + 1))]

        def upper(u):
            return w_hi_ready[u % RING], u // RING + 1

        def lower(u):
            return w_lo_ready[u % RING], u // RING + 1

        EU = 6
        POOL_UNITS = (3, 5)
        assert EU % RING == 0

        def expert_unit(e, j):
            w = ins["L0_ffn_" + ("w0", "w1", "w0", "w1", "wo", "wo")[j]]
            w = w[bass.ds(e, 1), :, :].rearrange("o (k p) n -> p (o k) n", p=P)
            return w[:, KD * (j - 4):KD * (j - 3), :] if j >= 4 else w[:, :, 512 * (j // 2):512 * (j // 2 + 1)]

        def slot(j):
            return (NU + j) % RING

        def turn_of(b, j):
            return (EU // RING) * b + (NU + j) // RING + 1

        TB = [bank[0], bank[1], bank[2]]
        SB = [bank[3], bank[4]]
        PB = [bank[5], bank[6]]
        VB = bank[7]
        G = FULL + 1
        PT_SPLIT = [(0, 8), (8, NKT)]

        def groups(c):
            if c < NC - 1:
                return [(CH * c + k, [k]) for k in range(KD)]
            return [(G - 1, list(range(KD)))]

        def width(c):
            return CH * P if c < NC - 1 else REM

        def t_bank(g):
            return TB[g % len(TB)]

        def t_before(b, g):
            if g >= len(TB):
                return G * b + g - len(TB) + 1
            if isinstance(b, int) and b == 0:
                return None
            last = max(h for h in range(G) if h % len(TB) == g)
            return G * (b - 1) + last + 1

        block = ctx.enter_context(nc.Block())

        @block.sync
        def _(sp):
            sp.dma_start(xt[:, :, :], x_v).then_inc(x_loaded, 16)
            sp.dma_start(Wn[:, :, :], ins["L0_xattn_W"].rearrange("(k p) h -> p k h", p=P)).then_inc(W_loaded, 16)
            with nc.allow_non_contiguous_dma(reason="512 bias values, once"):
                sp.dma_start(b_col[:, :], ins["L0_xattn_b"].rearrange("(k p) -> p k", p=P)).then_inc(b_loaded, 16)

            def load_ctx(b, c):
                src = ins["ctx_1024"][b]
                if c < NC - 1:
                    src = src[0:FULL * P, :].rearrange("(p j) d -> p j d", j=FULL)[:, CH * c:CH * (c + 1), :]
                    dst = raw[b % 2][:, CH * c:CH * (c + 1), :]
                else:
                    src, dst = src[FULL * P:KEYS, :], raw[b % 2][0:REM, FULL, :]
                sp.dma_start(dst, src).then_inc(ctx_loaded[b % 2][c], 16)

            sp.wait_ge(raw_zeroed, 2)
            for b in range(B):
                for c in range(NC):
                    if b >= 2:
                        sp.wait_ge(t_done, G * (b - 2) + groups(c)[-1][0] + 1)
                        sp.wait_ge(nat_lo_ready, NC * (b - 2) + c + 1)
                    load_ctx(b, c)
            sp.wait_ge(t_done, G * (B - 1))
            sp.wait_ge(nat_lo_ready, NC * (B - 1))
            sp.dma_start(We[:, :, :], ins["L0_xattn_W"].rearrange("(k p) h -> p k h", p=P)).then_inc(W_loaded, 16)
            sp.dma_start(b_bc[:, :], ins["L0_xattn_b"].partition_broadcast(P)).then_inc(b_loaded, 16)
            sp.wait_ge(x1_ready, NT)
            for name, dst in (("g1", gain), ("beta1", shift), ("b2", b2_bc)):
                sp.dma_start(dst[:, :], ins[f"L0_attn_{name}"].partition_broadcast(P)).then_inc(vec_loaded, 16)
            for u in range(NU):
                if u == 8:
                    sp.wait_ge(xT_lo_ready, KD)
                    for name, dst in (("g2", gain), ("beta2", shift)):
                        sp.dma_start(dst[:, :], ins[f"L0_attn_{name}"].partition_broadcast(P)).then_inc(vec2_loaded, 16)
                if u >= RING:
                    sp.wait_ge(*lower(u - RING))
                sp.dma_start(w_raw[u % RING][:, :, :], UNITS[u]).then_inc(w_loaded[u % RING], 16)
                if u == 0:
                    with nc.allow_non_contiguous_dma(reason="bias values by partition, once"):
                        sp.dma_start(b1_col[:, :], ins["L0_attn_b1"].rearrange("(f p) -> p f", p=P)).then_inc(b1_loaded, 16)
                    sp.wait_ge(proj_zero, 1)
                    for s in range(2):
                        sp.dma_start(proj2[DH * s:DH * (s + 1), DH * s:DH * (s + 1)], ins["L0_attn_proj"]).then_inc(proj_loaded, 16)
            sp.dma_start(w_router[:, :, :], ins["L0_ffn_w_router"].rearrange("(k p) e -> p k e", p=P)).then_inc(router_loaded, 16)
            sp.wait_ge(zeros_ready, 1)
            sp.dma_start(xs.rearrange("(n p) d -> p n d", p=P), zeros[:, :].unsqueeze(1).to_broadcast([P, NB, D])).then_inc(slots_zeroed, 16)

            def load_unit(e, b, j, count):
                sp.wait_ge(w_lo_ready[slot(j)], count)
                sp.dma_start(w_raw[slot(j)][:, :, :], expert_unit(e, j)).then_inc(w_loaded[slot(j)], 16)

            def load_rows(b):
                sp.dma_start(xg[:, :], xs[bass.ds(b * P, P), :]).then_inc(xg_loaded, 16)

            def store_rows(b):
                sp.dma_start(ys[bass.ds(b * P, P), :], yb[:, :]).then_inc(y_stored, 16)

            for j in range(EU):
                load_unit(0, 0, j, turn_of(0, j) - 1)
                if j == RING - 1:
                    sp.wait_ge(scattered, 16 * 2 * NT)
                    load_rows(0)

            def load_block(e, b):
                counts = [sp.snap(turn_of(b, j) - 1) for j in range(EU)]
                sp.wait_ge(xgT_done, b)
                load_rows(b)
                for j in range(EU):
                    load_unit(e, b, j, counts[j])
                sp.wait_ge(y_ready, b)
                store_rows(b - 1)

            with sp.Fori(1, E) as b:
                load_block(b, b)
            sp.wait_ge(slots_ready, 3)
            with sp.Fori(E, NB) as b:
                e = sp.value_load(block_expert[0:1, bass.ds(b - E, 1)], min_val=0, max_val=E - 1)
                load_block(e, b)
            sp.wait_ge(y_ready, NB)
            store_rows(NB - 1)
            sp.wait_ge(xo_ready, NT)
            sp.dma_start(out_v, xt[:, :, :]).then_inc(stored, 16)
            sp.wait_ge(stored, 16)

        @block.gpsimd
        def _(pool):
            steps = [0]

            def link(ins_):
                steps[0] += 1
                ins_.then_inc(pool_step, 1)
                pool.wait_ge(pool_step, steps[0])

            link(nc.gpsimd.memset(ident[:, :], 0.0))
            nc.gpsimd.affine_select(out=ident[:, :], in_=ident[:, :], compare_op=ALU.not_equal, fill=1.0, base=0,
                                    pattern=[[-1, P]], channel_multiplier=1).then_inc(const_ready, 1)
            link(nc.gpsimd.memset(mhalf[:, :], -0.5))
            pool.wait_ge(var_ready, 1)
            nc.gpsimd.tensor_tensor(rstd[:, :], rstd[:, :], mhalf[:, :], ALU.pow).then_inc(rstd_ready, 1)

            def take_pw(b, par):
                if not (isinstance(b, int) and b < 2):
                    pool.wait_ge(qk_done, NC * (b - 1))
                nc.gpsimd.tensor_copy(pw[par][:, :, :], pw_all[:, :, bass.ds(b, 1), :].rearrange("p k o m -> p k (o m)").bitcast(f32))\
                    .then_inc(pw_ready, 1)

            def split_ctx(b, par):
                for c in range(NC):
                    first, last = CH * c, min(CH * (c + 1), NKT)
                    pool.wait_ge(nat_hi_ready, NC * b + c + 1)
                    nc.gpsimd.tensor_tensor(nat_lo[:, first:last, :], raw[par][:, first:last, :],
                                            nat_hi[:, first:last, :].bitcast(f32), ALU.subtract).then_inc(nat_lo_ready, 1)

            pool.wait_ge(pw_hi_ready, KD)
            pool.wait_ge(pw_lo_ready, KD)
            take_pw(0, 0)
            take_pw(1, 1)
            split_ctx(0, 0)
            with pool.Fori(0, B // 2 - 1) as i:
                take_pw(2 * i + 2, 0)
                split_ctx(2 * i + 1, 1)
                take_pw(2 * i + 3, 1)
                split_ctx(2 * i + 2, 0)
            split_ctx(B - 1, 1)

            def root(n):
                pool.wait_ge(var_ready, n)
                nc.gpsimd.tensor_tensor(rstd[:, :], rstd[:, :], mhalf[:, :], ALU.pow).then_inc(rstd_ready, 1)

            pool.wait_ge(x1_ready, NT)
            link(nc.gpsimd.memset(mask[:, :], 1.0))
            link(nc.gpsimd.affine_select(out=mask[:, :], in_=mask[:, :], compare_op=ALU.is_ge, fill=0.0, base=0,
                                         pattern=[[1, P]], channel_multiplier=-1))
            nc.gpsimd.affine_select(out=mask[:, S:P], in_=mask[:, S:P], compare_op=ALU.is_ge, fill=0.0, base=-S,
                                    pattern=[[0, P - S]], channel_multiplier=1).then_inc(mask_ready, 1)
            root(2)
            root(3)
            nc.gpsimd.iota(e_int[:, :], pattern=[[1, E]], base=0, channel_multiplier=0).then_inc(index_ready, 1)
            link(nc.gpsimd.memset(ones[:, :], 1.0))
            nc.gpsimd.affine_select(out=before[:, :], in_=ones[:, :], compare_op=ALU.is_gt, fill=0.0, base=0,
                                    pattern=[[1, P]], channel_multiplier=-1).then_inc(order_ready, 1)
            nc.gpsimd.affine_select(out=upto[:, :, :], in_=ones[:, 0:E * E].rearrange("p (e f) -> p e f", e=E), compare_op=ALU.is_ge,
                                    fill=0.0, base=0, pattern=[[1, E], [-1, E]], channel_multiplier=0).then_inc(order_ready, 1)
            root(4)
            root(5)
            pool.wait_ge(slots_ready, 2)
            pool.wait_ge(slots_zeroed, 16)
            for k in range(2):
                for t in range(NT):
                    nc.gpsimd.indirect_dma_start(xs[:, :], bass.IndirectOffsetOnAxis(ap=slot_of[k][:, t:t + 1], axis=0),
                                                 xn[:, t, :], None).then_inc(scattered, 16)

            def split_w(b, j):
                pool.wait_ge(w_hi_ready[slot(j)], turn_of(b, j))
                nc.gpsimd.tensor_tensor(w_lo[slot(j)][:, :, :], w_raw[slot(j)][:, :, :], w_hi[slot(j)][:, :, :].bitcast(f32),
                                        ALU.subtract).then_inc(w_lo_ready[slot(j)], 1)

            for j in POOL_UNITS:
                split_w(0, j)
            with pool.Fori(1, NB) as b:
                for j in POOL_UNITS:
                    split_w(b, j)
            pool.wait_ge(y_stored, 16 * NB)
            for t in range(NT):
                for k in range(2):
                    nc.gpsimd.indirect_dma_start(yt[k][:, t, :], None, ys[:, :],
                                                 bass.IndirectOffsetOnAxis(ap=slot_of[k][:, t:t + 1], axis=0)).then_inc(gathered[t], 16)

        @block.scalar
        def _(act):
            act.wait_ge(W_loaded, 16)
            nc.scalar.activation(W_hi[:, :, :], Wn[:, :, :], ACT.Copy).then_inc(W_hi_ready, 1)
            for k in range(KD):
                act.wait_ge(pnT_done, k + 1)
                nc.scalar.activation(pnT_hi[:, k, :], bank[k][:, :], ACT.Copy).then_inc(pnT_hi_ready, 1)
                nc.scalar.activation(pnT[:, k, :], bank[k][:, :], ACT.Copy).then_inc(pnT_ready, 1)
            for m in range(KD):
                act.wait_ge(pwT_done, m + 1)
                nc.scalar.activation(pw_all[:, m, :, 0:S], bank[m][:, :].rearrange("p (b s) -> p b s", b=B),
                                     ACT.Copy).then_inc(pw_hi_ready, 1)
            act.wait_ge(pb_done, 1)
            nc.scalar.activation(pb[:, :], bank[4][0:S, 0:B], ACT.Copy).then_inc(pb_ready, 1)

            def evacuate(b, c):
                if c >= 2:
                    act.wait_ge(qk_done, NC * b + c - 1)
                elif not (isinstance(b, int) and b == 0):
                    act.wait_ge(qk_done, NC * (b - 1) + NC - 2 + c + 1)
                for g, ks in groups(c):
                    act.wait_ge(t_done, G * b + g + 1)
                    n = width(c) if len(ks) == 1 else REMP
                    nc.scalar.activation(ct_hi[c % 2][:, ks[0]:ks[-1] + 1, 0:n],
                                         t_bank(g)[:, 0:len(ks) * 512 // len(ks)].rearrange("p (k n) -> p k n", k=len(ks))[:, :, 0:n],
                                         ACT.Copy).then_inc(t_hi, 1)

            def low_scores(b, c):
                act.wait_ge(qk_done, NC * b + c + 1)
                if not (isinstance(b, int) and b == 0 and c < 2):
                    act.wait_ge(s_ready, NC * b + c - 1)
                nc.scalar.activation(sc_low[c % 2][:, 0:width(c)], SB[c % 2][S:2 * S, 0:width(c)], ACT.Copy).then_inc(s_low, 1)

            def take_av(b):
                act.wait_ge(avt_done, b + 1)
                nc.scalar.activation(avT[:, :, bass.ds(S * b, S)], VB[:, 0:KD * S].rearrange("p (k s) -> p k s", k=KD),
                                     ACT.Copy).then_inc(avt_ready, 1)

            def prob_parts(b):
                for h, (t0, t1) in enumerate(PT_SPLIT):
                    act.wait_ge(pt_done, 2 * b + h + 1)
                    if not (isinstance(b, int) and b == 0):
                        act.wait_ge(pv_done, NC * b)
                    nc.scalar.activation(pT[:, t0:t1, 0:S], PB[h][:, 0:(t1 - t0) * S].rearrange("p (j s) -> p j s", s=S),
                                         ACT.Copy).then_inc(pt_hi, 1)

            def exps(b, par):
                act.wait_ge(max_ready, b + 1)
                if not (isinstance(b, int) and b < 2):
                    act.wait_ge(rinv_ready, b - 1)
                nc.scalar.activation(sc[par][0:S, 0:KEYS], sc[par][0:S, 0:KEYS], ACT.Exp, bias=nbias[par][:, :],
                                     accum_out=rsum[par][:, :]).then_inc(exp_done, 1)

            def stage(b, par, scores=True, values=True, earlier=True):
                if scores:
                    evacuate(b + 1, 0)
                if earlier:
                    take_av(b - 1)
                if scores:
                    evacuate(b + 1, 1)
                if values:
                    prob_parts(b)
                if scores:
                    low_scores(b + 1, 0)
                    evacuate(b + 1, 2)
                    low_scores(b + 1, 1)
                    evacuate(b + 1, 3)
                    low_scores(b + 1, 2)
                if values:
                    act.wait_ge(pv_done, NC * (b + 1))
                    nc.scalar.activation(pv_low[:, :], VB[S:2 * S, :], ACT.Copy).then_inc(pv_low_ready, 1)
                if scores:
                    low_scores(b + 1, 3)
                if values:
                    act.wait_ge(rinv_ready, b + 1)
                    act.wait_ge(av_sum, b + 1)
                    nc.scalar.activation(av[0:S, :], pv_low[:, :], ACT.Copy, scale=rinv[:, :]).then_inc(av_ready, 1)
                if scores:
                    exps(b + 1, 1 - par)

            stage(-1, 1, values=False, earlier=False)
            stage(0, 0, earlier=False)
            with act.Fori(0, B // 2 - 1) as i:
                stage(2 * i + 1, 1)
                stage(2 * i + 2, 0)
            stage(B - 1, 1, scores=False)
            for k in range(KD):
                act.wait_ge(WT_done, k + 1)
                nc.scalar.activation(WT_hi[:, k, :], bank[k][:, :], ACT.Copy).then_inc(WT_hi_ready, 1)
            take_av(B - 1)
            act.wait_ge(avt_ready, B)
            nc.scalar.activation(avT_hi[:, :, :], avT[:, :, :], ACT.Copy).then_inc(avT_hi_ready, 1)

            def split_w(u):
                act.wait_ge(w_loaded[u % RING], 16 * (u // RING + 1))
                if u >= RING:
                    act.wait_ge(*USED[u - RING])
                nc.scalar.activation(w_hi[u % RING][:, :, :], w_raw[u % RING][:, :, :], ACT.Copy).then_inc(w_hi_ready[u % RING], 1)

            def upper_xT(n):
                for k in range(KD):
                    act.wait_ge(xT_done, KD * n + k + 1)
                    nc.scalar.activation(xT_hi[:, k, :], bank[k][:, :], ACT.Copy).then_inc(xT_hi_ready, 1)

            act.wait_ge(proj_loaded, 32)
            nc.scalar.activation(proj2_hi[:, :], proj2[:, :], ACT.Copy).then_inc(proj_hi_ready, 1)
            split_w(0)
            upper_xT(0)
            split_w(1)
            split_w(2)

            def upper_z(n):
                act.wait_ge(z_done, n + 1)
                if n >= 2:
                    act.wait_ge(f_done, n - 1)
                nc.scalar.activation(z_hi[n % 2][:, :], bank[n % 2][:, :], ACT.Copy).then_inc(z_hi_ready, 1)

            def exp_neg(n):
                act.wait_ge(neg_ready, n + 1)
                nc.scalar.activation(neg[n % 2][:, :], neg[n % 2][:, :], ACT.Exp).then_inc(e_ready, 1)

            for n in range(H):
                upper_z(n)
                if n >= 1:
                    exp_neg(n - 1)
                if n % 4 == 0 and n // 4 + 2 >= RING:
                    split_w(n // 4 + 2)
            exp_neg(H - 1)
            for u in range(2):
                for t in range(NT):
                    n = NT * u + t
                    act.wait_ge(v_done, n + 1)
                    nc.scalar.activation(v1[:, t, 8 * u:8 * (u + 1), 0:DH], bank[4 + n % 2][:, :].rearrange("p (h d) -> p h d", d=DH),
                                         ACT.Copy).then_inc(v_ready, 1)
                split_w(6 + u)
            for t in range(NT):
                for half in range(2):
                    act.wait_ge(oT_done, 2 * t + half + 1)
                    if t >= 1:
                        act.wait_ge(ao_done, t)
                    nc.scalar.activation(oT_hi[:, 4 * half:4 * (half + 1), :], bank[4 + half][:, :].rearrange("p (k n) -> p k n", n=P),
                                         ACT.Copy).then_inc(oT_hi_ready, 1)
                if t == 0:
                    split_w(8)
            split_w(9)
            upper_xT(1)
            split_w(10)
            act.wait_ge(b1_loaded, 16)
            for n in range(FF // P):
                act.wait_ge(up_done, n + 1)
                if n >= 2:
                    act.wait_ge(gl_lo_ready, n - 1)
                nc.scalar.activation(gl[n % 2][:, :], bank[n % 2][:, :], ACT.Gelu, bias=b1_col[:, n:n + 1]).then_inc(gelu_ready, 1)
                if n % 4 == 3 and n < FF // P - 1:
                    split_w(11 + 2 * (n // 4))
                if n % 4 == 0 and 4 <= n < FF // P - 4:
                    split_w(10 + n // 2)

            def split_e(b, j, wait=None):
                act.wait_ge(w_loaded[slot(j)], 16 * turn_of(b, j))
                act.wait_ge(*(wait or (unit_done, EU * b + j - RING + 1)))
                nc.scalar.activation(w_hi[slot(j)][:, :, :], w_raw[slot(j)][:, :, :], ACT.Copy).then_inc(w_hi_ready[slot(j)], 1)

            for j in range(RING):
                split_e(0, j, USED[NU - RING + j])
            for k in range(KD):
                act.wait_ge(xT_done, 2 * KD + k + 1)
                nc.scalar.activation(xT32[:, k, :], bank[k][:, :], ACT.Copy).then_inc(xT32_ready, 1)
            act.wait_ge(gap_ready, 1)
            nc.scalar.activation(gsum[:, :], gap[:, :], ACT.Exp).then_inc(gap_exp, 1)

            def upper_rows(b):
                act.wait_ge(xgT_done, b + 1)
                nc.scalar.activation(xgT_hi[:, :, :], bank[7][:, :].rearrange("p (k n) -> p k n", n=P), ACT.Copy).then_inc(xgT_hi_ready, 1)

            def silu(b, half):
                act.wait_ge(unit_done, EU * b + 2 * half + 1)
                nc.scalar.activation(sg[half][:, :], bank[2 * half][:, :], ACT.Silu).then_inc(silu_ready, 1)

            def upper_hidden(b, half):
                act.wait_ge(hmT_done, 2 * b + half + 1)
                nc.scalar.activation(hmT_hi[half][:, :, :], bank[4 + half][:, :].rearrange("p (k n) -> p k n", n=P),
                                     ACT.Copy).then_inc(hmT_hi_ready, 1)

            def expert_block(b, first=False, last=False):
                split_e(b, 3)
                silu(b, 0)
                split_e(b, 4)
                split_e(b, 5)
                upper_hidden(b, 0)
                silu(b, 1)
                if not last:
                    split_e(b + 1, 0)
                    upper_rows(b + 1)
                upper_hidden(b, 1)
                if not last:
                    split_e(b + 1, 1)
                act.wait_ge(unit_done, EU * (b + 1))
                if not first:
                    act.wait_ge(y_stored, 16 * b)
                nc.scalar.activation(yb[:, :], bank[6][:, :], ACT.Copy).then_inc(y_ready, 1)
                if not last:
                    split_e(b + 1, 2)

            upper_rows(0)
            expert_block(0, first=True)
            with act.Fori(1, NB - 1) as b:
                expert_block(b)
            expert_block(NB - 1, last=True)

        @block.vector
        def _(dve):
            steps = [0]

            def link(ins_):
                steps[0] += 1
                ins_.then_inc(dve_step, 1)
                dve.wait_ge(dve_step, steps[0])

            for par in range(2):
                nc.vector.memset(raw[par][64:P, FULL, :], 0.0).then_inc(raw_zeroed, 1)
                nc.vector.memset(sc[par][0:S, KEYS:NKT * P], 0.0).then_inc(sc_zeroed, 1)
            dve.wait_ge(x_loaded, 16)
            for t in range(NT):
                last = nc.vector.bn_stats(stats[:, t, :], xt[:, t, :])
            link(last)
            for t in range(NT):
                last = nc.vector.bn_aggr(mv[:, t, :], stats[:, t, :])
            link(last)
            nc.vector.tensor_scalar(rstd[:, :], mv[:, :, 1], EPS, None, ALU.add).then_inc(var_ready, 1)
            dve.wait_ge(rstd_ready, 1)
            for t in range(NT):
                nc.vector.tensor_scalar(pn[:, t, :], xt[:, t, :], mv[:, t, 0:1], rstd[:, t:t + 1],
                                        ALU.subtract, ALU.mult).then_inc(pn_ready, 1)
            dve.wait_ge(W_hi_ready, 1)
            nc.vector.tensor_tensor(W_lo[:, :, :], Wn[:, :, :], W_hi[:, :, :].bitcast(f32), ALU.subtract).then_inc(W_lo_ready, 1)
            for k in range(KD):
                dve.wait_ge(pnT_ready, k + 1)
                nc.vector.tensor_tensor(pnT_lo[:, k, :], bank[k][:, :], pnT_hi[:, k, :].bitcast(f32), ALU.subtract).then_inc(pnT_lo_ready, 1)
            for m in range(KD):
                dve.wait_ge(pw_hi_ready, m + 1)
                nc.vector.tensor_tensor(pw_all[:, m, :, S:2 * S], bank[m][:, :].rearrange("p (b s) -> p b s", b=B),
                                        pw_all[:, m, :, 0:S].bitcast(f32), ALU.subtract).then_inc(pw_lo_ready, 1)
            dve.wait_ge(pb_ready, 1)

            def evacuate(b, c):
                for g, ks in groups(c):
                    dve.wait_ge(t_hi, G * b + g + 1)
                    n = width(c) if len(ks) == 1 else REMP
                    nc.vector.tensor_tensor(ct_lo[c % 2][:, ks[0]:ks[-1] + 1, 0:n],
                                            t_bank(g)[:, :].rearrange("p (k n) -> p k n", k=len(ks))[:, :, 0:n],
                                            ct_hi[c % 2][:, ks[0]:ks[-1] + 1, 0:n].bitcast(f32), ALU.subtract).then_inc(t_lo, 1)

            def add_scores(b, par, c):
                dve.wait_ge(s_low, NC * b + c + 1)
                if c == 0 and not (isinstance(b, int) and b < 2):
                    dve.wait_ge(pt_done, 2 * (b - 1))
                nc.vector.tensor_tensor(sc[par][0:S, 512 * c:512 * c + width(c)], SB[c % 2][0:S, 0:width(c)],
                                        sc_low[c % 2][:, 0:width(c)], ALU.add).then_inc(s_ready, 1)

            def chunk_max(b, par, c):
                dve.wait_ge(s_ready, NC * b + c + 1)
                return nc.vector.reduce_max(mx4[:, c:c + 1], sc[par][0:S, 512 * c:512 * c + width(c)], AX.X)

            def split_ctx(b, par, c):
                first, last = CH * c, min(CH * (c + 1), NKT)
                dve.wait_ge(ctx_loaded[par][c], 16 * (b // 2 + 1) if isinstance(b, int) else 16 * ((b - par) // 2 + 1))
                if not (isinstance(b, int) and b == 0):
                    dve.wait_ge(pv_done, NC * (b - 1) + c + 1)
                nc.vector.tensor_copy(nat_hi[:, first:last, :], raw[par][:, first:last, :]).then_inc(nat_hi_ready, 1)

            def step_to(ins_, n):
                ins_.then_inc(dve_step, 1)
                dve.wait_ge(dve_step, n)

            base = steps[0]

            def max_stage(b, par):
                n = base + 3 * b
                step_to(chunk_max(b, par, 3), n + 1)
                step_to(nc.vector.reduce_max(mx[:, 0:1], mx4[:, :], AX.X), n + 2)
                step_to(nc.vector.tensor_tensor(mx[:, 1:2], mx[:, 0:1], pb[:, bass.ds(b, 1)], ALU.add), n + 3)
                if not (isinstance(b, int) and b < 2):
                    dve.wait_ge(exp_done, b - 1)
                nc.vector.tensor_tensor(nbias[par][:, :], pb[:, bass.ds(b, 1)], mx[:, 1:2], ALU.subtract).then_inc(max_ready, 1)

            def prob_parts(b):
                for h, (t0, t1) in enumerate(PT_SPLIT):
                    dve.wait_ge(pt_hi, 2 * b + h + 1)
                    nc.vector.tensor_tensor(pT[:, t0:t1, S:2 * S], PB[h][:, 0:(t1 - t0) * S].rearrange("p (j s) -> p j s", s=S),
                                            pT[:, t0:t1, 0:S].bitcast(f32), ALU.subtract).then_inc(pt_lo, 1)

            def stage(b, par, scores=True, values=True, earlier=True):
                n, npar = b + 1, 1 - par
                if scores:
                    evacuate(n, 0)
                if values:
                    split_ctx(b, par, 0)
                if scores:
                    evacuate(n, 1)
                if values:
                    split_ctx(b, par, 1)
                    prob_parts(b)
                    if earlier:
                        dve.wait_ge(av_ready, b)
                    dve.wait_ge(exp_done, b + 1)
                    nc.vector.reciprocal(rinv[:, :], rsum[par][:, :]).then_inc(rinv_ready, 1)
                if scores:
                    add_scores(n, npar, 0)
                    evacuate(n, 2)
                    chunk_max(n, npar, 0)
                if values:
                    split_ctx(b, par, 2)
                if scores:
                    add_scores(n, npar, 1)
                    evacuate(n, 3)
                    chunk_max(n, npar, 1)
                if values:
                    split_ctx(b, par, 3)
                if scores:
                    add_scores(n, npar, 2)
                    chunk_max(n, npar, 2)
                    add_scores(n, npar, 3)
                if values:
                    dve.wait_ge(pv_low_ready, b + 1)
                    nc.vector.tensor_tensor(pv_low[:, :], VB[0:S, :], pv_low[:, :], ALU.add).then_inc(av_sum, 1)
                if scores:
                    max_stage(n, npar)

            dve.wait_ge(sc_zeroed, 2)
            stage(-1, 1, values=False, earlier=False)
            stage(0, 0, earlier=False)
            with dve.Fori(0, B // 2 - 1) as i:
                stage(2 * i + 1, 1)
                stage(2 * i + 2, 0)
            stage(B - 1, 1, scores=False)
            for k in range(KD):
                dve.wait_ge(WT_hi_ready, k + 1)
                nc.vector.tensor_tensor(WT_lo[:, k, :], bank[k][:, :], WT_hi[:, k, :].bitcast(f32), ALU.subtract).then_inc(WT_lo_ready, 1)
            dve.wait_ge(avT_hi_ready, 1)
            nc.vector.tensor_tensor(avT_lo[:, :, :], avT[:, :, :], avT_hi[:, :, :].bitcast(f32), ALU.subtract).then_inc(avT_lo_ready, 1)
            dve.wait_ge(b_loaded, 32)
            for t in range(NT):
                dve.wait_ge(xo_done, t + 1)
                step_to(nc.vector.tensor_tensor(xo[:, t, :], bank[t][:, :], b_bc[:, :], ALU.add), base + 3 * B + t + 1)
                nc.vector.scalar_tensor_tensor(xt[:, t, :], xo[:, t, :], 0.0, xt[:, t, :], ALU.max, ALU.add).then_inc(x1_ready, 1)

            steps[0] = base + 3 * B + NT

            def norm_stats(src, n):
                for t in range(NT):
                    last = nc.vector.bn_stats(stats[:, t, :], src[:, t, :])
                link(last)
                for t in range(NT):
                    last = nc.vector.bn_aggr(mv[:, t, :], stats[:, t, :])
                link(last)
                nc.vector.tensor_scalar(rstd[:, :], mv[:, :, 1], EPS, None, ALU.add).then_inc(var_ready, 1)
                dve.wait_ge(rstd_ready, n)

            def normalise(dst, src, t):
                return nc.vector.tensor_scalar(dst[:, t, :], src[:, t, :], mv[:, t, 0:1], rstd[:, t:t + 1], ALU.subtract, ALU.mult)

            def gained(src):
                for t in range(NT):
                    last = normalise(xn, src, t)
                link(last)
                for t in range(NT):
                    last = nc.vector.tensor_tensor(xn[:, t, :], xn[:, t, :], gain[:, :], ALU.mult)
                link(last)
                for t in range(NT):
                    nc.vector.tensor_tensor(xn[:, t, :], xn[:, t, :], shift[:, :], ALU.add).then_inc(xn_ready, 1)

            def split_w(u):
                dve.wait_ge(*upper(u))
                if u >= RING:
                    dve.wait_ge(*USED[u - RING])
                nc.vector.tensor_tensor(w_lo[u % RING][:, :, :], w_raw[u % RING][:, :, :], w_hi[u % RING][:, :, :].bitcast(f32),
                                        ALU.subtract).then_inc(w_lo_ready[u % RING], 1)

            def lower_xT(n):
                for k in range(KD):
                    dve.wait_ge(xT_hi_ready, KD * n + k + 1)
                    nc.vector.tensor_tensor(xT_lo[:, k, :], bank[k][:, :], xT_hi[:, k, :].bitcast(f32), ALU.subtract).then_inc(xT_lo_ready, 1)

            dve.wait_ge(x1_ready, NT)
            nc.vector.memset(zeros[:, :], 0.0).then_inc(zeros_ready, 1)
            nc.vector.memset(proj2[:, :], 0.0).then_inc(proj_zero, 1)
            nc.vector.memset(v1[:, :, :, DH:DH + 1], 1.0).then_inc(v_one, 1)
            norm_stats(xt, 2)
            for t in range(NT):
                last = normalise(x1n, xt, t)
            link(last)
            norm_stats(x1n, 3)
            dve.wait_ge(vec_loaded, 48)
            gained(x1n)
            dve.wait_ge(proj_hi_ready, 1)
            nc.vector.tensor_tensor(proj2_lo[:, :], proj2[:, :], proj2_hi[:, :].bitcast(f32), ALU.subtract).then_inc(proj_lo_ready, 1)
            split_w(0)
            lower_xT(0)
            split_w(1)
            split_w(2)

            def lower_z(n):
                dve.wait_ge(z_hi_ready, n + 1)
                nc.vector.tensor_tensor(z_lo[n % 2][:, :], bank[n % 2][:, :], z_hi[n % 2][:, :].bitcast(f32), ALU.subtract).then_inc(z_lo_ready, 1)

            def negative(n):
                dve.wait_ge(f_done, n + 1)
                nc.vector.tensor_scalar(neg[n % 2][:, :], bank[2 + n % 2][:, :], 0.0, None, ALU.min).then_inc(neg_ready, 1)

            def feature(n):
                dve.wait_ge(e_ready, n + 1)
                nc.vector.scalar_tensor_tensor(phi[n // 8][:, n % 8, :], bank[2 + n % 2][:, :], 0.0, neg[n % 2][:, :],
                                               ALU.max, ALU.add).then_inc(phi_ready, 1)

            for n in range(H):
                lower_z(n)
                if n >= 1:
                    negative(n - 1)
                if n % 4 == 0 and n // 4 + 2 >= RING:
                    split_w(n // 4 + 2)
                if n >= 1:
                    feature(n - 1)
            negative(H - 1)
            feature(H - 1)
            for u in range(2):
                dve.wait_ge(v_ready, NT * (u + 1))
                split_w(6 + u)
            dve.wait_ge(mask_ready, 1)
            NG = 4 * NT

            def masked(n):
                dve.wait_ge(a_done, n + 1)
                if n >= 2:
                    dve.wait_ge(o_done, n - 1)
                nc.vector.tensor_tensor(at[n % 2][:, :, :], bank[n % 4][:, :].rearrange("p (h q) -> p h q", h=4),
                                        mask[:, :].unsqueeze(1).to_broadcast([P, 4, P]), ALU.mult).then_inc(a_ready, 1)

            def divided(n):
                t, g, s = n // 4, n // 2 % 2, n % 2
                o = bank[6 + n % 2][:, 0:4 * (DH + 1)].rearrange("p (h d) -> p h d", d=DH + 1)
                dve.wait_ge(o_done, n + 1)
                link(nc.vector.tensor_scalar(den[:, 0, :], o[:, :, DH], 1e-6, None, ALU.add))
                link(nc.vector.reciprocal(den[:, 1, :], den[:, 0, :]))
                if n % 4 == 0 and t >= 2:
                    dve.wait_ge(oT_done, 2 * (t - 1))
                dst = heads[:, t % 2, :].rearrange("p (m s d) -> p m s d", s=2, d=DH)[:, 4 * g:4 * (g + 1), s, :]
                nc.vector.tensor_tensor(dst, o[:, :, 0:DH], den[:, 1, :].unsqueeze(2).to_broadcast([P, 4, DH]), ALU.mult).then_inc(o_ready, 1)

            def lower_oT(t):
                for half in range(2):
                    dve.wait_ge(oT_hi_ready, 2 * t + half + 1)
                    nc.vector.tensor_tensor(oT_lo[:, 4 * half:4 * (half + 1), :], bank[4 + half][:, :].rearrange("p (k n) -> p k n", n=P),
                                            oT_hi[:, 4 * half:4 * (half + 1), :].bitcast(f32), ALU.subtract).then_inc(oT_lo_ready, 1)

            def attended(t):
                dve.wait_ge(ao_done, t + 1)
                nc.vector.tensor_tensor(x1n[:, t, :], x1n[:, t, :], bank[6 + t % 2][:, :], ALU.add).then_inc(xa_ready, 1)

            for t in range(NT):
                for n in range(4 * t, 4 * t + 4):
                    masked(n)
                    if n % 4 >= 1:
                        divided(n - 1)
                divided(4 * t + 3)
                lower_oT(t)
                if t == 0:
                    split_w(8)
                attended(t)
            dve.wait_ge(xa_ready, NT)
            norm_stats(x1n, 4)
            dve.wait_ge(vec2_loaded, 32)
            gained(x1n)
            split_w(9)
            lower_xT(1)
            split_w(10)
            for n in range(FF // P):
                dve.wait_ge(gelu_ready, n + 1)
                if n >= 2:
                    dve.wait_ge(dn_done, n - 1)
                nc.vector.tensor_copy(gl_hi[n % 2][:, :], gl[n % 2][:, :]).then_inc(gl_hi_ready, 1)
                dve.wait_ge(gl_hi_ready, n + 1)
                nc.vector.tensor_tensor(gl_lo[n % 2][:, :], gl[n % 2][:, :], gl_hi[n % 2][:, :].bitcast(f32), ALU.subtract).then_inc(gl_lo_ready, 1)
                if n % 4 == 3 and n < FF // P - 1:
                    split_w(11 + 2 * (n // 4))
                if n % 4 == 0 and 4 <= n < FF // P - 4:
                    split_w(10 + n // 2)
            for t in range(NT):
                last = nc.vector.tensor_tensor(xt[:, t, :], xt[:, t, :], x1n[:, t, :], ALU.add)
            link(last)
            for t in range(NT):
                last = nc.vector.tensor_tensor(xt[:, t, :], xt[:, t, :], b2_bc[:, :], ALU.add)
            link(last)
            dve.wait_ge(dn_done, FF // P)
            for t in range(NT):
                nc.vector.tensor_tensor(xt[:, t, :], xt[:, t, :], bank[4 + t][:, :], ALU.add).then_inc(x2_ready, 1)

            dve.wait_ge(x2_ready, NT)
            norm_stats(xt, 5)
            for t in range(NT):
                normalise(xn, xt, t).then_inc(xn_ready, 1)
            dve.wait_ge(index_ready, 1)
            link(nc.vector.tensor_copy(e_idx[:, :], e_int[:, :]))
            nc.vector.tensor_scalar(pref[:, :], e_idx[:, :], -1.0, float(E), ALU.mult, ALU.add)
            link(nc.vector.tensor_scalar(low_slot[:, :], e_idx[:, :], float(P), None, ALU.mult))

            def over_tokens(a):
                return a.unsqueeze(1).to_broadcast([P, NT, E])

            def over_experts(a):
                return a.unsqueeze(2).to_broadcast([P, NT, E])

            dve.wait_ge(logits_done, 1)
            link(nc.vector.tensor_copy(logits[:, :, :], bank[4][:, 0:NT * E].rearrange("p (t e) -> p t e", e=E)))
            for k in range(2):
                link(nc.vector.reduce_max(best[k][:, :], logits[:, :, :], AX.X))
                link(nc.vector.tensor_tensor(scr[:, :, :], logits[:, :, :], over_experts(best[k][:, :]), ALU.is_equal))
                link(nc.vector.tensor_tensor(scr[:, :, :], scr[:, :, :], over_tokens(pref[:, :]), ALU.mult))
                link(nc.vector.reduce_max(top[:, :], scr[:, :, :], AX.X))
                link(nc.vector.tensor_tensor(pick[k][:, :, :], scr[:, :, :], over_experts(top[:, :]), ALU.is_equal))
                if k == 0:
                    link(nc.vector.scalar_tensor_tensor(logits[:, :, :], pick[0][:, :, :], -3e38, logits[:, :, :], ALU.mult, ALU.add))
            nc.vector.tensor_tensor(chosen[:, :, :], pick[0][:, :, :], pick[1][:, :, :], ALU.add).then_inc(chosen_ready, 1)
            nc.vector.tensor_tensor(gap[:, :], best[1][:, :], best[0][:, :], ALU.subtract).then_inc(gap_ready, 1)
            dve.wait_ge(rank_done, 1)
            nc.vector.tensor_copy(rank[:, :, :], bank[5][:, 0:NT * E].rearrange("p (t e) -> p t e", e=E))
            link(nc.vector.tensor_copy(count[:, :], bank[5][:, NT * E:(NT + 1) * E]))
            link(nc.vector.tensor_scalar(extra[:, :], count[:, :], float(P), None, ALU.is_gt))
            for n in range(2, B * S // P):
                link(nc.vector.scalar_tensor_tensor(extra[:, :], count[:, :], float(n * P), extra[:, :], ALU.is_gt, ALU.add))
            dve.wait_ge(order_ready, 2)
            link(nc.vector.tensor_tensor(scr8[:, :, :], upto[:, :, :], extra[:, :].unsqueeze(1).to_broadcast([P, E, E]), ALU.mult))
            link(nc.vector.tensor_reduce(upto_extra[:, :], scr8[:, :, :], AX.X, ALU.add))
            link(nc.vector.tensor_tensor(shift8[:, :], upto_extra[:, :], extra[:, :], ALU.subtract))
            link(nc.vector.tensor_tensor(shift8[:, :], shift8[:, :], e_idx[:, :], ALU.subtract))
            link(nc.vector.tensor_scalar(shift8[:, :], shift8[:, :], float(E - 1), float(P), ALU.add, ALU.mult))
            link(nc.vector.tensor_scalar(scr[:, :, :], rank[:, :, :], float(P), None, ALU.is_ge))
            link(nc.vector.tensor_tensor(scr[:, :, :], scr[:, :, :], over_tokens(shift8[:, :]), ALU.mult))
            link(nc.vector.tensor_tensor(rank[:, :, :], rank[:, :, :], scr[:, :, :], ALU.add))
            link(nc.vector.tensor_tensor(rank[:, :, :], rank[:, :, :], over_tokens(low_slot[:, :]), ALU.add))
            for k in range(2):
                link(nc.vector.tensor_tensor(scr[:, :, :], rank[:, :, :], pick[k][:, :, :], ALU.mult))
                link(nc.vector.tensor_reduce(slotf[k][:, :], scr[:, :, :], AX.X, ALU.add))
                nc.vector.tensor_copy(slot_of[k][:, :], slotf[k][:, :]).then_inc(slots_ready, 1)
            link(nc.vector.tensor_tensor(scr8[:, 0:OV, :], upto_extra[:, :].unsqueeze(1).to_broadcast([P, OV, E]),
                                         e_idx[:, 0:OV].unsqueeze(2).to_broadcast([P, OV, E]), ALU.is_le))
            link(nc.vector.tensor_reduce(ovf[:, :], scr8[:, 0:OV, :], AX.X, ALU.add))
            nc.vector.tensor_scalar(block_expert[:, :], ovf[:, :], float(E - 1), None, ALU.min).then_inc(slots_ready, 1)
            dve.wait_ge(gap_exp, 1)
            link(nc.vector.tensor_scalar(gap[:, :], gsum[:, :], 1.0, None, ALU.add))
            link(nc.vector.reciprocal(gate[0][:, :], gap[:, :]))
            link(nc.vector.tensor_tensor(gate[1][:, :], gate[0][:, :], gsum[:, :], ALU.mult))

            def split_e(b, j):
                if j in POOL_UNITS:
                    return
                dve.wait_ge(w_hi_ready[slot(j)], turn_of(b, j))
                nc.vector.tensor_tensor(w_lo[slot(j)][:, :, :], w_raw[slot(j)][:, :, :], w_hi[slot(j)][:, :, :].bitcast(f32),
                                        ALU.subtract).then_inc(w_lo_ready[slot(j)], 1)

            def lower_rows(b):
                dve.wait_ge(xgT_hi_ready, b + 1)
                nc.vector.tensor_tensor(xgT_lo[:, :, :], bank[7][:, :].rearrange("p (k n) -> p k n", n=P), xgT_hi[:, :, :].bitcast(f32),
                                        ALU.subtract).then_inc(xgT_lo_ready, 1)

            def hidden(b, half):
                dve.wait_ge(silu_ready, 2 * b + half + 1)
                dve.wait_ge(unit_done, EU * b + 2 * half + 2)
                nc.vector.tensor_tensor(hm[half][:, :], bank[2 * half + 1][:, :], sg[half][:, :], ALU.mult).then_inc(hm_ready, 1)

            def lower_hidden(b, half):
                dve.wait_ge(hmT_hi_ready, 2 * b + half + 1)
                nc.vector.tensor_tensor(hmT_lo[half][:, :, :], bank[4 + half][:, :].rearrange("p (k n) -> p k n", n=P),
                                        hmT_hi[half][:, :, :].bitcast(f32), ALU.subtract).then_inc(hmT_lo_ready, 1)

            def expert_block(b, last=False):
                split_e(b, 3)
                hidden(b, 0)
                split_e(b, 4)
                split_e(b, 5)
                lower_hidden(b, 0)
                hidden(b, 1)
                if not last:
                    split_e(b + 1, 0)
                    lower_rows(b + 1)
                lower_hidden(b, 1)
                if not last:
                    split_e(b + 1, 1)
                    split_e(b + 1, 2)

            for j in range(RING):
                split_e(0, j)
            lower_rows(0)
            expert_block(0)
            with dve.Fori(1, NB - 1) as b:
                expert_block(b)
            expert_block(NB - 1, last=True)
            for t in range(NT):
                dve.wait_ge(gathered[t], 32)
                for k in range(2):
                    mm = nc.vector.scalar_tensor_tensor(xt[:, t, :], yt[k][:, t, :], gate[k][:, t:t + 1], xt[:, t, :], ALU.mult, ALU.add)
                    if k == 0:
                        link(mm)
                mm.then_inc(xo_ready, 1)

        @block.tensor
        def _(pe):
            def product(dst, left, right, first=True, last=True):
                n = len(left)
                for k, ((lh, ll), (rh, rl)) in enumerate(zip(left, right)):
                    nc.tensor.matmul(dst, lh, rh, start=first and k == 0, stop=False)
                    nc.tensor.matmul(dst, lh, rl, start=False, stop=False)
                    mm = nc.tensor.matmul(dst, ll, rh, start=False, stop=last and k == n - 1)
                return mm

            def turn(dst, src, waited):
                if waited:
                    return nc.tensor.matmul(dst, src, ident[0:S, 0:S], start=True, stop=True)
                return nc.tensor.transpose(dst, src, ident[0:S, 0:S])

            pe.wait_ge(const_ready, 1)
            pe.wait_ge(pn_ready, NT)
            for k in range(KD):
                for t in range(NT):
                    mm = nc.tensor.transpose(bank[k][:, t * P:(t + 1) * P], pn[:, t, k * P:(k + 1) * P], ident[:, :])
                mm.then_inc(pnT_done, 1)
            pe.wait_ge(W_lo_ready, 1)
            pe.wait_ge(pnT_lo_ready, KD)
            for m in range(KD):
                product(bank[m][:, :], [(W_hi[:, k, m * P:(m + 1) * P], W_lo[:, k, m * P:(m + 1) * P]) for k in range(KD)],
                        [(pnT_hi[:, k, :], pnT_lo[:, k, :]) for k in range(KD)]).then_inc(pwT_done, 1)
            pe.wait_ge(b_loaded, 16)
            for b in range(B):
                for k in range(KD):
                    mm = nc.tensor.matmul(bank[4][0:S, b:b + 1], pnT[:, k, b * S:(b + 1) * S], b_col[:, k:k + 1],
                                          start=k == 0, stop=k == KD - 1)
            mm.then_inc(pb_done, 1)
            pe.wait_ge(pw_lo_ready, KD)
            pe.wait_ge(pb_ready, 1)

            def transposes(b, par, c):
                pe.wait_ge(ctx_loaded[par][c], 16 * (b // 2 + 1) if isinstance(b, int) else 16 * ((b - par) // 2 + 1))
                tiles = range(CH * c, min(CH * (c + 1), NKT))
                for g, ks in groups(c):
                    before = t_before(b, g)
                    if before is not None:
                        pe.wait_ge(t_lo, before)
                    for k in ks:
                        for n, j in enumerate(tiles):
                            rows = P if j < FULL else REMP
                            at = (k - ks[0]) * P + n * P
                            mm = nc.tensor.transpose(t_bank(g)[:, at:at + rows], raw[par][0:rows, j, k * P:(k + 1) * P],
                                                     ident[0:rows, 0:rows])
                    mm.then_inc(t_done, 1)

            def scores(b, par, c):
                g_last = groups(c)[-1][0]
                pe.wait_ge(t_lo, G * b + g_last + 1)
                if c >= 2:
                    pe.wait_ge(s_ready, NC * b + c - 1)
                elif not (isinstance(b, int) and b == 0):
                    pe.wait_ge(s_ready, NC * (b - 1) + NC - 2 + c + 1)
                n = width(c) if c < NC - 1 else REMP
                for k in range(KD):
                    nc.tensor.matmul(SB[c % 2][:, 0:n], pw[par][:, k, :], ct_hi[c % 2][:, k, 0:n], start=k == 0, stop=False)
                    mm = nc.tensor.matmul(SB[c % 2][:, 0:n], pw[par][:, k, :], ct_lo[c % 2][:, k, 0:n], start=False, stop=k == KD - 1)
                mm.then_inc(qk_done, 1)

            def av_transposes(b):
                pe.wait_ge(av_ready, b + 1)
                for k in range(KD):
                    mm = turn(VB[:, k * S:(k + 1) * S], av[:, k * P:(k + 1) * P], k == 0)
                mm.then_inc(avt_done, 1)

            def prob_transposes(b, par):
                pe.wait_ge(exp_done, b + 1)
                for h, (t0, t1) in enumerate(PT_SPLIT):
                    if not (isinstance(b, int) and b == 0):
                        pe.wait_ge(pt_lo, 2 * (b - 1) + h + 1)
                    for j in range(t0, t1):
                        mm = turn(PB[h][:, (j - t0) * S:(j - t0 + 1) * S], sc[par][:, j * P:(j + 1) * P], j == t0)
                    mm.then_inc(pt_done, 1)

            def values_of(b, c):
                if c == 0 and not (isinstance(b, int) and b == 0):
                    pe.wait_ge(avt_ready, b)
                for h, (t0, t1) in enumerate(PT_SPLIT):
                    if CH * c == t0:
                        pe.wait_ge(pt_lo, 2 * b + h + 1)
                pe.wait_ge(nat_lo_ready, NC * b + c + 1)
                for j in range(CH * c, min(CH * (c + 1), NKT)):
                    nc.tensor.matmul(VB[:, :], pT[:, j, :], nat_hi[:, j, :], start=j == 0, stop=False)
                    mm = nc.tensor.matmul(VB[:, :], pT[:, j, :], nat_lo[:, j, :], start=False, stop=j == NKT - 1)
                mm.then_inc(pv_done, 1)

            def stage(b, par, scores_too=True, values=True, earlier=True):
                n, npar = b + 1, 1 - par
                if scores_too:
                    transposes(n, npar, 0)
                if earlier:
                    av_transposes(b - 1)
                if scores_too:
                    transposes(n, npar, 1)
                if values:
                    prob_transposes(b, par)
                if scores_too:
                    pe.wait_ge(pw_ready, n + 1)
                    scores(n, npar, 0)
                if values:
                    values_of(b, 0)
                if scores_too:
                    transposes(n, npar, 2)
                    scores(n, npar, 1)
                if values:
                    values_of(b, 1)
                if scores_too:
                    transposes(n, npar, 3)
                    scores(n, npar, 2)
                if values:
                    values_of(b, 2)
                    values_of(b, 3)
                if scores_too:
                    scores(n, npar, 3)

            stage(-1, 1, values=False, earlier=False)
            stage(0, 0, earlier=False)
            with pe.Fori(0, B // 2 - 1) as i:
                stage(2 * i + 1, 1)
                stage(2 * i + 2, 0)
            stage(B - 1, 1, scores_too=False)
            pe.wait_ge(W_loaded, 32)
            for k in range(KD):
                for m in range(KD):
                    mm = nc.tensor.transpose(bank[k][:, m * P:(m + 1) * P], We[:, m, k * P:(k + 1) * P], ident[:, :])
                mm.then_inc(WT_done, 1)
            av_transposes(B - 1)
            pe.wait_ge(WT_lo_ready, KD)
            pe.wait_ge(avT_lo_ready, 1)
            for t in range(NT):
                product(bank[t][:, :], [(avT_hi[:, k, t * P:(t + 1) * P], avT_lo[:, k, t * P:(t + 1) * P]) for k in range(KD)],
                        [(WT_hi[:, k, :], WT_lo[:, k, :]) for k in range(KD)]).then_inc(xo_done, 1)

            def parts(u):
                return w_hi[u % RING], w_lo[u % RING]

            def transpose_xn(n):
                pe.wait_ge(xn_ready, NT * (n + 1))
                for k in range(KD):
                    for t in range(NT):
                        mm = nc.tensor.transpose(bank[k][:, t * P:(t + 1) * P], xn[:, t, k * P:(k + 1) * P], ident[:, :])
                    mm.then_inc(xT_done, 1)
                pe.wait_ge(xT_lo_ready, KD * (n + 1))

            xT = [(xT_hi[:, k, :], xT_lo[:, k, :]) for k in range(KD)]

            def columns(u, m):
                hi, lo = parts(u)
                return [(hi[:, k, m * P:(m + 1) * P], lo[:, k, m * P:(m + 1) * P]) for k in range(KD)]

            def rows(u):
                hi, lo = parts(u)
                return [(hi[:, k, :], lo[:, k, :]) for k in range(KD)]

            pe.wait_ge(x1_ready, NT)
            transpose_xn(0)

            def features(n):
                pe.wait_ge(z_lo_ready, n + 1)
                if n >= 2:
                    pe.wait_ge(phi_ready, n - 1)
                product(bank[2 + n % 2][:, :], [(proj2_hi[:, :], proj2_lo[:, :])], [(z_hi[n % 2][:, :], z_lo[n % 2][:, :])]).then_inc(f_done, 1)

            pe.wait_ge(proj_lo_ready, 1)
            for n in range(H):
                u = n // 4
                if n % 4 == 0:
                    pe.wait_ge(*lower(u))
                if n >= 2:
                    pe.wait_ge(z_lo_ready, n - 1)
                product(bank[n % 2][:, :], columns(u, n % 4), xT).then_inc(z_done, 1)
                if n >= 1:
                    features(n - 1)
            features(H - 1)
            for u in range(2):
                pe.wait_ge(*lower(4 + u))
                for t in range(NT):
                    n = NT * u + t
                    if n >= 2:
                        pe.wait_ge(v_ready, n - 1)
                    product(bank[4 + n % 2][:, :], [(hi[:, t * P:(t + 1) * P], lo[:, t * P:(t + 1) * P]) for hi, lo in xT],
                            rows(4 + u)).then_inc(v_done, 1)
            pe.wait_ge(v_ready, 2 * NT)
            pe.wait_ge(v_one, 1)
            pe.wait_ge(phi_ready, H)

            def weights(n):
                t, g, s = n // 4, n // 2 % 2, n % 2
                if n >= 4:
                    pe.wait_ge(a_ready, n - 3)
                half = slice(DH * s, DH * (s + 1))
                for m in range(4):
                    k, q = (phi[i][half, 4 * g + m, t * P:(t + 1) * P] for i in (1, 0))
                    mm = nc.tensor.matmul(bank[n % 4][:, m * P:(m + 1) * P], k, q, start=True, stop=True)
                mm.then_inc(a_done, 1)

            def weighted(n):
                t, g, s = n // 4, n // 2 % 2, n % 2
                pe.wait_ge(a_ready, n + 1)
                if n >= 2:
                    pe.wait_ge(o_ready, n - 1)
                if t and n % 4 < 2:
                    pe.wait_ge(xa_ready, t)
                for m in range(4):
                    head = 2 * (4 * g + m) + s
                    mm = nc.tensor.matmul(bank[6 + n % 2][:, m * (DH + 1):(m + 1) * (DH + 1)], at[n % 2][:, m, :], v1[:, t, head, :],
                                          start=True, stop=True)
                mm.then_inc(o_done, 1)

            for t in range(NT):
                for n in range(4 * t, 4 * t + 4):
                    weights(n)
                    if n % 4 >= 1:
                        weighted(n - 1)
                weighted(4 * t + 3)
                pe.wait_ge(o_ready, 4 * t + 4)
                for half in range(2):
                    if t >= 1:
                        pe.wait_ge(oT_lo_ready, 2 * t - 1 + half)
                    for k in range(4):
                        at_ = (4 * half + k) * P
                        mm = nc.tensor.transpose(bank[4 + half][:, k * P:(k + 1) * P], heads[:, t % 2, at_:at_ + P], ident[:, :])
                    mm.then_inc(oT_done, 1)
                pe.wait_ge(oT_lo_ready, 2 * t + 2)
                pe.wait_ge(*lower(6))
                pe.wait_ge(*lower(7))
                product(bank[6 + t % 2][:, :], [(oT_hi[:, k, :], oT_lo[:, k, :]) for k in range(HD // P)],
                        rows(6) + rows(7)).then_inc(ao_done, 1)
            transpose_xn(1)

            def down(n):
                if n % 4 == 0:
                    pe.wait_ge(*lower(9 + 2 * (n // 4)))
                hi, lo = parts(9 + 2 * (n // 4))
                pe.wait_ge(gl_lo_ready, n + 1)
                for t in range(NT):
                    left = (gl_hi[n % 2][:, t * P:(t + 1) * P], gl_lo[n % 2][:, t * P:(t + 1) * P])
                    mm = product(bank[4 + t][:, :], [left], [(hi[:, n % 4, :], lo[:, n % 4, :])], n == 0, n == FF // P - 1)
                mm.then_inc(dn_done, 1)

            for n in range(FF // P):
                u = 8 + 2 * (n // 4)
                if n % 4 == 0:
                    pe.wait_ge(*lower(u))
                if n >= 2:
                    pe.wait_ge(gelu_ready, n - 1)
                product(bank[n % 2][:, :], columns(u, n % 4), xT).then_inc(up_done, 1)
                if n >= 1:
                    down(n - 1)
            down(FF // P - 1)

            pe.wait_ge(xn_ready, 3 * NT)
            pe.wait_ge(gelu_ready, FF // P)
            for k in range(KD):
                for t in range(NT):
                    mm = nc.tensor.transpose(bank[k][:, t * P:(t + 1) * P], xn[:, t, k * P:(k + 1) * P], ident[:, :])
                mm.then_inc(xT_done, 1)
            pe.wait_ge(xT32_ready, KD)
            pe.wait_ge(router_loaded, 16)
            for t in range(NT):
                for k in range(KD):
                    mm = nc.tensor.matmul(bank[4][:, t * E:(t + 1) * E], xT32[:, k, t * P:(t + 1) * P], w_router[:, k, :],
                                          start=k == 0, stop=k == KD - 1)
            mm.then_inc(logits_done, 1)
            pe.wait_ge(chosen_ready, 1)
            pe.wait_ge(order_ready, 2)
            for t in range(NT + 1):
                for m in range(min(t + 1, NT)):
                    mm = nc.tensor.matmul(bank[5][:, t * E:(t + 1) * E], before[:, :] if m == t else ones[:, :], chosen[:, m, :],
                                          start=m == 0, stop=m == min(t, NT - 1))
            mm.then_inc(rank_done, 1)

            def wait_unit(b, j):
                pe.wait_ge(w_lo_ready[slot(j)], turn_of(b, j))

            def rows_transposed(b):
                pe.wait_ge(xg_loaded, 16 * (b + 1))
                for k in range(KD):
                    mm = nc.tensor.transpose(bank[7][:, k * P:(k + 1) * P], xg[:, k * P:(k + 1) * P], ident[:, :])
                mm.then_inc(xgT_done, 1)

            def unit_rows(j):
                return [(w_hi[slot(j)][:, k, :], w_lo[slot(j)][:, k, :]) for k in range(KD)]

            def up(b, j):
                wait_unit(b, j)
                product(bank[j][:, :], [(xgT_hi[:, k, :], xgT_lo[:, k, :]) for k in range(KD)], unit_rows(j)).then_inc(unit_done, 1)

            def hidden_transposed(b, half):
                pe.wait_ge(hm_ready, 2 * b + half + 1)
                for k in range(4):
                    mm = nc.tensor.transpose(bank[4 + half][:, k * P:(k + 1) * P], hm[half][:, k * P:(k + 1) * P], ident[:, :])
                mm.then_inc(hmT_done, 1)

            def down_half(b, half):
                wait_unit(b, 4 + half)
                pe.wait_ge(hmT_lo_ready, 2 * b + half + 1)
                product(bank[6][:, :], [(hmT_hi[half][:, k, :], hmT_lo[half][:, k, :]) for k in range(4)], unit_rows(4 + half),
                        half == 0, half == 1).then_inc(unit_done, 1)

            def expert_block(b, last=False):
                pe.wait_ge(xgT_lo_ready, b + 1)
                up(b, 0)
                up(b, 1)
                up(b, 2)
                hidden_transposed(b, 0)
                up(b, 3)
                if not last:
                    rows_transposed(b + 1)
                if not (isinstance(b, int) and b == 0):
                    pe.wait_ge(y_ready, b)
                down_half(b, 0)
                hidden_transposed(b, 1)
                down_half(b, 1)

            rows_transposed(0)
            expert_block(0)
            with pe.Fori(1, NB - 1) as b:
                expert_block(b)
            expert_block(NB - 1, last=True)


def kernel(**inputs):
    import numpy as _np
    import concourse.bacc as _bacc
    from concourse import mybir as _mybir
    from concourse.bass_utils import run_bass_kernel_spmd as _run

    nc = _bacc.Bacc("TRN2", target_bir_lowering=False, num_devices=1)
    arrays, args = {}, {}
    for name in inputs:
        a = _np.ascontiguousarray(inputs[name])
        arrays[f"in_{name}_dram"] = a
        args[name] = nc.dram_tensor(f"in_{name}_dram", a.shape, _mybir.dt.from_np(a.dtype), kind="ExternalInput").ap()
    out = nc.dram_tensor("out_0_dram", inputs["x"].shape, _mybir.dt.float32, kind="ExternalOutput").ap()
    perceiver_block(nc, args, out)
    r = _run(nc, [arrays], core_ids=[0])
    return r.results[0]["out_0_dram"]
```

```python
import concourse.bass as bass
from concourse import mybir
from contextlib import ExitStack


def perceiver_block(nc, ins, out):
    f32, f32r = mybir.dt.float32, mybir.dt.float32r
    ACT = mybir.ActivationFunctionType
    ALU = mybir.AluOpType
    AX = mybir.AxisListType

    P = 128
    B, S, D = ins["x"].shape
    KEYS = ins["ctx_1024"].shape[1]
    NT = B * S // P
    KD = D // P
    CH = 4
    FULL = KEYS // P
    NC = FULL // CH + 1
    REM = KEYS - FULL * P
    REMP = REM + REM % 2
    NKT = FULL + 1
    assert FULL % CH == 0 and REM > 0
    EPS = 1e-5

    H, DH = 16, 64
    HD = H * DH
    FF = ins["L0_attn_w1"].shape[1]
    E, _, FE = ins["L0_ffn_w0"].shape
    OV = 7
    NB = E + OV
    RING = 3
    assert HD == 2 * 512 and FE == 2 * 512 and D == 512 and FF == 4 * 512
    assert 2 * B * S <= (OV + 1) * P and E <= OV + 1

    x_v = ins["x"].rearrange("b s d -> (b s) d").rearrange("(t p) d -> p t d", p=P)
    out_v = out.rearrange("b s d -> (b s) d").rearrange("(t p) d -> p t d", p=P)

    with ExitStack() as ctx:
        def sb(name, shape, dt=f32, scope=ctx):
            return scope.enter_context(nc.sbuf_tensor(name, shape, dt))

        def sem(name):
            return ctx.enter_context(nc.semaphore(name))

        bank = [ctx.enter_context(nc.psum_tensor(f"bank{i}", [P, 512], f32)) for i in range(8)]

        ident = sb("ident", [P, P])
        xt = sb("xt", [P, NT, D])
        stats = sb("stats", [P, NT, 6])
        mv = sb("mv", [P, NT, 2])
        rstd = sb("rstd", [P, NT])
        mhalf = sb("mhalf", [P, NT])

        xscope = ExitStack()
        b_col = sb("b_col", [P, KD], f32, xscope)
        avT = sb("avT", [P, KD, B * S], f32, xscope)
        pw_all = sb("pw_all", [P, KD, B, P], f32r, xscope)
        pw = [sb(f"pw{i}", [P, KD, P], f32r, xscope) for i in range(2)]
        pb = sb("pb", [S, B], f32, xscope)
        sc = [sb(f"sc{i}", [S, NKT * P], f32, xscope) for i in range(2)]
        sc_low = [sb(f"sc_low{i}", [S, 512], f32, xscope) for i in range(2)]
        pv_low = sb("pv_low", [S, D], f32, xscope)
        av = sb("av", [S, D], f32, xscope)
        mx4 = sb("mx4", [S, NC], f32, xscope)
        mx = sb("mx", [S, 2], f32, xscope)
        nbias = [sb(f"nbias{i}", [S, 1], f32, xscope) for i in range(2)]
        rsum = [sb(f"rsum{i}", [S, 1], f32, xscope) for i in range(2)]
        rinv = sb("rinv", [S, 1], f32, xscope)
        raw_scope = ExitStack()
        raw = [sb(f"raw{i}", [P, NKT, D], f32, raw_scope) for i in range(2)]
        loop_scope = ExitStack()
        nat_hi = sb("nat_hi", [P, NKT, D], f32r, loop_scope)
        nat_lo = sb("nat_lo", [P, NKT, D], f32r, loop_scope)
        ct_hi = [sb(f"ct_hi{i}", [P, KD, 512], f32r, loop_scope) for i in range(2)]
        ct_lo = [sb(f"ct_lo{i}", [P, KD, 512], f32r, loop_scope) for i in range(2)]
        pT = sb("pT", [P, NKT, P], f32r, loop_scope)
        loop_scope.close()
        pro_scope = ExitStack()
        Wn = sb("Wn", [P, KD, D], f32, pro_scope)
        pn = sb("pn", [P, NT, D], f32, pro_scope)
        pnT = sb("pnT", [P, KD, B * S], f32, pro_scope)
        pnT_hi = sb("pnT_hi", [P, KD, B * S], f32r, pro_scope)
        pnT_lo = sb("pnT_lo", [P, KD, B * S], f32r, pro_scope)
        W_hi = sb("W_hi", [P, KD, D], f32r, pro_scope)
        W_lo = sb("W_lo", [P, KD, D], f32r, pro_scope)
        pro_scope.close()
        raw_scope.close()
        epi_scope = ExitStack()
        We = sb("We", [P, KD, D], f32, epi_scope)
        b_bc = sb("b_bc", [P, D], f32, epi_scope)
        WT_hi = sb("WT_hi", [P, KD, D], f32r, epi_scope)
        WT_lo = sb("WT_lo", [P, KD, D], f32r, epi_scope)
        avT_hi = sb("avT_hi", [P, KD, B * S], f32r, epi_scope)
        avT_lo = sb("avT_lo", [P, KD, B * S], f32r, epi_scope)
        xo = sb("xo", [P, NT, D], f32, epi_scope)
        epi_scope.close()
        xscope.close()

        xn = sb("xn", [P, NT, D])
        heads = xn[:, :, :].rearrange("p (r a) d -> p r (a d)", r=2)
        w_raw = [sb(f"w_raw{i}", [P, KD, 512]) for i in range(RING)]
        w_hi = [sb(f"w_hi{i}", [P, KD, 512], f32r) for i in range(RING)]
        w_lo = [sb(f"w_lo{i}", [P, KD, 512], f32r) for i in range(RING)]
        zeros = sb("zeros", [P, D])
        ones = sb("ones", [P, P])
        before = sb("before", [P, P])
        e_int = sb("e_int", [P, E], mybir.dt.int32)
        e_idx = sb("e_idx", [P, E])
        upto = sb("upto", [P, E, E])
        w_router = sb("w_router", [P, KD, E])
        layer = ExitStack()
        x1n = sb("x1n", [P, NT, D], f32, layer)
        xT_hi = sb("xT_hi", [P, KD, B * S], f32r, layer)
        xT_lo = sb("xT_lo", [P, KD, B * S], f32r, layer)
        gain = sb("gain", [P, D], f32, layer)
        shift = sb("shift", [P, D], f32, layer)
        b2_bc = sb("b2_bc", [P, D], f32, layer)
        b1_col = sb("b1_col", [P, FF // P], f32, layer)
        late = ExitStack()
        proj2 = sb("proj2", [P, P], f32, late)
        proj2_hi = sb("proj2_hi", [P, P], f32r, late)
        proj2_lo = sb("proj2_lo", [P, P], f32r, late)
        mask = sb("mask", [P, P], f32, late)
        z_hi = [sb(f"z_hi{i}", [P, B * S], f32r, late) for i in range(2)]
        z_lo = [sb(f"z_lo{i}", [P, B * S], f32r, late) for i in range(2)]
        neg = [sb(f"neg{i}", [P, B * S], f32, late) for i in range(2)]
        phi = [sb(f"phi_{n}", [P, H // 2, B * S], f32, late) for n in "qk"]
        v1 = sb("v1", [P, NT, H, DH + 1], f32, late)
        at = [sb(f"at{i}", [P, 4, P], f32, late) for i in range(2)]
        oT_hi = sb("oT_hi", [P, HD // P, P], f32r, late)
        oT_lo = sb("oT_lo", [P, HD // P, P], f32r, late)
        den = sb("den", [P, 2, 4], f32, late)
        late.close()
        ffn = ExitStack()
        gl = [sb(f"gl{i}", [P, B * S], f32, ffn) for i in range(2)]
        gl_hi = [sb(f"gl_hi{i}", [P, B * S], f32r, ffn) for i in range(2)]
        gl_lo = [sb(f"gl_lo{i}", [P, B * S], f32r, ffn) for i in range(2)]
        ffn.close()
        layer.close()

        moe = ExitStack()
        xT32 = sb("xT32", [P, KD, B * S], f32, moe)
        logits = sb("logits", [P, NT, E], f32, moe)
        pref = sb("pref", [P, E], f32, moe)
        pick = [sb(f"pick{k}", [P, NT, E], f32, moe) for k in range(2)]
        scr = sb("scr", [P, NT, E], f32, moe)
        scr8 = sb("scr8", [P, E, E], f32, moe)
        best = [sb(f"best{k}", [P, NT], f32, moe) for k in range(2)]
        top = sb("top", [P, NT], f32, moe)
        chosen = sb("chosen", [P, NT, E], f32, moe)
        rank = sb("rank", [P, NT, E], f32, moe)
        count = sb("count", [P, E], f32, moe)
        extra = sb("extra", [P, E], f32, moe)
        upto_extra = sb("upto_extra", [P, E], f32, moe)
        first_block = sb("first_block", [P, E], f32, moe)
        slotf = [sb(f"slotf{k}", [P, NT], f32, moe) for k in range(2)]
        slot_of = [sb(f"slot_of{k}", [P, NT], mybir.dt.uint32, moe) for k in range(2)]
        blocks = sb("blocks", [P, 2, E], mybir.dt.int32, moe)
        gate = [sb(f"gate{k}", [P, NT], f32, moe) for k in range(2)]
        gap = sb("gap", [P, NT], f32, moe)
        gsum = sb("gsum", [P, NT], f32, moe)
        xg = sb("xg", [P, D], f32, moe)
        xgT_hi = sb("xgT_hi", [P, KD, P], f32r, moe)
        xgT_lo = sb("xgT_lo", [P, KD, P], f32r, moe)
        sg = [sb(f"sg{i}", [P, 512], f32, moe) for i in range(2)]
        hm = [sb(f"hm{i}", [P, 512], f32, moe) for i in range(2)]
        hmT_hi = [sb(f"hmT_hi{i}", [P, 4, P], f32r, moe) for i in range(2)]
        hmT_lo = [sb(f"hmT_lo{i}", [P, 4, P], f32r, moe) for i in range(2)]
        yb = sb("yb", [P, D], f32, moe)
        units = ExitStack()
        e_raw = w_raw + [sb(f"e_raw{j}", [P, KD, 512], f32, units) for j in range(RING, 6)]
        e_hi = w_hi + [sb(f"e_hi{j}", [P, KD, 512], f32r, units) for j in range(RING, 6)]
        e_lo = w_lo + [sb(f"e_lo{j}", [P, KD, 512], f32r, units) for j in range(RING, 6)]
        units.close()
        yt = [sb(f"yt{k}", [P, NT, D], f32, moe) for k in range(2)]
        moe.close()
        xs = nc.dram_tensor("slots_x", [(NB + 1) * P, D], f32).ap()
        ys = nc.dram_tensor("slots_y", [NB * P, D], f32).ap()

        x_loaded, W_loaded, b_loaded = sem("x_loaded"), sem("W_loaded"), sem("b_loaded")
        ctx_loaded = [[sem(f"ctx_loaded{p}_{c}") for c in range(NC)] for p in range(2)]
        raw_zeroed, sc_zeroed = sem("raw_zeroed"), sem("sc_zeroed")
        const_ready = sem("const_ready")
        dve_step, pool_step = sem("dve_step"), sem("pool_step")
        var_ready, rstd_ready, pn_ready = sem("var_ready"), sem("rstd_ready"), sem("pn_ready")
        pnT_done, pnT_hi_ready, pnT_ready, pnT_lo_ready = sem("pnT_done"), sem("pnT_hi_ready"), sem("pnT_ready"), sem("pnT_lo_ready")
        W_hi_ready, W_lo_ready = sem("W_hi_ready"), sem("W_lo_ready")
        pwT_done, pw_hi_ready, pw_lo_ready, pw_ready = sem("pwT_done"), sem("pw_hi_ready"), sem("pw_lo_ready"), sem("pw_ready")
        pb_done, pb_ready = sem("pb_done"), sem("pb_ready")
        t_done, t_hi, t_lo = sem("t_done"), sem("t_hi"), sem("t_lo")
        qk_done, s_low, s_ready = sem("qk_done"), sem("s_low"), sem("s_ready")
        max_ready, exp_done, rinv_ready = sem("max_ready"), sem("exp_done"), sem("rinv_ready")
        pt_done, pt_hi, pt_lo = sem("pt_done"), sem("pt_hi"), sem("pt_lo")
        nat_hi_ready = sem("nat_hi_ready")
        nat_lo_ready = [sem(f"nat_lo_ready{c}") for c in range(NC)]
        pv_done, pv_low_ready, av_sum, av_ready = sem("pv_done"), sem("pv_low_ready"), sem("av_sum"), sem("av_ready")
        avt_done, avt_ready = sem("avt_done"), sem("avt_ready")
        WT_done, WT_hi_ready, WT_lo_ready = sem("WT_done"), sem("WT_hi_ready"), sem("WT_lo_ready")
        avT_hi_ready, avT_lo_ready, xo_done, x1_ready = sem("avT_hi_ready"), sem("avT_lo_ready"), sem("xo_done"), sem("x1_ready")
        stored = sem("stored")
        zeros_ready, slots_zeroed, router_loaded, index_ready, order_ready = sem("zeros_ready"), sem("slots_zeroed"), sem("router_loaded"), sem("index_ready"), sem("order_ready")
        xT32_ready, logits_done, chosen_ready, rank_done = sem("xT32_ready"), sem("logits_done"), sem("chosen_ready"), sem("rank_done")
        gap_ready, gap_exp, slots_ready, scattered = sem("gap_ready"), sem("gap_exp"), sem("slots_ready"), sem("scattered")
        xo_ready = sem("xo_ready")
        xg_loaded, xgT_done, xgT_hi_ready, xgT_lo_ready = sem("xg_loaded"), sem("xgT_done"), sem("xgT_hi_ready"), sem("xgT_lo_ready")
        unit_done = [sem(f"unit_done{j}") for j in range(6)]
        last_y_stored = sem("last_y_stored")
        silu_ready, hm_ready, hmT_done = sem("silu_ready"), sem("hm_ready"), sem("hmT_done")
        hmT_hi_ready, hmT_lo_ready, y_ready, y_stored = sem("hmT_hi_ready"), sem("hmT_lo_ready"), sem("y_ready"), sem("y_stored")
        gathered = [sem(f"gathered{t}") for t in range(NT)]
        w_loaded = [sem(f"w_loaded{i}") for i in range(RING)]
        w_hi_ready = [sem(f"w_hi_ready{i}") for i in range(RING)]
        w_lo_ready = [sem(f"w_lo_ready{i}") for i in range(RING)]
        e_loaded = w_loaded + [sem(f"e_loaded{j}") for j in range(RING, 6)]
        e_hi_ready = w_hi_ready + [sem(f"e_hi_ready{j}") for j in range(RING, 6)]
        e_lo_ready = w_lo_ready + [sem(f"e_lo_ready{j}") for j in range(RING, 6)]
        b1_loaded = sem("b1_loaded")
        vec_loaded, vec2_loaded = sem("vec_loaded"), sem("vec2_loaded")
        proj_loaded, proj_zero, proj_hi_ready, proj_lo_ready, mask_ready = sem("proj_loaded"), sem("proj_zero"), sem("proj_hi_ready"), sem("proj_lo_ready"), sem("mask_ready")
        xn_ready, xT_done, xT_hi_ready, xT_lo_ready = sem("xn_ready"), sem("xT_done"), sem("xT_hi_ready"), sem("xT_lo_ready")
        z_done, z_hi_ready, z_lo_ready = sem("z_done"), sem("z_hi_ready"), sem("z_lo_ready")
        f_done, neg_ready, e_ready, phi_ready = sem("f_done"), sem("neg_ready"), sem("e_ready"), sem("phi_ready")
        v_done, v_ready, v_one = sem("v_done"), sem("v_ready"), sem("v_one")
        a_done, a_ready, o_done, o_ready = sem("a_done"), sem("a_ready"), sem("o_done"), sem("o_ready")
        oT_done, oT_hi_ready, oT_lo_ready = sem("oT_done"), sem("oT_hi_ready"), sem("oT_lo_ready")
        ao_done, xa_ready = sem("ao_done"), sem("xa_ready")
        up_done, gelu_ready, gl_hi_ready, gl_lo_ready, dn_done, x2_ready = sem("up_done"), sem("gelu_ready"), sem("gl_hi_ready"), sem("gl_lo_ready"), sem("dn_done"), sem("x2_ready")

        def unit(name, half, rows=False):
            w = ins[name].rearrange("(k p) n -> p k n", p=P)
            return w[:, KD * half:KD * (half + 1), :] if rows else w[:, :, 512 * half:512 * (half + 1)]

        UNITS = [unit(f"L0_attn_{n}", half) for n in ("wq", "wk", "wv") for half in range(2)]
        UNITS += [unit("L0_attn_wo", half, rows=True) for half in range(2)]
        for i in range(FF // 512):
            UNITS += [unit("L0_attn_w1", i), unit("L0_attn_w2", i, rows=True)]
        NU = len(UNITS)
        USED = [(z_done, 4 * (u + 1)) for u in range(4)] + [(v_done, NT), (v_done, 2 * NT), (ao_done, NT), (ao_done, NT)]
        for i in range(FF // 512):
            USED += [(up_done, 4 * (i + 1)), (dn_done, 4 * (i + 1))]

        def upper(u):
            return w_hi_ready[u % RING], u // RING + 1

        def lower(u):
            return w_lo_ready[u % RING], u // RING + 1

        EU = 6
        POOL_UNITS = (4, 5)

        def expert_unit(e, j):
            w = ins["L0_ffn_" + ("w0", "w1", "w0", "w1", "wo", "wo")[j]]
            w = w[bass.ds(e, 1), :, :].rearrange("o (k p) n -> p (o k) n", p=P)
            return w[:, KD * (j - 4):KD * (j - 3), :] if j >= 4 else w[:, :, 512 * (j // 2):512 * (j // 2 + 1)]

        def turn_of(e, j):
            before = len(range(j, NU, RING)) if j < RING else 0
            return before + e + 1

        def expert_blocks(engine, e):
            most = NB - 1 if isinstance(e, int) else NB - 2
            return [engine.value_load(blocks[0:1, i, bass.ds(e, 1)], min_val=0, max_val=most) for i in range(2)]

        TB = [bank[0], bank[1], bank[2]]
        SB = [bank[3], bank[4]]
        PB = [bank[5], bank[6]]
        VB = bank[7]
        G = FULL + 1
        POOL_CHUNKS = (0, 2, 3)
        PT_SPLIT = [(0, 8), (8, NKT)]

        def groups(c):
            if c < NC - 1:
                return [(CH * c + k, [k]) for k in range(KD)]
            return [(G - 1, list(range(KD)))]

        def width(c):
            return CH * P if c < NC - 1 else REM

        def t_bank(g):
            return TB[g % len(TB)]

        def t_before(b, g):
            if g >= len(TB):
                return G * b + g - len(TB) + 1
            if isinstance(b, int) and b == 0:
                return None
            last = max(h for h in range(G) if h % len(TB) == g)
            return G * (b - 1) + last + 1

        block = ctx.enter_context(nc.Block())

        @block.sync
        def _(sp):
            sp.dma_start(xt[:, :, :], x_v).then_inc(x_loaded, 16)
            sp.dma_start(Wn[:, :, :], ins["L0_xattn_W"].rearrange("(k p) h -> p k h", p=P)).then_inc(W_loaded, 16)
            with nc.allow_non_contiguous_dma(reason="512 bias values, once"):
                sp.dma_start(b_col[:, :], ins["L0_xattn_b"].rearrange("(k p) -> p k", p=P)).then_inc(b_loaded, 16)

            def load_ctx(b, c):
                src = ins["ctx_1024"][b]
                if c < NC - 1:
                    src = src[0:FULL * P, :].rearrange("(p j) d -> p j d", j=FULL)[:, CH * c:CH * (c + 1), :]
                    dst = raw[b % 2][:, CH * c:CH * (c + 1), :]
                else:
                    src, dst = src[FULL * P:KEYS, :], raw[b % 2][0:REM, FULL, :]
                sp.dma_start(dst, src).then_inc(ctx_loaded[b % 2][c], 16)

            sp.wait_ge(raw_zeroed, 2)
            for b in range(B):
                for c in range(NC):
                    if b >= 2:
                        sp.wait_ge(t_done, G * (b - 2) + groups(c)[-1][0] + 1)
                        sp.wait_ge(nat_lo_ready[c], b - 1)
                    load_ctx(b, c)
            sp.wait_ge(t_done, G * (B - 1))
            for c in range(NC):
                sp.wait_ge(nat_lo_ready[c], B - 1)
            sp.dma_start(We[:, :, :], ins["L0_xattn_W"].rearrange("(k p) h -> p k h", p=P)).then_inc(W_loaded, 16)
            sp.dma_start(b_bc[:, :], ins["L0_xattn_b"].partition_broadcast(P)).then_inc(b_loaded, 16)
            sp.wait_ge(x1_ready, NT)
            for name, dst in (("g1", gain), ("beta1", shift), ("b2", b2_bc)):
                sp.dma_start(dst[:, :], ins[f"L0_attn_{name}"].partition_broadcast(P)).then_inc(vec_loaded, 16)
            for u in range(NU):
                if u == 8:
                    sp.wait_ge(xT_lo_ready, KD)
                    for name, dst in (("g2", gain), ("beta2", shift)):
                        sp.dma_start(dst[:, :], ins[f"L0_attn_{name}"].partition_broadcast(P)).then_inc(vec2_loaded, 16)
                if u >= RING:
                    sp.wait_ge(*lower(u - RING))
                sp.dma_start(w_raw[u % RING][:, :, :], UNITS[u]).then_inc(w_loaded[u % RING], 16)
                if u == 0:
                    with nc.allow_non_contiguous_dma(reason="bias values by partition, once"):
                        sp.dma_start(b1_col[:, :], ins["L0_attn_b1"].rearrange("(f p) -> p f", p=P)).then_inc(b1_loaded, 16)
                    sp.wait_ge(proj_zero, 1)
                    for s in range(2):
                        sp.dma_start(proj2[DH * s:DH * (s + 1), DH * s:DH * (s + 1)], ins["L0_attn_proj"]).then_inc(proj_loaded, 16)
            sp.dma_start(w_router[:, :, :], ins["L0_ffn_w_router"].rearrange("(k p) e -> p k e", p=P)).then_inc(router_loaded, 16)
            sp.wait_ge(zeros_ready, 1)
            sp.dma_start(xs.rearrange("(n p) d -> p n d", p=P), zeros[:, :].unsqueeze(1).to_broadcast([P, NB + 1, D])).then_inc(slots_zeroed, 16)
            sp.dma_start(ys[E * P:NB * P, :].rearrange("(n p) d -> p n d", p=P), zeros[:, :].unsqueeze(1).to_broadcast([P, OV, D])).then_inc(slots_zeroed, 16)

            def load_expert(e):
                for j in range(EU):
                    if not (isinstance(e, int) and j >= RING):
                        sp.wait_ge(e_lo_ready[j], turn_of(e, j) - 1)
                    sp.dma_start(e_raw[j][:, :, :], expert_unit(e, j)).then_inc(e_loaded[j], 16)
                    if isinstance(e, int) and j == RING - 1:
                        sp.wait_ge(x2_ready, NT)

            load_expert(0)
            with sp.Fori(1, E) as e:
                load_expert(e)
            sp.wait_ge(xo_ready, NT)
            sp.dma_start(out_v, xt[:, :, :]).then_inc(stored, 16)
            sp.wait_ge(stored, 16)

        @block.gpsimd
        def _(pool):
            steps = [0]

            def link(ins_):
                steps[0] += 1
                ins_.then_inc(pool_step, 1)
                pool.wait_ge(pool_step, steps[0])

            link(nc.gpsimd.memset(ident[:, :], 0.0))
            nc.gpsimd.affine_select(out=ident[:, :], in_=ident[:, :], compare_op=ALU.not_equal, fill=1.0, base=0,
                                    pattern=[[-1, P]], channel_multiplier=1).then_inc(const_ready, 1)
            link(nc.gpsimd.memset(mhalf[:, :], -0.5))
            pool.wait_ge(var_ready, 1)
            nc.gpsimd.tensor_tensor(rstd[:, :], rstd[:, :], mhalf[:, :], ALU.pow).then_inc(rstd_ready, 1)

            def take_pw(b, par):
                if not (isinstance(b, int) and b < 2):
                    pool.wait_ge(qk_done, NC * (b - 1))
                nc.gpsimd.tensor_copy(pw[par][:, :, :], pw_all[:, :, bass.ds(b, 1), :].rearrange("p k o m -> p k (o m)").bitcast(f32))\
                    .then_inc(pw_ready, 1)

            def split_ctx(b, par):
                for c in POOL_CHUNKS:
                    first, last = CH * c, min(CH * (c + 1), NKT)
                    pool.wait_ge(nat_hi_ready, NC * b + c + 1)
                    nc.gpsimd.tensor_tensor(nat_lo[:, first:last, :], raw[par][:, first:last, :],
                                            nat_hi[:, first:last, :].bitcast(f32), ALU.subtract).then_inc(nat_lo_ready[c], 1)

            pool.wait_ge(pw_hi_ready, KD)
            pool.wait_ge(pw_lo_ready, KD)
            take_pw(0, 0)
            take_pw(1, 1)
            split_ctx(0, 0)
            with pool.Fori(0, B // 2 - 1) as i:
                take_pw(2 * i + 2, 0)
                split_ctx(2 * i + 1, 1)
                take_pw(2 * i + 3, 1)
                split_ctx(2 * i + 2, 0)
            split_ctx(B - 1, 1)

            def root(n):
                pool.wait_ge(var_ready, n)
                nc.gpsimd.tensor_tensor(rstd[:, :], rstd[:, :], mhalf[:, :], ALU.pow).then_inc(rstd_ready, 1)

            pool.wait_ge(x1_ready, NT)
            link(nc.gpsimd.memset(mask[:, :], 1.0))
            link(nc.gpsimd.affine_select(out=mask[:, :], in_=mask[:, :], compare_op=ALU.is_ge, fill=0.0, base=0,
                                         pattern=[[1, P]], channel_multiplier=-1))
            nc.gpsimd.affine_select(out=mask[:, S:P], in_=mask[:, S:P], compare_op=ALU.is_ge, fill=0.0, base=-S,
                                    pattern=[[0, P - S]], channel_multiplier=1).then_inc(mask_ready, 1)
            root(2)
            root(3)
            nc.gpsimd.iota(e_int[:, :], pattern=[[1, E]], base=0, channel_multiplier=0).then_inc(index_ready, 1)
            link(nc.gpsimd.memset(ones[:, :], 1.0))
            nc.gpsimd.affine_select(out=before[:, :], in_=ones[:, :], compare_op=ALU.is_gt, fill=0.0, base=0,
                                    pattern=[[1, P]], channel_multiplier=-1).then_inc(order_ready, 1)
            nc.gpsimd.affine_select(out=upto[:, :, :], in_=ones[:, 0:E * E].rearrange("p (e f) -> p e f", e=E), compare_op=ALU.is_ge,
                                    fill=0.0, base=0, pattern=[[1, E], [-1, E]], channel_multiplier=0).then_inc(order_ready, 1)
            root(4)
            root(5)
            def split_w(e, j):
                pool.wait_ge(e_hi_ready[j], turn_of(e, j))
                nc.gpsimd.tensor_tensor(e_lo[j][:, :, :], e_raw[j][:, :, :], e_hi[j][:, :, :].bitcast(f32),
                                        ALU.subtract).then_inc(e_lo_ready[j], 1)

            for j in POOL_UNITS:
                split_w(0, j)
            pool.wait_ge(slots_ready, 2)
            pool.wait_ge(slots_zeroed, 32)
            for k in range(2):
                for t in range(NT):
                    nc.gpsimd.indirect_dma_start(xs[:, :], bass.IndirectOffsetOnAxis(ap=slot_of[k][:, t:t + 1], axis=0),
                                                 xn[:, t, :], None).then_inc(scattered, 16)
            with pool.Fori(1, E) as e:
                for j in POOL_UNITS:
                    split_w(e, j)
            pool.wait_ge(last_y_stored, 16)
            for t in range(NT):
                for k in range(2):
                    nc.gpsimd.indirect_dma_start(yt[k][:, t, :], None, ys[:, :],
                                                 bass.IndirectOffsetOnAxis(ap=slot_of[k][:, t:t + 1], axis=0)).then_inc(gathered[t], 16)

        @block.scalar
        def _(act):
            act.wait_ge(W_loaded, 16)
            nc.scalar.activation(W_hi[:, :, :], Wn[:, :, :], ACT.Copy).then_inc(W_hi_ready, 1)
            for k in range(KD):
                act.wait_ge(pnT_done, k + 1)
                nc.scalar.activation(pnT_hi[:, k, :], bank[k][:, :], ACT.Copy).then_inc(pnT_hi_ready, 1)
                nc.scalar.activation(pnT[:, k, :], bank[k][:, :], ACT.Copy).then_inc(pnT_ready, 1)
            for m in range(KD):
                act.wait_ge(pwT_done, m + 1)
                nc.scalar.activation(pw_all[:, m, :, 0:S], bank[m][:, :].rearrange("p (b s) -> p b s", b=B),
                                     ACT.Copy).then_inc(pw_hi_ready, 1)
            act.wait_ge(pb_done, 1)
            nc.scalar.activation(pb[:, :], bank[4][0:S, 0:B], ACT.Copy).then_inc(pb_ready, 1)

            def evacuate(b, c):
                if c >= 2:
                    act.wait_ge(qk_done, NC * b + c - 1)
                elif not (isinstance(b, int) and b == 0):
                    act.wait_ge(qk_done, NC * (b - 1) + NC - 2 + c + 1)
                for g, ks in groups(c):
                    act.wait_ge(t_done, G * b + g + 1)
                    n = width(c) if len(ks) == 1 else REMP
                    nc.scalar.activation(ct_hi[c % 2][:, ks[0]:ks[-1] + 1, 0:n],
                                         t_bank(g)[:, 0:len(ks) * 512 // len(ks)].rearrange("p (k n) -> p k n", k=len(ks))[:, :, 0:n],
                                         ACT.Copy).then_inc(t_hi, 1)

            def low_scores(b, c):
                act.wait_ge(qk_done, NC * b + c + 1)
                if not (isinstance(b, int) and b == 0 and c < 2):
                    act.wait_ge(s_ready, NC * b + c - 1)
                nc.scalar.activation(sc_low[c % 2][:, 0:width(c)], SB[c % 2][S:2 * S, 0:width(c)], ACT.Copy).then_inc(s_low, 1)

            def take_av(b):
                act.wait_ge(avt_done, b + 1)
                nc.scalar.activation(avT[:, :, bass.ds(S * b, S)], VB[:, 0:KD * S].rearrange("p (k s) -> p k s", k=KD),
                                     ACT.Copy).then_inc(avt_ready, 1)

            def prob_parts(b):
                for h, (t0, t1) in enumerate(PT_SPLIT):
                    act.wait_ge(pt_done, 2 * b + h + 1)
                    if not (isinstance(b, int) and b == 0):
                        act.wait_ge(pv_done, NC * b)
                    nc.scalar.activation(pT[:, t0:t1, 0:S], PB[h][:, 0:(t1 - t0) * S].rearrange("p (j s) -> p j s", s=S),
                                         ACT.Copy).then_inc(pt_hi, 1)

            def exps(b, par):
                act.wait_ge(max_ready, b + 1)
                if not (isinstance(b, int) and b < 2):
                    act.wait_ge(rinv_ready, b - 1)
                nc.scalar.activation(sc[par][0:S, 0:KEYS], sc[par][0:S, 0:KEYS], ACT.Exp, bias=nbias[par][:, :],
                                     accum_out=rsum[par][:, :]).then_inc(exp_done, 1)

            def split_ctx(b, par, c):
                first, last = CH * c, min(CH * (c + 1), NKT)
                act.wait_ge(ctx_loaded[par][c], 16 * (b // 2 + 1) if isinstance(b, int) else 16 * ((b - par) // 2 + 1))
                if not (isinstance(b, int) and b == 0):
                    act.wait_ge(pv_done, NC * (b - 1) + c + 1)
                nc.scalar.activation(nat_hi[:, first:last, :], raw[par][:, first:last, :], ACT.Copy).then_inc(nat_hi_ready, 1)

            def stage(b, par, scores=True, values=True, earlier=True):
                if values:
                    split_ctx(b, par, 0)
                if scores:
                    evacuate(b + 1, 0)
                if earlier:
                    take_av(b - 1)
                if values:
                    split_ctx(b, par, 1)
                if scores:
                    evacuate(b + 1, 1)
                if values:
                    prob_parts(b)
                    split_ctx(b, par, 2)
                if scores:
                    low_scores(b + 1, 0)
                    evacuate(b + 1, 2)
                if values:
                    split_ctx(b, par, 3)
                if scores:
                    low_scores(b + 1, 1)
                    evacuate(b + 1, 3)
                    low_scores(b + 1, 2)
                if values:
                    act.wait_ge(pv_done, NC * (b + 1))
                    nc.scalar.activation(pv_low[:, :], VB[S:2 * S, :], ACT.Copy).then_inc(pv_low_ready, 1)
                if scores:
                    low_scores(b + 1, 3)
                if values:
                    act.wait_ge(rinv_ready, b + 1)
                    act.wait_ge(av_sum, b + 1)
                    nc.scalar.activation(av[0:S, :], pv_low[:, :], ACT.Copy, scale=rinv[:, :]).then_inc(av_ready, 1)
                if scores:
                    exps(b + 1, 1 - par)

            stage(-1, 1, values=False, earlier=False)
            stage(0, 0, earlier=False)
            with act.Fori(0, B // 2 - 1) as i:
                stage(2 * i + 1, 1)
                stage(2 * i + 2, 0)
            stage(B - 1, 1, scores=False)
            for k in range(KD):
                act.wait_ge(WT_done, k + 1)
                nc.scalar.activation(WT_hi[:, k, :], bank[k][:, :], ACT.Copy).then_inc(WT_hi_ready, 1)
            take_av(B - 1)
            act.wait_ge(avt_ready, B)
            nc.scalar.activation(avT_hi[:, :, :], avT[:, :, :], ACT.Copy).then_inc(avT_hi_ready, 1)

            def split_w(u):
                act.wait_ge(w_loaded[u % RING], 16 * (u // RING + 1))
                if u >= RING:
                    act.wait_ge(*USED[u - RING])
                nc.scalar.activation(w_hi[u % RING][:, :, :], w_raw[u % RING][:, :, :], ACT.Copy).then_inc(w_hi_ready[u % RING], 1)

            def upper_xT(n):
                for k in range(KD):
                    act.wait_ge(xT_done, KD * n + k + 1)
                    nc.scalar.activation(xT_hi[:, k, :], bank[k][:, :], ACT.Copy).then_inc(xT_hi_ready, 1)

            act.wait_ge(proj_loaded, 32)
            nc.scalar.activation(proj2_hi[:, :], proj2[:, :], ACT.Copy).then_inc(proj_hi_ready, 1)
            split_w(0)
            upper_xT(0)
            split_w(1)
            split_w(2)

            def upper_z(n):
                act.wait_ge(z_done, n + 1)
                if n >= 2:
                    act.wait_ge(f_done, n - 1)
                nc.scalar.activation(z_hi[n % 2][:, :], bank[n % 2][:, :], ACT.Copy).then_inc(z_hi_ready, 1)

            def exp_neg(n):
                act.wait_ge(neg_ready, n + 1)
                nc.scalar.activation(neg[n % 2][:, :], neg[n % 2][:, :], ACT.Exp).then_inc(e_ready, 1)

            for n in range(H):
                upper_z(n)
                if n >= 1:
                    exp_neg(n - 1)
                if n % 4 == 0 and n // 4 + 2 >= RING:
                    split_w(n // 4 + 2)
            exp_neg(H - 1)
            for u in range(2):
                for t in range(NT):
                    n = NT * u + t
                    act.wait_ge(v_done, n + 1)
                    nc.scalar.activation(v1[:, t, 8 * u:8 * (u + 1), 0:DH], bank[4 + n % 2][:, :].rearrange("p (h d) -> p h d", d=DH),
                                         ACT.Copy).then_inc(v_ready, 1)
                split_w(6 + u)
            for t in range(NT):
                for half in range(2):
                    act.wait_ge(oT_done, 2 * t + half + 1)
                    if t >= 1:
                        act.wait_ge(ao_done, t)
                    nc.scalar.activation(oT_hi[:, 4 * half:4 * (half + 1), :], bank[4 + half][:, :].rearrange("p (k n) -> p k n", n=P),
                                         ACT.Copy).then_inc(oT_hi_ready, 1)
                if t == 0:
                    split_w(8)
            split_w(9)
            upper_xT(1)
            split_w(10)
            act.wait_ge(b1_loaded, 16)
            for n in range(FF // P):
                act.wait_ge(up_done, n + 1)
                if n >= 2:
                    act.wait_ge(gl_lo_ready, n - 1)
                nc.scalar.activation(gl[n % 2][:, :], bank[n % 2][:, :], ACT.Gelu, bias=b1_col[:, n:n + 1]).then_inc(gelu_ready, 1)
                if n % 4 == 3 and n < FF // P - 1:
                    split_w(11 + 2 * (n // 4))
                if n % 4 == 0 and 4 <= n < FF // P - 4:
                    split_w(10 + n // 2)

            def split_e(e, j, wait):
                act.wait_ge(e_loaded[j], 16 * turn_of(e, j))
                act.wait_ge(*wait)
                nc.scalar.activation(e_hi[j][:, :, :], e_raw[j][:, :, :], ACT.Copy).then_inc(e_hi_ready[j], 1)

            for j in range(RING):
                split_e(0, j, USED[max(u for u in range(NU) if u % RING == j)])
            for k in range(KD):
                act.wait_ge(xT_done, 2 * KD + k + 1)
                nc.scalar.activation(xT32[:, k, :], bank[k][:, :], ACT.Copy).then_inc(xT32_ready, 1)
            for j in range(RING, EU):
                split_e(0, j, (x2_ready, NT))
            act.wait_ge(gap_ready, 1)
            nc.scalar.activation(gsum[:, :], gap[:, :], ACT.Exp).then_inc(gap_exp, 1)

            def load_rows(b):
                nc.scalar.dma_start(xg[:, :], xs[bass.ds(b * P, P), :]).then_inc(xg_loaded, 16)

            def upper_rows(b):
                act.wait_ge(xgT_done, b + 1)
                nc.scalar.activation(xgT_hi[:, :, :], bank[7][:, :].rearrange("p (k n) -> p k n", n=P), ACT.Copy).then_inc(xgT_hi_ready, 1)

            def silu(b, half):
                act.wait_ge(unit_done[2 * half], b + 1)
                nc.scalar.activation(sg[half][:, :], bank[2 * half][:, :], ACT.Silu).then_inc(silu_ready, 1)

            def upper_hidden(b, half):
                act.wait_ge(hmT_done, 2 * b + half + 1)
                nc.scalar.activation(hmT_hi[half][:, :, :], bank[4 + half][:, :].rearrange("p (k n) -> p k n", n=P),
                                     ACT.Copy).then_inc(hmT_hi_ready, 1)

            def expert_block(b, e, again=False, last=False):
                def split(j):
                    if not again and not last:
                        split_e(e + 1, j, (unit_done[j], b + 1))

                silu(b, 0)
                split(0)
                silu(b, 1)
                upper_hidden(b, 0)
                split(1)
                if not last:
                    upper_rows(b + 1)
                    load_rows(b + 2)
                split(2)
                upper_hidden(b, 1)
                split(3)
                split(4)
                act.wait_ge(unit_done[5], b + 1)
                act.wait_ge(y_stored, 16 * b + 1)
                nc.scalar.activation(yb[:, :], bank[6][:, :], ACT.Copy).then_inc(y_ready, 1)
                split(5)
                act.wait_ge(y_ready, b + 2)
                nc.scalar.dma_start(ys[bass.ds(b * P, P), :], yb[:, :]).then_inc(last_y_stored if last else y_stored, 16)

            act.wait_ge(slots_ready, 4)
            act.wait_ge(scattered, 16 * 2 * NT)
            load_rows(0)
            upper_rows(0)
            load_rows(1)
            with act.Fori(0, E - 1) as e:
                first_b, last_b = expert_blocks(act, e)
                with act.If(first_b < last_b):
                    with act.Fori(first_b, last_b) as b:
                        expert_block(b, e, again=True)
                expert_block(last_b, e)
            first_b, last_b = expert_blocks(act, E - 1)
            with act.If(first_b < last_b):
                with act.Fori(first_b, last_b) as b:
                    expert_block(b, E - 1, again=True)
            expert_block(last_b, E - 1, last=True)

        @block.vector
        def _(dve):
            steps = [0]

            def link(ins_):
                steps[0] += 1
                ins_.then_inc(dve_step, 1)
                dve.wait_ge(dve_step, steps[0])

            for par in range(2):
                nc.vector.memset(raw[par][64:P, FULL, :], 0.0).then_inc(raw_zeroed, 1)
                nc.vector.memset(sc[par][0:S, KEYS:NKT * P], 0.0).then_inc(sc_zeroed, 1)
            dve.wait_ge(x_loaded, 16)
            for t in range(NT):
                last = nc.vector.bn_stats(stats[:, t, :], xt[:, t, :])
            link(last)
            for t in range(NT):
                last = nc.vector.bn_aggr(mv[:, t, :], stats[:, t, :])
            link(last)
            nc.vector.tensor_scalar(rstd[:, :], mv[:, :, 1], EPS, None, ALU.add).then_inc(var_ready, 1)
            dve.wait_ge(rstd_ready, 1)
            for t in range(NT):
                nc.vector.tensor_scalar(pn[:, t, :], xt[:, t, :], mv[:, t, 0:1], rstd[:, t:t + 1],
                                        ALU.subtract, ALU.mult).then_inc(pn_ready, 1)
            dve.wait_ge(W_hi_ready, 1)
            nc.vector.tensor_tensor(W_lo[:, :, :], Wn[:, :, :], W_hi[:, :, :].bitcast(f32), ALU.subtract).then_inc(W_lo_ready, 1)
            for k in range(KD):
                dve.wait_ge(pnT_ready, k + 1)
                nc.vector.tensor_tensor(pnT_lo[:, k, :], bank[k][:, :], pnT_hi[:, k, :].bitcast(f32), ALU.subtract).then_inc(pnT_lo_ready, 1)
            for m in range(KD):
                dve.wait_ge(pw_hi_ready, m + 1)
                nc.vector.tensor_tensor(pw_all[:, m, :, S:2 * S], bank[m][:, :].rearrange("p (b s) -> p b s", b=B),
                                        pw_all[:, m, :, 0:S].bitcast(f32), ALU.subtract).then_inc(pw_lo_ready, 1)
            dve.wait_ge(pb_ready, 1)

            def evacuate(b, c):
                for g, ks in groups(c):
                    dve.wait_ge(t_hi, G * b + g + 1)
                    n = width(c) if len(ks) == 1 else REMP
                    nc.vector.tensor_tensor(ct_lo[c % 2][:, ks[0]:ks[-1] + 1, 0:n],
                                            t_bank(g)[:, :].rearrange("p (k n) -> p k n", k=len(ks))[:, :, 0:n],
                                            ct_hi[c % 2][:, ks[0]:ks[-1] + 1, 0:n].bitcast(f32), ALU.subtract).then_inc(t_lo, 1)

            def add_scores(b, par, c):
                dve.wait_ge(s_low, NC * b + c + 1)
                if c == 0 and not (isinstance(b, int) and b < 2):
                    dve.wait_ge(pt_done, 2 * (b - 1))
                nc.vector.tensor_tensor(sc[par][0:S, 512 * c:512 * c + width(c)], SB[c % 2][0:S, 0:width(c)],
                                        sc_low[c % 2][:, 0:width(c)], ALU.add).then_inc(s_ready, 1)

            def chunk_max(b, par, c):
                dve.wait_ge(s_ready, NC * b + c + 1)
                return nc.vector.reduce_max(mx4[:, c:c + 1], sc[par][0:S, 512 * c:512 * c + width(c)], AX.X)

            def split_ctx(b, par, c):
                if c in POOL_CHUNKS:
                    return
                first, last = CH * c, min(CH * (c + 1), NKT)
                dve.wait_ge(nat_hi_ready, NC * b + c + 1)
                nc.vector.tensor_tensor(nat_lo[:, first:last, :], raw[par][:, first:last, :],
                                        nat_hi[:, first:last, :].bitcast(f32), ALU.subtract).then_inc(nat_lo_ready[c], 1)

            def step_to(ins_, n):
                ins_.then_inc(dve_step, 1)
                dve.wait_ge(dve_step, n)

            base = steps[0]

            def max_stage(b, par):
                n = base + 3 * b
                step_to(chunk_max(b, par, 3), n + 1)
                step_to(nc.vector.reduce_max(mx[:, 0:1], mx4[:, :], AX.X), n + 2)
                step_to(nc.vector.tensor_tensor(mx[:, 1:2], mx[:, 0:1], pb[:, bass.ds(b, 1)], ALU.add), n + 3)
                if not (isinstance(b, int) and b < 2):
                    dve.wait_ge(exp_done, b - 1)
                nc.vector.tensor_tensor(nbias[par][:, :], pb[:, bass.ds(b, 1)], mx[:, 1:2], ALU.subtract).then_inc(max_ready, 1)

            def prob_parts(b):
                for h, (t0, t1) in enumerate(PT_SPLIT):
                    dve.wait_ge(pt_hi, 2 * b + h + 1)
                    nc.vector.tensor_tensor(pT[:, t0:t1, S:2 * S], PB[h][:, 0:(t1 - t0) * S].rearrange("p (j s) -> p j s", s=S),
                                            pT[:, t0:t1, 0:S].bitcast(f32), ALU.subtract).then_inc(pt_lo, 1)

            def stage(b, par, scores=True, values=True, earlier=True):
                n, npar = b + 1, 1 - par
                if scores:
                    evacuate(n, 0)
                if values:
                    split_ctx(b, par, 0)
                if scores:
                    evacuate(n, 1)
                if values:
                    split_ctx(b, par, 1)
                    prob_parts(b)
                    if earlier:
                        dve.wait_ge(av_ready, b)
                    dve.wait_ge(exp_done, b + 1)
                    nc.vector.reciprocal(rinv[:, :], rsum[par][:, :]).then_inc(rinv_ready, 1)
                if scores:
                    add_scores(n, npar, 0)
                    evacuate(n, 2)
                    chunk_max(n, npar, 0)
                if values:
                    split_ctx(b, par, 2)
                if scores:
                    add_scores(n, npar, 1)
                    evacuate(n, 3)
                    chunk_max(n, npar, 1)
                if values:
                    split_ctx(b, par, 3)
                if scores:
                    add_scores(n, npar, 2)
                    chunk_max(n, npar, 2)
                    add_scores(n, npar, 3)
                if values:
                    dve.wait_ge(pv_low_ready, b + 1)
                    nc.vector.tensor_tensor(pv_low[:, :], VB[0:S, :], pv_low[:, :], ALU.add).then_inc(av_sum, 1)
                if scores:
                    max_stage(n, npar)

            dve.wait_ge(sc_zeroed, 2)
            stage(-1, 1, values=False, earlier=False)
            stage(0, 0, earlier=False)
            with dve.Fori(0, B // 2 - 1) as i:
                stage(2 * i + 1, 1)
                stage(2 * i + 2, 0)
            stage(B - 1, 1, scores=False)
            for k in range(KD):
                dve.wait_ge(WT_hi_ready, k + 1)
                nc.vector.tensor_tensor(WT_lo[:, k, :], bank[k][:, :], WT_hi[:, k, :].bitcast(f32), ALU.subtract).then_inc(WT_lo_ready, 1)
            dve.wait_ge(avT_hi_ready, 1)
            nc.vector.tensor_tensor(avT_lo[:, :, :], avT[:, :, :], avT_hi[:, :, :].bitcast(f32), ALU.subtract).then_inc(avT_lo_ready, 1)
            dve.wait_ge(b_loaded, 32)
            for t in range(NT):
                dve.wait_ge(xo_done, t + 1)
                step_to(nc.vector.tensor_tensor(xo[:, t, :], bank[t][:, :], b_bc[:, :], ALU.add), base + 3 * B + t + 1)
                nc.vector.scalar_tensor_tensor(xt[:, t, :], xo[:, t, :], 0.0, xt[:, t, :], ALU.max, ALU.add).then_inc(x1_ready, 1)

            steps[0] = base + 3 * B + NT

            def norm_stats(src, n):
                for t in range(NT):
                    last = nc.vector.bn_stats(stats[:, t, :], src[:, t, :])
                link(last)
                for t in range(NT):
                    last = nc.vector.bn_aggr(mv[:, t, :], stats[:, t, :])
                link(last)
                nc.vector.tensor_scalar(rstd[:, :], mv[:, :, 1], EPS, None, ALU.add).then_inc(var_ready, 1)
                dve.wait_ge(rstd_ready, n)

            def normalise(dst, src, t):
                return nc.vector.tensor_scalar(dst[:, t, :], src[:, t, :], mv[:, t, 0:1], rstd[:, t:t + 1], ALU.subtract, ALU.mult)

            def gained(src):
                for t in range(NT):
                    last = normalise(xn, src, t)
                link(last)
                for t in range(NT):
                    last = nc.vector.tensor_tensor(xn[:, t, :], xn[:, t, :], gain[:, :], ALU.mult)
                link(last)
                for t in range(NT):
                    nc.vector.tensor_tensor(xn[:, t, :], xn[:, t, :], shift[:, :], ALU.add).then_inc(xn_ready, 1)

            def split_w(u):
                dve.wait_ge(*upper(u))
                if u >= RING:
                    dve.wait_ge(*USED[u - RING])
                nc.vector.tensor_tensor(w_lo[u % RING][:, :, :], w_raw[u % RING][:, :, :], w_hi[u % RING][:, :, :].bitcast(f32),
                                        ALU.subtract).then_inc(w_lo_ready[u % RING], 1)

            def lower_xT(n):
                for k in range(KD):
                    dve.wait_ge(xT_hi_ready, KD * n + k + 1)
                    nc.vector.tensor_tensor(xT_lo[:, k, :], bank[k][:, :], xT_hi[:, k, :].bitcast(f32), ALU.subtract).then_inc(xT_lo_ready, 1)

            dve.wait_ge(x1_ready, NT)
            nc.vector.memset(zeros[:, :], 0.0).then_inc(zeros_ready, 1)
            nc.vector.memset(proj2[:, :], 0.0).then_inc(proj_zero, 1)
            nc.vector.memset(v1[:, :, :, DH:DH + 1], 1.0).then_inc(v_one, 1)
            norm_stats(xt, 2)
            for t in range(NT):
                last = normalise(x1n, xt, t)
            link(last)
            norm_stats(x1n, 3)
            dve.wait_ge(vec_loaded, 48)
            gained(x1n)
            dve.wait_ge(proj_hi_ready, 1)
            nc.vector.tensor_tensor(proj2_lo[:, :], proj2[:, :], proj2_hi[:, :].bitcast(f32), ALU.subtract).then_inc(proj_lo_ready, 1)
            split_w(0)
            lower_xT(0)
            split_w(1)
            split_w(2)

            def lower_z(n):
                dve.wait_ge(z_hi_ready, n + 1)
                nc.vector.tensor_tensor(z_lo[n % 2][:, :], bank[n % 2][:, :], z_hi[n % 2][:, :].bitcast(f32), ALU.subtract).then_inc(z_lo_ready, 1)

            def negative(n):
                dve.wait_ge(f_done, n + 1)
                nc.vector.tensor_scalar(neg[n % 2][:, :], bank[2 + n % 2][:, :], 0.0, None, ALU.min).then_inc(neg_ready, 1)

            def feature(n):
                dve.wait_ge(e_ready, n + 1)
                nc.vector.scalar_tensor_tensor(phi[n // 8][:, n % 8, :], bank[2 + n % 2][:, :], 0.0, neg[n % 2][:, :],
                                               ALU.max, ALU.add).then_inc(phi_ready, 1)

            for n in range(H):
                lower_z(n)
                if n >= 1:
                    negative(n - 1)
                if n % 4 == 0 and n // 4 + 2 >= RING:
                    split_w(n // 4 + 2)
                if n >= 1:
                    feature(n - 1)
            negative(H - 1)
            feature(H - 1)
            for u in range(2):
                dve.wait_ge(v_ready, NT * (u + 1))
                split_w(6 + u)
            dve.wait_ge(mask_ready, 1)
            NG = 4 * NT

            def masked(n):
                dve.wait_ge(a_done, n + 1)
                if n >= 2:
                    dve.wait_ge(o_done, n - 1)
                nc.vector.tensor_tensor(at[n % 2][:, :, :], bank[n % 4][:, :].rearrange("p (h q) -> p h q", h=4),
                                        mask[:, :].unsqueeze(1).to_broadcast([P, 4, P]), ALU.mult).then_inc(a_ready, 1)

            def divided(n):
                t, g, s = n // 4, n // 2 % 2, n % 2
                o = bank[6 + n % 2][:, 0:4 * (DH + 1)].rearrange("p (h d) -> p h d", d=DH + 1)
                dve.wait_ge(o_done, n + 1)
                link(nc.vector.tensor_scalar(den[:, 0, :], o[:, :, DH], 1e-6, None, ALU.add))
                link(nc.vector.reciprocal(den[:, 1, :], den[:, 0, :]))
                if n % 4 == 0 and t >= 2:
                    dve.wait_ge(oT_done, 2 * (t - 1))
                dst = heads[:, t % 2, :].rearrange("p (m s d) -> p m s d", s=2, d=DH)[:, 4 * g:4 * (g + 1), s, :]
                nc.vector.tensor_tensor(dst, o[:, :, 0:DH], den[:, 1, :].unsqueeze(2).to_broadcast([P, 4, DH]), ALU.mult).then_inc(o_ready, 1)

            def lower_oT(t):
                for half in range(2):
                    dve.wait_ge(oT_hi_ready, 2 * t + half + 1)
                    nc.vector.tensor_tensor(oT_lo[:, 4 * half:4 * (half + 1), :], bank[4 + half][:, :].rearrange("p (k n) -> p k n", n=P),
                                            oT_hi[:, 4 * half:4 * (half + 1), :].bitcast(f32), ALU.subtract).then_inc(oT_lo_ready, 1)

            def attended(t):
                dve.wait_ge(ao_done, t + 1)
                nc.vector.tensor_tensor(x1n[:, t, :], x1n[:, t, :], bank[6 + t % 2][:, :], ALU.add).then_inc(xa_ready, 1)

            for t in range(NT):
                for n in range(4 * t, 4 * t + 4):
                    masked(n)
                    if n % 4 >= 1:
                        divided(n - 1)
                divided(4 * t + 3)
                lower_oT(t)
                if t == 0:
                    split_w(8)
                attended(t)
            dve.wait_ge(xa_ready, NT)
            norm_stats(x1n, 4)
            dve.wait_ge(vec2_loaded, 32)
            gained(x1n)
            split_w(9)
            lower_xT(1)
            split_w(10)
            for n in range(FF // P):
                dve.wait_ge(gelu_ready, n + 1)
                if n >= 2:
                    dve.wait_ge(dn_done, n - 1)
                nc.vector.tensor_copy(gl_hi[n % 2][:, :], gl[n % 2][:, :]).then_inc(gl_hi_ready, 1)
                dve.wait_ge(gl_hi_ready, n + 1)
                nc.vector.tensor_tensor(gl_lo[n % 2][:, :], gl[n % 2][:, :], gl_hi[n % 2][:, :].bitcast(f32), ALU.subtract).then_inc(gl_lo_ready, 1)
                if n % 4 == 3 and n < FF // P - 1:
                    split_w(11 + 2 * (n // 4))
                if n % 4 == 0 and 4 <= n < FF // P - 4:
                    split_w(10 + n // 2)
            for t in range(NT):
                last = nc.vector.tensor_tensor(xt[:, t, :], xt[:, t, :], x1n[:, t, :], ALU.add)
            link(last)
            for t in range(NT):
                last = nc.vector.tensor_tensor(xt[:, t, :], xt[:, t, :], b2_bc[:, :], ALU.add)
            link(last)
            dve.wait_ge(dn_done, FF // P)
            for t in range(NT):
                nc.vector.tensor_tensor(xt[:, t, :], xt[:, t, :], bank[4 + t][:, :], ALU.add).then_inc(x2_ready, 1)

            dve.wait_ge(x2_ready, NT)
            norm_stats(xt, 5)
            for t in range(NT):
                normalise(xn, xt, t).then_inc(xn_ready, 1)
            dve.wait_ge(index_ready, 1)
            link(nc.vector.tensor_copy(e_idx[:, :], e_int[:, :]))
            link(nc.vector.tensor_scalar(pref[:, :], e_idx[:, :], -1.0, float(E), ALU.mult, ALU.add))
            nc.vector.memset(yb[:, 0:256], 0.0).then_inc(y_ready, 1)
            nc.vector.memset(yb[:, 256:512], 0.0).then_inc(y_stored, 1)

            def over_tokens(a):
                return a.unsqueeze(1).to_broadcast([P, NT, E])

            def over_experts(a):
                return a.unsqueeze(2).to_broadcast([P, NT, E])

            def split_e(e, j):
                if j not in POOL_UNITS:
                    dve.wait_ge(e_hi_ready[j], turn_of(e, j))
                    nc.vector.tensor_tensor(e_lo[j][:, :, :], e_raw[j][:, :, :], e_hi[j][:, :, :].bitcast(f32),
                                            ALU.subtract).then_inc(e_lo_ready[j], 1)

            for j in range(RING):
                split_e(0, j)
            dve.wait_ge(logits_done, 1)
            link(nc.vector.tensor_copy(logits[:, :, :], bank[4][:, 0:NT * E].rearrange("p (t e) -> p t e", e=E)))
            for k in range(2):
                link(nc.vector.reduce_max(best[k][:, :], logits[:, :, :], AX.X))
                link(nc.vector.tensor_tensor(scr[:, :, :], logits[:, :, :], over_experts(best[k][:, :]), ALU.is_equal))
                link(nc.vector.tensor_tensor(scr[:, :, :], scr[:, :, :], over_tokens(pref[:, :]), ALU.mult))
                link(nc.vector.reduce_max(top[:, :], scr[:, :, :], AX.X))
                link(nc.vector.tensor_tensor(pick[k][:, :, :], scr[:, :, :], over_experts(top[:, :]), ALU.is_equal))
                if k == 0:
                    link(nc.vector.scalar_tensor_tensor(logits[:, :, :], pick[0][:, :, :], -3e38, logits[:, :, :], ALU.mult, ALU.add))
            nc.vector.tensor_tensor(chosen[:, :, :], pick[0][:, :, :], pick[1][:, :, :], ALU.add).then_inc(chosen_ready, 1)
            nc.vector.tensor_tensor(gap[:, :], best[1][:, :], best[0][:, :], ALU.subtract).then_inc(gap_ready, 1)
            split_e(0, 3)
            dve.wait_ge(rank_done, 1)
            nc.vector.tensor_copy(rank[:, :, :], bank[5][:, 0:NT * E].rearrange("p (t e) -> p t e", e=E))
            link(nc.vector.tensor_copy(count[:, :], bank[5][:, NT * E:(NT + 1) * E]))
            link(nc.vector.tensor_scalar(extra[:, :], count[:, :], float(P), None, ALU.is_gt))
            for n in range(2, B * S // P):
                link(nc.vector.scalar_tensor_tensor(extra[:, :], count[:, :], float(n * P), extra[:, :], ALU.is_gt, ALU.add))
            dve.wait_ge(order_ready, 2)
            link(nc.vector.tensor_tensor(scr8[:, :, :], upto[:, :, :], extra[:, :].unsqueeze(1).to_broadcast([P, E, E]), ALU.mult))
            link(nc.vector.tensor_reduce(upto_extra[:, :], scr8[:, :, :], AX.X, ALU.add))
            link(nc.vector.tensor_tensor(upto_extra[:, :], upto_extra[:, :], e_idx[:, :], ALU.add))
            link(nc.vector.tensor_tensor(first_block[:, :], upto_extra[:, :], extra[:, :], ALU.subtract))
            link(nc.vector.scalar_tensor_tensor(rank[:, :, :], over_tokens(first_block[:, :]), float(P), rank[:, :, :], ALU.mult, ALU.add))
            for k in range(2):
                link(nc.vector.tensor_tensor(scr[:, :, :], rank[:, :, :], pick[k][:, :, :], ALU.mult))
                link(nc.vector.tensor_reduce(slotf[k][:, :], scr[:, :, :], AX.X, ALU.add))
                nc.vector.tensor_copy(slot_of[k][:, :], slotf[k][:, :]).then_inc(slots_ready, 1)
            nc.vector.tensor_copy(blocks[:, 0, :], first_block[:, :]).then_inc(slots_ready, 1)
            nc.vector.tensor_copy(blocks[:, 1, :], upto_extra[:, :]).then_inc(slots_ready, 1)
            dve.wait_ge(gap_exp, 1)
            link(nc.vector.tensor_scalar(gap[:, :], gsum[:, :], 1.0, None, ALU.add))
            link(nc.vector.reciprocal(gate[0][:, :], gap[:, :]))
            link(nc.vector.tensor_tensor(gate[1][:, :], gate[0][:, :], gsum[:, :], ALU.mult))

            def lower_rows(b):
                dve.wait_ge(xgT_hi_ready, b + 1)
                nc.vector.tensor_tensor(xgT_lo[:, :, :], bank[7][:, :].rearrange("p (k n) -> p k n", n=P), xgT_hi[:, :, :].bitcast(f32),
                                        ALU.subtract).then_inc(xgT_lo_ready, 1)

            def hidden(b, half):
                dve.wait_ge(silu_ready, 2 * b + half + 1)
                dve.wait_ge(unit_done[2 * half + 1], b + 1)
                nc.vector.tensor_tensor(hm[half][:, :], bank[2 * half + 1][:, :], sg[half][:, :], ALU.mult).then_inc(hm_ready, 1)

            def lower_hidden(b, half):
                dve.wait_ge(hmT_hi_ready, 2 * b + half + 1)
                nc.vector.tensor_tensor(hmT_lo[half][:, :, :], bank[4 + half][:, :].rearrange("p (k n) -> p k n", n=P),
                                        hmT_hi[half][:, :, :].bitcast(f32), ALU.subtract).then_inc(hmT_lo_ready, 1)

            def expert_block(b, e, again=False, last=False):
                def split(j):
                    if not again and not last:
                        split_e(e + 1, j)

                hidden(b, 0)
                split(0)
                lower_hidden(b, 0)
                hidden(b, 1)
                if not last:
                    lower_rows(b + 1)
                split(1)
                lower_hidden(b, 1)
                split(2)
                split(3)

            lower_rows(0)
            dve.wait_ge(slots_ready, 4)
            with dve.Fori(0, E - 1) as e:
                first_b, last_b = expert_blocks(dve, e)
                with dve.If(first_b < last_b):
                    with dve.Fori(first_b, last_b) as b:
                        expert_block(b, e, again=True)
                expert_block(last_b, e)
            first_b, last_b = expert_blocks(dve, E - 1)
            with dve.If(first_b < last_b):
                with dve.Fori(first_b, last_b) as b:
                    expert_block(b, E - 1, again=True)
            expert_block(last_b, E - 1, last=True)
            for t in range(NT):
                dve.wait_ge(gathered[t], 32)
                for k in range(2):
                    mm = nc.vector.scalar_tensor_tensor(xt[:, t, :], yt[k][:, t, :], gate[k][:, t:t + 1], xt[:, t, :], ALU.mult, ALU.add)
                    if k == 0:
                        link(mm)
                mm.then_inc(xo_ready, 1)

        @block.tensor
        def _(pe):
            def product(dst, left, right, first=True, last=True):
                n = len(left)
                for k, ((lh, ll), (rh, rl)) in enumerate(zip(left, right)):
                    nc.tensor.matmul(dst, lh, rh, start=first and k == 0, stop=False)
                    nc.tensor.matmul(dst, lh, rl, start=False, stop=False)
                    mm = nc.tensor.matmul(dst, ll, rh, start=False, stop=last and k == n - 1)
                return mm

            def turn(dst, src, waited):
                if waited:
                    return nc.tensor.matmul(dst, src, ident[0:S, 0:S], start=True, stop=True)
                return nc.tensor.transpose(dst, src, ident[0:S, 0:S])

            pe.wait_ge(const_ready, 1)
            pe.wait_ge(pn_ready, NT)
            for k in range(KD):
                for t in range(NT):
                    mm = nc.tensor.transpose(bank[k][:, t * P:(t + 1) * P], pn[:, t, k * P:(k + 1) * P], ident[:, :])
                mm.then_inc(pnT_done, 1)
            pe.wait_ge(W_lo_ready, 1)
            pe.wait_ge(pnT_lo_ready, KD)
            for m in range(KD):
                product(bank[m][:, :], [(W_hi[:, k, m * P:(m + 1) * P], W_lo[:, k, m * P:(m + 1) * P]) for k in range(KD)],
                        [(pnT_hi[:, k, :], pnT_lo[:, k, :]) for k in range(KD)]).then_inc(pwT_done, 1)
            pe.wait_ge(b_loaded, 16)
            for b in range(B):
                for k in range(KD):
                    mm = nc.tensor.matmul(bank[4][0:S, b:b + 1], pnT[:, k, b * S:(b + 1) * S], b_col[:, k:k + 1],
                                          start=k == 0, stop=k == KD - 1)
            mm.then_inc(pb_done, 1)
            pe.wait_ge(pw_lo_ready, KD)
            pe.wait_ge(pb_ready, 1)

            def transposes(b, par, c):
                pe.wait_ge(ctx_loaded[par][c], 16 * (b // 2 + 1) if isinstance(b, int) else 16 * ((b - par) // 2 + 1))
                tiles = range(CH * c, min(CH * (c + 1), NKT))
                for g, ks in groups(c):
                    before = t_before(b, g)
                    if before is not None:
                        pe.wait_ge(t_lo, before)
                    for k in ks:
                        for n, j in enumerate(tiles):
                            rows = P if j < FULL else REMP
                            at = (k - ks[0]) * P + n * P
                            mm = nc.tensor.transpose(t_bank(g)[:, at:at + rows], raw[par][0:rows, j, k * P:(k + 1) * P],
                                                     ident[0:rows, 0:rows])
                    mm.then_inc(t_done, 1)

            def scores(b, par, c):
                g_last = groups(c)[-1][0]
                pe.wait_ge(t_lo, G * b + g_last + 1)
                if c >= 2:
                    pe.wait_ge(s_ready, NC * b + c - 1)
                elif not (isinstance(b, int) and b == 0):
                    pe.wait_ge(s_ready, NC * (b - 1) + NC - 2 + c + 1)
                n = width(c) if c < NC - 1 else REMP
                for k in range(KD):
                    nc.tensor.matmul(SB[c % 2][:, 0:n], pw[par][:, k, :], ct_hi[c % 2][:, k, 0:n], start=k == 0, stop=False)
                    mm = nc.tensor.matmul(SB[c % 2][:, 0:n], pw[par][:, k, :], ct_lo[c % 2][:, k, 0:n], start=False, stop=k == KD - 1)
                mm.then_inc(qk_done, 1)

            def av_transposes(b):
                pe.wait_ge(av_ready, b + 1)
                for k in range(KD):
                    mm = turn(VB[:, k * S:(k + 1) * S], av[:, k * P:(k + 1) * P], k == 0)
                mm.then_inc(avt_done, 1)

            def prob_transposes(b, par):
                pe.wait_ge(exp_done, b + 1)
                for h, (t0, t1) in enumerate(PT_SPLIT):
                    if not (isinstance(b, int) and b == 0):
                        pe.wait_ge(pt_lo, 2 * (b - 1) + h + 1)
                    for j in range(t0, t1):
                        mm = turn(PB[h][:, (j - t0) * S:(j - t0 + 1) * S], sc[par][:, j * P:(j + 1) * P], j == t0)
                    mm.then_inc(pt_done, 1)

            def values_of(b, c):
                if c == 0 and not (isinstance(b, int) and b == 0):
                    pe.wait_ge(avt_ready, b)
                for h, (t0, t1) in enumerate(PT_SPLIT):
                    if CH * c == t0:
                        pe.wait_ge(pt_lo, 2 * b + h + 1)
                pe.wait_ge(nat_lo_ready[c], b + 1)
                for j in range(CH * c, min(CH * (c + 1), NKT)):
                    nc.tensor.matmul(VB[:, :], pT[:, j, :], nat_hi[:, j, :], start=j == 0, stop=False)
                    mm = nc.tensor.matmul(VB[:, :], pT[:, j, :], nat_lo[:, j, :], start=False, stop=j == NKT - 1)
                mm.then_inc(pv_done, 1)

            def stage(b, par, scores_too=True, values=True, earlier=True):
                n, npar = b + 1, 1 - par
                if scores_too:
                    transposes(n, npar, 0)
                if earlier:
                    av_transposes(b - 1)
                if scores_too:
                    transposes(n, npar, 1)
                if values:
                    prob_transposes(b, par)
                if scores_too:
                    pe.wait_ge(pw_ready, n + 1)
                    scores(n, npar, 0)
                if values:
                    values_of(b, 0)
                if scores_too:
                    transposes(n, npar, 2)
                    scores(n, npar, 1)
                if values:
                    values_of(b, 1)
                if scores_too:
                    transposes(n, npar, 3)
                    scores(n, npar, 2)
                if values:
                    values_of(b, 2)
                    values_of(b, 3)
                if scores_too:
                    scores(n, npar, 3)

            stage(-1, 1, values=False, earlier=False)
            stage(0, 0, earlier=False)
            with pe.Fori(0, B // 2 - 1) as i:
                stage(2 * i + 1, 1)
                stage(2 * i + 2, 0)
            stage(B - 1, 1, scores_too=False)
            pe.wait_ge(W_loaded, 32)
            for k in range(KD):
                for m in range(KD):
                    mm = nc.tensor.transpose(bank[k][:, m * P:(m + 1) * P], We[:, m, k * P:(k + 1) * P], ident[:, :])
                mm.then_inc(WT_done, 1)
            av_transposes(B - 1)
            pe.wait_ge(WT_lo_ready, KD)
            pe.wait_ge(avT_lo_ready, 1)
            for t in range(NT):
                product(bank[t][:, :], [(avT_hi[:, k, t * P:(t + 1) * P], avT_lo[:, k, t * P:(t + 1) * P]) for k in range(KD)],
                        [(WT_hi[:, k, :], WT_lo[:, k, :]) for k in range(KD)]).then_inc(xo_done, 1)

            def parts(u):
                return w_hi[u % RING], w_lo[u % RING]

            def transpose_xn(n):
                pe.wait_ge(xn_ready, NT * (n + 1))
                for k in range(KD):
                    for t in range(NT):
                        mm = nc.tensor.transpose(bank[k][:, t * P:(t + 1) * P], xn[:, t, k * P:(k + 1) * P], ident[:, :])
                    mm.then_inc(xT_done, 1)
                pe.wait_ge(xT_lo_ready, KD * (n + 1))

            xT = [(xT_hi[:, k, :], xT_lo[:, k, :]) for k in range(KD)]

            def columns(u, m):
                hi, lo = parts(u)
                return [(hi[:, k, m * P:(m + 1) * P], lo[:, k, m * P:(m + 1) * P]) for k in range(KD)]

            def rows(u):
                hi, lo = parts(u)
                return [(hi[:, k, :], lo[:, k, :]) for k in range(KD)]

            pe.wait_ge(x1_ready, NT)
            transpose_xn(0)

            def features(n):
                pe.wait_ge(z_lo_ready, n + 1)
                if n >= 2:
                    pe.wait_ge(phi_ready, n - 1)
                product(bank[2 + n % 2][:, :], [(proj2_hi[:, :], proj2_lo[:, :])], [(z_hi[n % 2][:, :], z_lo[n % 2][:, :])]).then_inc(f_done, 1)

            pe.wait_ge(proj_lo_ready, 1)
            for n in range(H):
                u = n // 4
                if n % 4 == 0:
                    pe.wait_ge(*lower(u))
                if n >= 2:
                    pe.wait_ge(z_lo_ready, n - 1)
                product(bank[n % 2][:, :], columns(u, n % 4), xT).then_inc(z_done, 1)
                if n >= 1:
                    features(n - 1)
            features(H - 1)
            for u in range(2):
                pe.wait_ge(*lower(4 + u))
                for t in range(NT):
                    n = NT * u + t
                    if n >= 2:
                        pe.wait_ge(v_ready, n - 1)
                    product(bank[4 + n % 2][:, :], [(hi[:, t * P:(t + 1) * P], lo[:, t * P:(t + 1) * P]) for hi, lo in xT],
                            rows(4 + u)).then_inc(v_done, 1)
            pe.wait_ge(v_ready, 2 * NT)
            pe.wait_ge(v_one, 1)
            pe.wait_ge(phi_ready, H)

            def weights(n):
                t, g, s = n // 4, n // 2 % 2, n % 2
                if n >= 4:
                    pe.wait_ge(a_ready, n - 3)
                half = slice(DH * s, DH * (s + 1))
                for m in range(4):
                    k, q = (phi[i][half, 4 * g + m, t * P:(t + 1) * P] for i in (1, 0))
                    mm = nc.tensor.matmul(bank[n % 4][:, m * P:(m + 1) * P], k, q, start=True, stop=True)
                mm.then_inc(a_done, 1)

            def weighted(n):
                t, g, s = n // 4, n // 2 % 2, n % 2
                pe.wait_ge(a_ready, n + 1)
                if n >= 2:
                    pe.wait_ge(o_ready, n - 1)
                if t and n % 4 < 2:
                    pe.wait_ge(xa_ready, t)
                for m in range(4):
                    head = 2 * (4 * g + m) + s
                    mm = nc.tensor.matmul(bank[6 + n % 2][:, m * (DH + 1):(m + 1) * (DH + 1)], at[n % 2][:, m, :], v1[:, t, head, :],
                                          start=True, stop=True)
                mm.then_inc(o_done, 1)

            for t in range(NT):
                for n in range(4 * t, 4 * t + 4):
                    weights(n)
                    if n % 4 >= 1:
                        weighted(n - 1)
                weighted(4 * t + 3)
                pe.wait_ge(o_ready, 4 * t + 4)
                for half in range(2):
                    if t >= 1:
                        pe.wait_ge(oT_lo_ready, 2 * t - 1 + half)
                    for k in range(4):
                        at_ = (4 * half + k) * P
                        mm = nc.tensor.transpose(bank[4 + half][:, k * P:(k + 1) * P], heads[:, t % 2, at_:at_ + P], ident[:, :])
                    mm.then_inc(oT_done, 1)
                pe.wait_ge(oT_lo_ready, 2 * t + 2)
                pe.wait_ge(*lower(6))
                pe.wait_ge(*lower(7))
                product(bank[6 + t % 2][:, :], [(oT_hi[:, k, :], oT_lo[:, k, :]) for k in range(HD // P)],
                        rows(6) + rows(7)).then_inc(ao_done, 1)
            transpose_xn(1)

            def down(n):
                if n % 4 == 0:
                    pe.wait_ge(*lower(9 + 2 * (n // 4)))
                hi, lo = parts(9 + 2 * (n // 4))
                pe.wait_ge(gl_lo_ready, n + 1)
                for t in range(NT):
                    left = (gl_hi[n % 2][:, t * P:(t + 1) * P], gl_lo[n % 2][:, t * P:(t + 1) * P])
                    mm = product(bank[4 + t][:, :], [left], [(hi[:, n % 4, :], lo[:, n % 4, :])], n == 0, n == FF // P - 1)
                mm.then_inc(dn_done, 1)

            for n in range(FF // P):
                u = 8 + 2 * (n // 4)
                if n % 4 == 0:
                    pe.wait_ge(*lower(u))
                if n >= 2:
                    pe.wait_ge(gelu_ready, n - 1)
                product(bank[n % 2][:, :], columns(u, n % 4), xT).then_inc(up_done, 1)
                if n >= 1:
                    down(n - 1)
            down(FF // P - 1)

            pe.wait_ge(xn_ready, 3 * NT)
            pe.wait_ge(gelu_ready, FF // P)
            for k in range(KD):
                for t in range(NT):
                    mm = nc.tensor.transpose(bank[k][:, t * P:(t + 1) * P], xn[:, t, k * P:(k + 1) * P], ident[:, :])
                mm.then_inc(xT_done, 1)
            pe.wait_ge(xT32_ready, KD)
            pe.wait_ge(router_loaded, 16)
            for t in range(NT):
                for k in range(KD):
                    mm = nc.tensor.matmul(bank[4][:, t * E:(t + 1) * E], xT32[:, k, t * P:(t + 1) * P], w_router[:, k, :],
                                          start=k == 0, stop=k == KD - 1)
            mm.then_inc(logits_done, 1)
            pe.wait_ge(chosen_ready, 1)
            pe.wait_ge(order_ready, 2)
            for t in range(NT + 1):
                for m in range(min(t + 1, NT)):
                    mm = nc.tensor.matmul(bank[5][:, t * E:(t + 1) * E], before[:, :] if m == t else ones[:, :], chosen[:, m, :],
                                          start=m == 0, stop=m == min(t, NT - 1))
            mm.then_inc(rank_done, 1)

            def rows_transposed(b):
                pe.wait_ge(xg_loaded, 16 * (b + 1))
                for k in range(KD):
                    mm = nc.tensor.transpose(bank[7][:, k * P:(k + 1) * P], xg[:, k * P:(k + 1) * P], ident[:, :])
                mm.then_inc(xgT_done, 1)

            def unit_rows(j):
                return [(e_hi[j][:, k, :], e_lo[j][:, k, :]) for k in range(KD)]

            def up(e, j):
                pe.wait_ge(e_lo_ready[j], turn_of(e, j))
                product(bank[j][:, :], [(xgT_hi[:, k, :], xgT_lo[:, k, :]) for k in range(KD)], unit_rows(j)).then_inc(unit_done[j], 1)

            def hidden_transposed(b, half):
                pe.wait_ge(hm_ready, 2 * b + half + 1)
                for k in range(4):
                    mm = nc.tensor.transpose(bank[4 + half][:, k * P:(k + 1) * P], hm[half][:, k * P:(k + 1) * P], ident[:, :])
                mm.then_inc(hmT_done, 1)

            def down_half(b, e, half):
                pe.wait_ge(e_lo_ready[4 + half], turn_of(e, 4 + half))
                pe.wait_ge(hmT_lo_ready, 2 * b + half + 1)
                product(bank[6][:, :], [(hmT_hi[half][:, k, :], hmT_lo[half][:, k, :]) for k in range(4)], unit_rows(4 + half),
                        half == 0, half == 1).then_inc(unit_done[4 + half], 1)

            def expert_block(b, e, again=False, last=False):
                up(e, 1)
                up(e, 2)
                hidden_transposed(b, 0)
                up(e, 3)
                if not last:
                    rows_transposed(b + 1)
                pe.wait_ge(y_ready, b + 1)
                down_half(b, e, 0)
                hidden_transposed(b, 1)
                if not last:
                    pe.wait_ge(xgT_lo_ready, b + 2)
                    up(e if again else e + 1, 0)
                down_half(b, e, 1)

            rows_transposed(0)
            pe.wait_ge(xgT_lo_ready, 1)
            up(0, 0)
            pe.wait_ge(slots_ready, 4)
            with pe.Fori(0, E - 1) as e:
                first_b, last_b = expert_blocks(pe, e)
                with pe.If(first_b < last_b):
                    with pe.Fori(first_b, last_b) as b:
                        expert_block(b, e, again=True)
                expert_block(last_b, e)
            first_b, last_b = expert_blocks(pe, E - 1)
            with pe.If(first_b < last_b):
                with pe.Fori(first_b, last_b) as b:
                    expert_block(b, E - 1, again=True)
            expert_block(last_b, E - 1, last=True)


def kernel(**inputs):
    import numpy as _np
    import concourse.bacc as _bacc
    from concourse import mybir as _mybir
    from concourse.bass_utils import run_bass_kernel_spmd as _run

    nc = _bacc.Bacc("TRN2", target_bir_lowering=False, num_devices=1)
    arrays, args = {}, {}
    for name in inputs:
        a = _np.ascontiguousarray(inputs[name])
        arrays[f"in_{name}_dram"] = a
        args[name] = nc.dram_tensor(f"in_{name}_dram", a.shape, _mybir.dt.from_np(a.dtype), kind="ExternalInput").ap()
    out = nc.dram_tensor("out_0_dram", inputs["x"].shape, _mybir.dt.float32, kind="ExternalOutput").ap()
    perceiver_block(nc, args, out)
    r = _run(nc, [arrays], core_ids=[0])
    return r.results[0]["out_0_dram"]
```

```python
import concourse.bass as bass
from concourse import mybir
from contextlib import ExitStack


def perceiver_block(nc, ins, out):
    f32, f32r = mybir.dt.float32, mybir.dt.float32r
    ACT = mybir.ActivationFunctionType
    ALU = mybir.AluOpType
    AX = mybir.AxisListType

    P = 128
    B, S, D = ins["x"].shape
    KEYS = ins["ctx_1024"].shape[1]
    NT = B * S // P
    KD = D // P
    CH = 4
    FULL = KEYS // P
    NC = FULL // CH + 1
    REM = KEYS - FULL * P
    REMP = REM + REM % 2
    NKT = FULL + 1
    assert FULL % CH == 0 and REM > 0
    EPS = 1e-5

    H, DH = 16, 64
    HD = H * DH
    FF = ins["L0_attn_w1"].shape[1]
    E, _, FE = ins["L0_ffn_w0"].shape
    OV = 7
    NB = E + OV
    RING = 3
    assert HD == 2 * 512 and FE == 2 * 512 and D == 512 and FF == 4 * 512
    assert 2 * B * S <= (OV + 1) * P and E <= OV + 1

    x_v = ins["x"].rearrange("b s d -> (b s) d").rearrange("(t p) d -> p t d", p=P)
    out_v = out.rearrange("b s d -> (b s) d").rearrange("(t p) d -> p t d", p=P)

    with ExitStack() as ctx:
        def sb(name, shape, dt=f32, scope=ctx):
            return scope.enter_context(nc.sbuf_tensor(name, shape, dt))

        def sem(name):
            return ctx.enter_context(nc.semaphore(name))

        bank = [ctx.enter_context(nc.psum_tensor(f"bank{i}", [P, 512], f32)) for i in range(8)]

        ident = sb("ident", [P, P])
        xt = sb("xt", [P, NT, D])
        stats = sb("stats", [P, NT, 6])
        mv = sb("mv", [P, NT, 2])
        rstd = sb("rstd", [P, NT])
        mhalf = sb("mhalf", [P, NT])

        xscope = ExitStack()
        pb_tile = sb("pb_tile", [P, NT], f32, xscope)
        avT = sb("avT", [P, KD, B * S], f32, xscope)
        pw_all = sb("pw_all", [P, KD, B, P], f32r, xscope)
        pw = [sb(f"pw{i}", [P, KD, P], f32r, xscope) for i in range(2)]
        pb = sb("pb", [S, B], f32, xscope)
        sc = [sb(f"sc{i}", [S, NKT * P], f32, xscope) for i in range(2)]
        sc_low = [sb(f"sc_low{i}", [S, 512], f32, xscope) for i in range(2)]
        pv_low = sb("pv_low", [S, D], f32, xscope)
        av = sb("av", [S, D], f32, xscope)
        mx4 = sb("mx4", [S, NC], f32, xscope)
        mx = sb("mx", [S, 2], f32, xscope)
        nbias = [sb(f"nbias{i}", [S, 1], f32, xscope) for i in range(2)]
        rsum = [sb(f"rsum{i}", [S, 1], f32, xscope) for i in range(2)]
        rinv = sb("rinv", [S, 1], f32, xscope)
        raw_scope = ExitStack()
        raw = [sb(f"raw{i}", [P, NKT, D], f32, raw_scope) for i in range(2)]
        loop_scope = ExitStack()
        nat_hi = sb("nat_hi", [P, NKT, D], f32r, loop_scope)
        nat_lo = sb("nat_lo", [P, NKT, D], f32r, loop_scope)
        ct_hi = [sb(f"ct_hi{i}", [P, KD, 512], f32r, loop_scope) for i in range(2)]
        ct_lo = [sb(f"ct_lo{i}", [P, KD, 512], f32r, loop_scope) for i in range(2)]
        pT = sb("pT", [P, NKT, P], f32r, loop_scope)
        loop_scope.close()
        pro_scope = ExitStack()
        Wn = sb("Wn", [P, KD, D], f32, pro_scope)
        pn = sb("pn", [P, NT, D], f32, pro_scope)
        b_row = sb("b_row", [P, D], f32, pro_scope)
        pnT_hi = sb("pnT_hi", [P, KD, B * S], f32r, pro_scope)
        pnT_lo = sb("pnT_lo", [P, KD, B * S], f32r, pro_scope)
        W_hi = sb("W_hi", [P, KD, D], f32r, pro_scope)
        W_lo = sb("W_lo", [P, KD, D], f32r, pro_scope)
        pro_scope.close()
        raw_scope.close()
        epi_scope = ExitStack()
        We = sb("We", [P, KD, D], f32, epi_scope)
        b_bc = sb("b_bc", [P, D], f32, epi_scope)
        WT_hi = sb("WT_hi", [P, KD, D], f32r, epi_scope)
        WT_lo = sb("WT_lo", [P, KD, D], f32r, epi_scope)
        sb("last_context", [P, 3, NKT, D], f32, epi_scope)
        avT_hi = sb("avT_hi", [P, KD, B * S], f32r, epi_scope)
        avT_lo = sb("avT_lo", [P, KD, B * S], f32r, epi_scope)
        xo = sb("xo", [P, NT, D], f32, epi_scope)
        epi_scope.close()
        xscope.close()

        xn = sb("xn", [P, NT, D])
        heads = xn[:, :, :].rearrange("p (r a) d -> p r (a d)", r=2)
        w_raw = [sb(f"w_raw{i}", [P, KD, 512]) for i in range(RING)]
        w_hi = [sb(f"w_hi{i}", [P, KD, 512], f32r) for i in range(RING)]
        w_lo = [sb(f"w_lo{i}", [P, KD, 512], f32r) for i in range(RING)]
        zeros = sb("zeros", [P, D])
        ones = sb("ones", [P, P])
        before = sb("before", [P, P])
        e_int = sb("e_int", [P, E], mybir.dt.int32)
        e_idx = sb("e_idx", [P, E])
        upto = sb("upto", [P, E, E])
        w_router = sb("w_router", [P, KD, E])
        layer = ExitStack()
        x1n = sb("x1n", [P, NT, D], f32, layer)
        xT_hi = sb("xT_hi", [P, KD, B * S], f32r, layer)
        xT_lo = sb("xT_lo", [P, KD, B * S], f32r, layer)
        gain = sb("gain", [P, D], f32, layer)
        shift = sb("shift", [P, D], f32, layer)
        b2_bc = sb("b2_bc", [P, D], f32, layer)
        b1_col = sb("b1_col", [P, FF // P], f32, layer)
        late = ExitStack()
        proj2 = sb("proj2", [P, P], f32, late)
        proj2_hi = sb("proj2_hi", [P, P], f32r, late)
        proj2_lo = sb("proj2_lo", [P, P], f32r, late)
        mask = sb("mask", [P, P], f32, late)
        z_hi = [sb(f"z_hi{i}", [P, B * S], f32r, late) for i in range(2)]
        z_lo = [sb(f"z_lo{i}", [P, B * S], f32r, late) for i in range(2)]
        neg = [sb(f"neg{i}", [P, B * S], f32, late) for i in range(2)]
        phi = [sb(f"phi_{n}", [P, H // 2, B * S], f32, late) for n in "qk"]
        v1 = sb("v1", [P, NT, H, DH + 1], f32, late)
        at = [sb(f"at{i}", [P, 4, P], f32, late) for i in range(2)]
        oT_hi = sb("oT_hi", [P, HD // P, P], f32r, late)
        oT_lo = sb("oT_lo", [P, HD // P, P], f32r, late)
        den = sb("den", [P, 2, 4], f32, late)
        late.close()
        ffn = ExitStack()
        gl = [sb(f"gl{i}", [P, B * S], f32, ffn) for i in range(2)]
        gl_hi = [sb(f"gl_hi{i}", [P, B * S], f32r, ffn) for i in range(2)]
        gl_lo = [sb(f"gl_lo{i}", [P, B * S], f32r, ffn) for i in range(2)]
        ffn.close()
        layer.close()

        moe = ExitStack()
        xT32 = sb("xT32", [P, KD, B * S], f32, moe)
        logits = sb("logits", [P, NT, E], f32, moe)
        pref = sb("pref", [P, E], f32, moe)
        pick = [sb(f"pick{k}", [P, NT, E], f32, moe) for k in range(2)]
        scr = sb("scr", [P, NT, E], f32, moe)
        scr8 = sb("scr8", [P, E, E], f32, moe)
        best = [sb(f"best{k}", [P, NT], f32, moe) for k in range(2)]
        top = sb("top", [P, NT], f32, moe)
        chosen = sb("chosen", [P, NT + 1, E], f32, moe)
        rank = sb("rank", [P, NT, E], f32, moe)
        count = sb("count", [P, E], f32, moe)
        extra = sb("extra", [P, E], f32, moe)
        upto_extra = sb("upto_extra", [P, E], f32, moe)
        first_block = sb("first_block", [P, E], f32, moe)
        slotf = [sb(f"slotf{k}", [P, NT], f32, moe) for k in range(2)]
        slot_of = [sb(f"slot_of{k}", [P, NT], mybir.dt.uint32, moe) for k in range(2)]
        blocks = sb("blocks", [P, 2, E], mybir.dt.int32, moe)
        gate = [sb(f"gate{k}", [P, NT], f32, moe) for k in range(2)]
        gap = sb("gap", [P, NT], f32, moe)
        gsum = sb("gsum", [P, NT], f32, moe)
        xg = sb("xg", [P, D], f32, moe)
        xgT_hi = sb("xgT_hi", [P, KD, P], f32r, moe)
        xgT_lo = sb("xgT_lo", [P, KD, P], f32r, moe)
        sg = [sb(f"sg{i}", [P, 512], f32, moe) for i in range(2)]
        hm = [sb(f"hm{i}", [P, 512], f32, moe) for i in range(2)]
        hmT_hi = [sb(f"hmT_hi{i}", [P, 4, P], f32r, moe) for i in range(2)]
        hmT_lo = [sb(f"hmT_lo{i}", [P, 4, P], f32r, moe) for i in range(2)]
        yb = sb("yb", [P, D], f32, moe)
        units = ExitStack()
        e_raw = w_raw + [sb(f"e_raw{j}", [P, KD, 512], f32, units) for j in range(RING, 6)]
        e_hi = w_hi + [sb(f"e_hi{j}", [P, KD, 512], f32r, units) for j in range(RING, 6)]
        e_lo = w_lo + [sb(f"e_lo{j}", [P, KD, 512], f32r, units) for j in range(RING, 6)]
        units.close()
        yt = [sb(f"yt{k}", [P, NT, D], f32, moe) for k in range(2)]
        moe.close()
        xs = nc.dram_tensor("slots_x", [(NB + 1) * P, D], f32).ap()
        ys = nc.dram_tensor("slots_y", [NB * P, D], f32).ap()

        x_loaded = [sem(f"x_loaded{t}") for t in range(NT)]
        W_loaded, b_loaded = sem("W_loaded"), sem("b_loaded")
        ctx_loaded = [[sem(f"ctx_loaded{p}_{c}") for c in range(NC)] for p in range(2)]
        raw_zeroed, sc_zeroed = sem("raw_zeroed"), sem("sc_zeroed")
        const_ready = sem("const_ready")
        dve_step, pool_step = sem("dve_step"), sem("pool_step")
        var_ready, rstd_ready, pn_ready = sem("var_ready"), sem("rstd_ready"), sem("pn_ready")
        pnT_done, pnT_hi_ready, pnT_lo_ready = sem("pnT_done"), sem("pnT_hi_ready"), sem("pnT_lo_ready")
        W_hi_ready, W_lo_ready = sem("W_hi_ready"), sem("W_lo_ready")
        pwT_done, pw_hi_ready, pw_lo_ready, pw_ready = sem("pwT_done"), sem("pw_hi_ready"), sem("pw_lo_ready"), sem("pw_ready")
        pb_done, pb_ready = sem("pb_done"), sem("pb_ready")
        t_done, t_hi, t_lo = sem("t_done"), sem("t_hi"), sem("t_lo")
        qk_done, s_low, s_ready = sem("qk_done"), sem("s_low"), sem("s_ready")
        max_ready, exp_done, rinv_ready = sem("max_ready"), sem("exp_done"), sem("rinv_ready")
        pt_done, pt_hi, pt_lo = sem("pt_done"), sem("pt_hi"), sem("pt_lo")
        nat_hi_ready, nat_hi_dve = sem("nat_hi_ready"), sem("nat_hi_dve")
        nat_lo_ready = [sem(f"nat_lo_ready{c}") for c in range(NC)]
        pv_done, pv_low_ready, av_sum, av_ready = sem("pv_done"), sem("pv_low_ready"), sem("av_sum"), sem("av_ready")
        avt_done, avt_ready = sem("avt_done"), sem("avt_ready")
        WT_done, WT_hi_ready, WT_lo_ready = sem("WT_done"), sem("WT_hi_ready"), sem("WT_lo_ready")
        avT_hi_ready, avT_lo_ready, xo_done, x1_ready = sem("avT_hi_ready"), sem("avT_lo_ready"), sem("xo_done"), sem("x1_ready")
        stored = sem("stored")
        zeros_ready, slots_zeroed, router_loaded, index_ready, order_ready = sem("zeros_ready"), sem("slots_zeroed"), sem("router_loaded"), sem("index_ready"), sem("order_ready")
        xT32_ready, logits_done, chosen_ready, rank_done = sem("xT32_ready"), sem("logits_done"), sem("chosen_ready"), sem("rank_done")
        gap_ready, gap_exp, slots_ready, scattered = sem("gap_ready"), sem("gap_exp"), sem("slots_ready"), sem("scattered")
        xo_ready = sem("xo_ready")
        last_dn = sem("last_dn")
        xg_loaded, xgT_done, xgT_hi_ready, xgT_lo_ready = sem("xg_loaded"), sem("xgT_done"), sem("xgT_hi_ready"), sem("xgT_lo_ready")
        unit_done = [sem(f"unit_done{j}") for j in range(6)]
        last_y_stored = sem("last_y_stored")
        silu_ready, hm_ready, hmT_done = sem("silu_ready"), sem("hm_ready"), sem("hmT_done")
        hmT_hi_ready, hmT_lo_ready, y_ready, y_stored = sem("hmT_hi_ready"), sem("hmT_lo_ready"), sem("y_ready"), sem("y_stored")
        gathered = [sem(f"gathered{t}") for t in range(NT)]
        w_loaded = [sem(f"w_loaded{i}") for i in range(RING)]
        w_hi_ready = [sem(f"w_hi_ready{i}") for i in range(RING)]
        w_lo_ready = [sem(f"w_lo_ready{i}") for i in range(RING)]
        e_loaded = w_loaded + [sem(f"e_loaded{j}") for j in range(RING, 6)]
        e_hi_ready = w_hi_ready + [sem(f"e_hi_ready{j}") for j in range(RING, 6)]
        e_lo_ready = w_lo_ready + [sem(f"e_lo_ready{j}") for j in range(RING, 6)]
        b1_loaded = sem("b1_loaded")
        vec_loaded, vec2_loaded = sem("vec_loaded"), sem("vec2_loaded")
        proj_loaded, proj_zero, proj_hi_ready, proj_lo_ready, mask_ready = sem("proj_loaded"), sem("proj_zero"), sem("proj_hi_ready"), sem("proj_lo_ready"), sem("mask_ready")
        xn_ready, xT_done, xT_hi_ready, xT_lo_ready = sem("xn_ready"), sem("xT_done"), sem("xT_hi_ready"), sem("xT_lo_ready")
        z_done, z_hi_ready, z_lo_ready = sem("z_done"), sem("z_hi_ready"), sem("z_lo_ready")
        f_done, neg_ready, e_ready, phi_ready = sem("f_done"), sem("neg_ready"), sem("e_ready"), sem("phi_ready")
        v_done, v_ready, v_one = sem("v_done"), sem("v_ready"), sem("v_one")
        a_done, a_ready, o_done, o_ready = sem("a_done"), sem("a_ready"), sem("o_done"), sem("o_ready")
        oT_done, oT_hi_ready, oT_lo_ready = sem("oT_done"), sem("oT_hi_ready"), sem("oT_lo_ready")
        ao_done, xa_ready = sem("ao_done"), sem("xa_ready")
        up_done, gelu_ready, gl_hi_ready, gl_lo_ready, dn_done, x2_ready = sem("up_done"), sem("gelu_ready"), sem("gl_hi_ready"), sem("gl_lo_ready"), sem("dn_done"), sem("x2_ready")

        def unit(name, half, rows=False):
            w = ins[name].rearrange("(k p) n -> p k n", p=P)
            return w[:, KD * half:KD * (half + 1), :] if rows else w[:, :, 512 * half:512 * (half + 1)]

        UNITS = [unit(f"L0_attn_{n}", half) for n in ("wq", "wk", "wv") for half in range(2)]
        UNITS += [unit("L0_attn_wo", half, rows=True) for half in range(2)]
        for i in range(FF // 512):
            UNITS += [unit("L0_attn_w1", i), unit("L0_attn_w2", i, rows=True)]
        NU = len(UNITS)
        USED = [(z_done, 4 * (u + 1)) for u in range(4)] + [(v_done, NT), (v_done, 2 * NT), (ao_done, NT), (ao_done, NT)]
        for i in range(FF // 512):
            USED += [(up_done, 4 * (i + 1)), (dn_done, 4 * (i + 1))]

        def upper(u):
            return w_hi_ready[u % RING], u // RING + 1

        def lower(u):
            return w_lo_ready[u % RING], u // RING + 1

        POOL_WEIGHTS = range(1, 9)

        EU = 6
        POOL_UNITS = (4, 5)

        def expert_unit(e, j):
            w = ins["L0_ffn_" + ("w0", "w1", "w0", "w1", "wo", "wo")[j]]
            w = w[bass.ds(e, 1), :, :].rearrange("o (k p) n -> p (o k) n", p=P)
            return w[:, KD * (j - 4):KD * (j - 3), :] if j >= 4 else w[:, :, 512 * (j // 2):512 * (j // 2 + 1)]

        def turn_of(e, j):
            before = len(range(j, NU, RING)) if j < RING else 0
            return before + e + 1

        def expert_blocks(engine, e):
            most = NB - 1 if isinstance(e, int) else NB - 2
            return [engine.value_load(blocks[0:1, i, bass.ds(e, 1)], min_val=0, max_val=most) for i in range(2)]

        TB = [bank[0], bank[1], bank[2]]
        SB = [bank[3], bank[4]]
        PB = [bank[5], bank[6]]
        VB = bank[7]
        G = FULL + 1
        DVE_TILES = (8, 10)

        def act_tiles(last):
            return last - max(0, min(last, DVE_TILES[1]) - DVE_TILES[0])

        LO_STEPS = (2, 1, 1, 1)
        PT_SPLIT = [(0, 8), (8, NKT)]

        def groups(c):
            if c < NC - 1:
                return [(CH * c + k, [k]) for k in range(KD)]
            return [(G - 1, list(range(KD)))]

        def width(c):
            return CH * P if c < NC - 1 else REM

        def t_bank(g):
            return TB[g % len(TB)]

        def t_before(b, g):
            if g >= len(TB):
                return G * b + g - len(TB) + 1
            if isinstance(b, int) and b == 0:
                return None
            last = max(h for h in range(G) if h % len(TB) == g)
            return G * (b - 1) + last + 1

        block = ctx.enter_context(nc.Block())

        @block.sync
        def _(sp):
            for t in range(NT):
                sp.dma_start(xt[:, t, :], x_v[:, t, :]).then_inc(x_loaded[t], 16)
            sp.dma_start(Wn[:, :, :], ins["L0_xattn_W"].rearrange("(k p) h -> p k h", p=P)).then_inc(W_loaded, 16)
            sp.dma_start(b_row[:, :], ins["L0_xattn_b"].partition_broadcast(P)).then_inc(b_loaded, 16)

            def load_ctx(b, c):
                src = ins["ctx_1024"][b]
                if c < NC - 1:
                    src = src[0:FULL * P, :].rearrange("(p j) d -> p j d", j=FULL)[:, CH * c:CH * (c + 1), :]
                    dst = raw[b % 2][:, CH * c:CH * (c + 1), :]
                else:
                    src, dst = src[FULL * P:KEYS, :], raw[b % 2][0:REM, FULL, :]
                sp.dma_start(dst, src).then_inc(ctx_loaded[b % 2][c], 16)

            sp.wait_ge(raw_zeroed, 2)
            for b in range(B):
                for c in range(NC):
                    if b >= 2:
                        sp.wait_ge(t_done, G * (b - 2) + groups(c)[-1][0] + 1)
                        sp.wait_ge(nat_lo_ready[c], LO_STEPS[c] * (b - 1))
                    load_ctx(b, c)
            sp.wait_ge(t_done, G * (B - 1))
            for c in range(NC):
                sp.wait_ge(nat_lo_ready[c], LO_STEPS[c] * (B - 1))
            sp.dma_start(We[:, :, :], ins["L0_xattn_W"].rearrange("(k p) h -> p k h", p=P)).then_inc(W_loaded, 16)
            sp.dma_start(b_bc[:, :], ins["L0_xattn_b"].partition_broadcast(P)).then_inc(b_loaded, 16)
            sp.wait_ge(x1_ready, NT)
            for name, dst in (("g1", gain), ("beta1", shift), ("b2", b2_bc)):
                sp.dma_start(dst[:, :], ins[f"L0_attn_{name}"].partition_broadcast(P)).then_inc(vec_loaded, 16)
            for u in range(NU):
                if u == 8:
                    sp.wait_ge(xT_lo_ready, KD)
                    for name, dst in (("g2", gain), ("beta2", shift)):
                        sp.dma_start(dst[:, :], ins[f"L0_attn_{name}"].partition_broadcast(P)).then_inc(vec2_loaded, 16)
                if u >= RING:
                    sp.wait_ge(*lower(u - RING))
                sp.dma_start(w_raw[u % RING][:, :, :], UNITS[u]).then_inc(w_loaded[u % RING], 16)
                if u == 0:
                    with nc.allow_non_contiguous_dma(reason="bias values by partition, once"):
                        sp.dma_start(b1_col[:, :], ins["L0_attn_b1"].rearrange("(f p) -> p f", p=P)).then_inc(b1_loaded, 16)
                    sp.wait_ge(proj_zero, 1)
                    for s in range(2):
                        sp.dma_start(proj2[DH * s:DH * (s + 1), DH * s:DH * (s + 1)], ins["L0_attn_proj"]).then_inc(proj_loaded, 16)
            sp.dma_start(w_router[:, :, :], ins["L0_ffn_w_router"].rearrange("(k p) e -> p k e", p=P)).then_inc(router_loaded, 16)
            sp.wait_ge(zeros_ready, 1)
            sp.dma_start(xs.rearrange("(n p) d -> p n d", p=P), zeros[:, :].unsqueeze(1).to_broadcast([P, NB + 1, D])).then_inc(slots_zeroed, 16)
            sp.dma_start(ys[E * P:NB * P, :].rearrange("(n p) d -> p n d", p=P), zeros[:, :].unsqueeze(1).to_broadcast([P, OV, D])).then_inc(slots_zeroed, 16)

            def load_expert(e):
                for j in range(EU):
                    if not (isinstance(e, int) and e == 0 and j >= RING):
                        sp.wait_ge(e_lo_ready[j], turn_of(e, j) - 1)
                    sp.dma_start(e_raw[j][:, :, :], expert_unit(e, j)).then_inc(e_loaded[j], 16)
                    if isinstance(e, int) and j == RING - 1:
                        if e == 0:
                            sp.wait_ge(x2_ready, NT)
                        else:
                            sp.wait_ge(xg_loaded, 16)

            load_expert(0)
            load_expert(1)
            with sp.Fori(2, E) as e:
                load_expert(e)
            for t in range(NT):
                sp.wait_ge(xo_ready, t + 1)
                sp.dma_start(out_v[:, t, :], xt[:, t, :]).then_inc(stored, 16)
            sp.wait_ge(stored, 16 * NT)

        @block.gpsimd
        def _(pool):
            steps = [0]

            def link(ins_):
                steps[0] += 1
                ins_.then_inc(pool_step, 1)
                pool.wait_ge(pool_step, steps[0])

            link(nc.gpsimd.memset(ident[:, :], 0.0))
            nc.gpsimd.affine_select(out=ident[:, :], in_=ident[:, :], compare_op=ALU.not_equal, fill=1.0, base=0,
                                    pattern=[[-1, P]], channel_multiplier=1).then_inc(const_ready, 1)
            link(nc.gpsimd.memset(mhalf[:, :], -0.5))
            pool.wait_ge(var_ready, 1)
            nc.gpsimd.tensor_tensor(rstd[:, :], rstd[:, :], mhalf[:, :], ALU.pow).then_inc(rstd_ready, 1)

            def take_pw(b, par):
                if not (isinstance(b, int) and b < 2):
                    pool.wait_ge(qk_done, NC * (b - 1))
                nc.gpsimd.tensor_copy(pw[par][:, :, :], pw_all[:, :, bass.ds(b, 1), :].rearrange("p k o m -> p k (o m)").bitcast(f32))\
                    .then_inc(pw_ready, 1)

            def split_ctx(b, par, c):
                first, last = CH * c, min(CH * (c + 1), NKT)
                pool.wait_ge(nat_hi_ready, act_tiles(NKT) * b + act_tiles(last))
                if c == DVE_TILES[0] // CH:
                    pool.wait_ge(nat_hi_dve, b + 1)
                nc.gpsimd.tensor_tensor(nat_lo[:, first:last, :], raw[par][:, first:last, :],
                                        nat_hi[:, first:last, :].bitcast(f32), ALU.subtract).then_inc(nat_lo_ready[c], 1)

            def split_half(b, par):
                pool.wait_ge(nat_hi_ready, act_tiles(NKT) * b + CH)
                nc.gpsimd.tensor_tensor(nat_lo[:, CH // 2:CH, :], raw[par][:, CH // 2:CH, :],
                                        nat_hi[:, CH // 2:CH, :].bitcast(f32), ALU.subtract).then_inc(nat_lo_ready[0], 1)

            def stage(b, par, queries=True, following=True):
                split_ctx(b, par, 2)
                split_ctx(b, par, 3)
                if following:
                    split_half(b + 1, 1 - par)
                if queries:
                    take_pw(b + 2, par)
                if following:
                    split_ctx(b + 1, 1 - par, 1)

            pool.wait_ge(pw_hi_ready, KD)
            pool.wait_ge(pw_lo_ready, KD)
            take_pw(0, 0)
            take_pw(1, 1)
            split_half(0, 0)
            split_ctx(0, 0, 1)
            stage(0, 0)
            with pool.Fori(0, B // 2 - 2) as i:
                stage(2 * i + 1, 1)
                stage(2 * i + 2, 0)
            stage(B - 3, 1)
            stage(B - 2, 0, queries=False)
            stage(B - 1, 1, queries=False, following=False)

            def root(count, t):
                pool.wait_ge(var_ready, count)
                nc.gpsimd.tensor_tensor(rstd[:, t:t + 1], rstd[:, t:t + 1], mhalf[:, t:t + 1], ALU.pow).then_inc(rstd_ready, 1)

            for n in range(2):
                for t in range(NT):
                    root(2 + n * NT + t, t)
            pool.wait_ge(x1_ready, NT)
            link(nc.gpsimd.memset(mask[:, :], 1.0))
            link(nc.gpsimd.affine_select(out=mask[:, :], in_=mask[:, :], compare_op=ALU.is_ge, fill=0.0, base=0,
                                         pattern=[[1, P]], channel_multiplier=-1))
            nc.gpsimd.affine_select(out=mask[:, S:P], in_=mask[:, S:P], compare_op=ALU.is_ge, fill=0.0, base=-S,
                                    pattern=[[0, P - S]], channel_multiplier=1).then_inc(mask_ready, 1)
            nc.gpsimd.iota(e_int[:, :], pattern=[[1, E]], base=0, channel_multiplier=0).then_inc(index_ready, 1)
            link(nc.gpsimd.memset(ones[:, :], 1.0))
            nc.gpsimd.affine_select(out=before[:, :], in_=ones[:, :], compare_op=ALU.is_gt, fill=0.0, base=0,
                                    pattern=[[1, P]], channel_multiplier=-1).then_inc(order_ready, 1)
            nc.gpsimd.affine_select(out=upto[:, :, :], in_=ones[:, 0:E * E].rearrange("p (e f) -> p e f", e=E), compare_op=ALU.is_ge,
                                    fill=0.0, base=0, pattern=[[1, E], [-1, E]], channel_multiplier=0).then_inc(order_ready, 1)
            for u in POOL_WEIGHTS:
                pool.wait_ge(*upper(u))
                nc.gpsimd.tensor_tensor(w_lo[u % RING][:, :, :], w_raw[u % RING][:, :, :], w_hi[u % RING][:, :, :].bitcast(f32),
                                        ALU.subtract).then_inc(w_lo_ready[u % RING], 1)
            for t in range(NT):
                root(2 * NT + t + 2, t)
            pool.wait_ge(var_ready, 3 * NT + 2)
            nc.gpsimd.tensor_tensor(rstd[:, :], rstd[:, :], mhalf[:, :], ALU.pow).then_inc(rstd_ready, 1)

            def split_w(e, j):
                pool.wait_ge(e_hi_ready[j], turn_of(e, j))
                nc.gpsimd.tensor_tensor(e_lo[j][:, :, :], e_raw[j][:, :, :], e_hi[j][:, :, :].bitcast(f32),
                                        ALU.subtract).then_inc(e_lo_ready[j], 1)

            for j in POOL_UNITS:
                split_w(0, j)
            pool.wait_ge(slots_ready, 2)
            pool.wait_ge(slots_zeroed, 32)
            for k in range(2):
                for t in range(NT):
                    nc.gpsimd.indirect_dma_start(xs[:, :], bass.IndirectOffsetOnAxis(ap=slot_of[k][:, t:t + 1], axis=0),
                                                 xn[:, t, :], None).then_inc(scattered, 16)
            with pool.Fori(1, E) as e:
                for j in POOL_UNITS:
                    split_w(e, j)
            pool.wait_ge(last_y_stored, 16)
            for t in range(NT):
                for k in range(2):
                    nc.gpsimd.indirect_dma_start(yt[k][:, t, :], None, ys[:, :],
                                                 bass.IndirectOffsetOnAxis(ap=slot_of[k][:, t:t + 1], axis=0)).then_inc(gathered[t], 16)

        @block.scalar
        def _(act):
            act.wait_ge(W_loaded, 16)
            nc.scalar.activation(W_hi[:, :, :], Wn[:, :, :], ACT.Copy).then_inc(W_hi_ready, 1)
            for k in range(KD):
                act.wait_ge(pnT_done, k + 1)
                nc.scalar.activation(pnT_hi[:, k, :], bank[k][:, :], ACT.Copy).then_inc(pnT_hi_ready, 1)
            act.wait_ge(pb_done, 1)
            for half in range(2):
                nc.scalar.activation(pb[:, :].rearrange("p (t h) -> p t h", h=2)[:, :, half], pb_tile[half * S:(half + 1) * S, :],
                                     ACT.Copy).then_inc(pb_ready, 1)
            for m in range(KD):
                act.wait_ge(pwT_done, m + 1)
                nc.scalar.activation(pw_all[:, m, :, 0:S], bank[m][:, :].rearrange("p (b s) -> p b s", b=B),
                                     ACT.Copy).then_inc(pw_hi_ready, 1)

            def evacuate(b, c, between=()):
                if c >= 2:
                    act.wait_ge(qk_done, NC * b + c - 1)
                elif not (isinstance(b, int) and b == 0):
                    act.wait_ge(qk_done, NC * (b - 1) + NC - 2 + c + 1)
                for (g, ks), after in zip(groups(c), tuple(between) + (None,) * KD):
                    act.wait_ge(t_done, G * b + g + 1)
                    n = width(c) if len(ks) == 1 else REMP
                    nc.scalar.activation(ct_hi[c % 2][:, ks[0]:ks[-1] + 1, 0:n],
                                         t_bank(g)[:, 0:len(ks) * 512 // len(ks)].rearrange("p (k n) -> p k n", k=len(ks))[:, :, 0:n],
                                         ACT.Copy).then_inc(t_hi, 1)
                    if after:
                        after()

            def low_scores(b, c):
                act.wait_ge(qk_done, NC * b + c + 1)
                if not (isinstance(b, int) and b == 0 and c < 2):
                    act.wait_ge(s_ready, NC * b + c - 1)
                nc.scalar.activation(sc_low[c % 2][:, 0:width(c)], SB[c % 2][S:2 * S, 0:width(c)], ACT.Copy).then_inc(s_low, 1)

            def take_av(b):
                act.wait_ge(avt_done, b + 1)
                nc.scalar.activation(avT[:, :, bass.ds(S * b, S)], VB[:, 0:KD * S].rearrange("p (k s) -> p k s", k=KD),
                                     ACT.Copy).then_inc(avt_ready, 1)

            def prob_parts(b):
                for h, (t0, t1) in enumerate(PT_SPLIT):
                    act.wait_ge(pt_done, 2 * b + h + 1)
                    if not (isinstance(b, int) and b == 0):
                        act.wait_ge(pv_done, NC * b)
                    nc.scalar.activation(pT[:, t0:t1, 0:S], PB[h][:, 0:(t1 - t0) * S].rearrange("p (j s) -> p j s", s=S),
                                         ACT.Copy).then_inc(pt_hi, 1)

            def exps(b, par):
                act.wait_ge(max_ready, b + 1)
                if not (isinstance(b, int) and b < 2):
                    act.wait_ge(rinv_ready, b - 1)
                nc.scalar.activation(sc[par][0:S, 0:KEYS], sc[par][0:S, 0:KEYS], ACT.Exp, bias=nbias[par][:, :],
                                     accum_out=rsum[par][:, :]).then_inc(exp_done, 1)

            def split_tiles(b, par, tiles):
                for j in tiles:
                    if j % CH == 0 or j == DVE_TILES[1]:
                        c = j // CH
                        act.wait_ge(ctx_loaded[par][c], 16 * (b // 2 + 1) if isinstance(b, int) else 16 * ((b - par) // 2 + 1))
                        if not (isinstance(b, int) and b == 0):
                            act.wait_ge(pv_done, NC * (b - 1) + c + 1)
                    nc.scalar.activation(nat_hi[:, j, :], raw[par][:, j, :], ACT.Copy).then_inc(nat_hi_ready, 1)

            def take_low_values(b):
                act.wait_ge(pv_done, NC * (b + 1))
                nc.scalar.activation(pv_low[:, :], VB[S:2 * S, :], ACT.Copy).then_inc(pv_low_ready, 1)

            def scale_values(b):
                act.wait_ge(rinv_ready, b + 1)
                act.wait_ge(av_sum, b + 1)
                nc.scalar.activation(av[0:S, :], pv_low[:, :], ACT.Copy, scale=rinv[:, :]).then_inc(av_ready, 1)

            def stage(b, par, scores=True, values=True, earlier=True, ahead=True):
                n, npar = b + 1, 1 - par

                def tiles(*js):
                    if values:
                        split_tiles(b, par, js)

                def parts():
                    if values:
                        prob_parts(b)
                    if earlier:
                        scale_values(b - 1)
                    tiles(6)

                if earlier:
                    take_low_values(b - 1)
                if scores:
                    evacuate(n, 1, (parts, None, lambda: tiles(7)))
                    low_scores(n, 0)
                    evacuate(n, 2, ((lambda: take_av(b - 1)) if earlier else None,))
                    low_scores(n, 1)
                else:
                    parts()
                    tiles(7)
                    take_av(b - 1)
                tiles(10, 11)
                if scores:
                    evacuate(n, 3)
                tiles(12)
                if scores:
                    split_tiles(n, npar, range(0, 2))
                    low_scores(n, 2)
                    split_tiles(n, npar, range(2, 5))
                    low_scores(n, 3)
                    exp_step = lambda: exps(n, npar)
                    if ahead:
                        evacuate(n + 1, 0, (None, None, exp_step))
                    else:
                        exp_step()
                    split_tiles(n, npar, range(5, 6))

            evacuate(0, 0)
            stage(-1, 1, values=False, earlier=False)
            stage(0, 0, earlier=False)
            with act.Fori(0, B // 2 - 2) as i:
                stage(2 * i + 1, 1)
                stage(2 * i + 2, 0)
            stage(B - 3, 1)
            stage(B - 2, 0, ahead=False)
            stage(B - 1, 1, scores=False)
            def upper_vectors(first, last):
                act.wait_ge(avt_ready, 2 * last)
                nc.scalar.activation(avT_hi[:, :, first * P:last * P], avT[:, :, first * P:last * P], ACT.Copy).then_inc(avT_hi_ready, 1)

            upper_vectors(0, NT - 1)
            for k in range(KD):
                act.wait_ge(WT_done, k + 1)
                nc.scalar.activation(WT_hi[:, k, :], bank[k][:, :], ACT.Copy).then_inc(WT_hi_ready, 1)
            take_low_values(B - 1)
            scale_values(B - 1)
            take_av(B - 1)
            upper_vectors(NT - 1, NT)

            def split_w(u):
                act.wait_ge(w_loaded[u % RING], 16 * (u // RING + 1))
                if u >= RING:
                    act.wait_ge(*USED[u - RING])
                nc.scalar.activation(w_hi[u % RING][:, :, :], w_raw[u % RING][:, :, :], ACT.Copy).then_inc(w_hi_ready[u % RING], 1)

            def upper_xT(n):
                for k in range(KD):
                    act.wait_ge(xT_done, KD * n + k + 1)
                    nc.scalar.activation(xT_hi[:, k, :], bank[k][:, :], ACT.Copy).then_inc(xT_hi_ready, 1)

            split_w(0)
            act.wait_ge(proj_loaded, 32)
            nc.scalar.activation(proj2_hi[:, :], proj2[:, :], ACT.Copy).then_inc(proj_hi_ready, 1)
            upper_xT(0)
            split_w(1)
            split_w(2)

            def upper_z(n):
                act.wait_ge(z_done, n + 1)
                if n >= 2:
                    act.wait_ge(f_done, n - 1)
                nc.scalar.activation(z_hi[n % 2][:, :], bank[n % 2][:, :], ACT.Copy).then_inc(z_hi_ready, 1)

            def exp_neg(n):
                act.wait_ge(neg_ready, n + 1)
                nc.scalar.activation(neg[n % 2][:, :], neg[n % 2][:, :], ACT.Exp).then_inc(e_ready, 1)

            for n in range(H):
                upper_z(n)
                if n >= 1:
                    exp_neg(n - 1)
                if n % 4 == 0 and n // 4 + 2 >= RING:
                    split_w(n // 4 + 2)
            exp_neg(H - 1)
            for u in range(2):
                for t in range(NT):
                    n = NT * u + t
                    act.wait_ge(v_done, n + 1)
                    nc.scalar.activation(v1[:, t, 8 * u:8 * (u + 1), 0:DH], bank[4 + n % 2][:, :].rearrange("p (h d) -> p h d", d=DH),
                                         ACT.Copy).then_inc(v_ready, 1)
                split_w(6 + u)
            for t in range(NT):
                for half in range(2):
                    act.wait_ge(oT_done, 2 * t + half + 1)
                    if t >= 1:
                        act.wait_ge(ao_done, t)
                    nc.scalar.activation(oT_hi[:, 4 * half:4 * (half + 1), :], bank[4 + half][:, :].rearrange("p (k n) -> p k n", n=P),
                                         ACT.Copy).then_inc(oT_hi_ready, 1)
                if t == 0:
                    split_w(8)
            split_w(9)
            upper_xT(1)
            split_w(10)
            act.wait_ge(b1_loaded, 16)
            for n in range(FF // P):
                act.wait_ge(up_done, n + 1)
                if n >= 2:
                    act.wait_ge(gl_lo_ready, n - 1)
                nc.scalar.activation(gl[n % 2][:, :], bank[n % 2][:, :], ACT.Gelu, bias=b1_col[:, n:n + 1]).then_inc(gelu_ready, 1)
                if n % 4 == 3 and n < FF // P - 1:
                    split_w(11 + 2 * (n // 4))
                if n % 4 == 0 and 4 <= n < FF // P - 4:
                    split_w(10 + n // 2)

            def split_e(e, j, wait):
                act.wait_ge(e_loaded[j], 16 * turn_of(e, j))
                act.wait_ge(*wait)
                nc.scalar.activation(e_hi[j][:, :, :], e_raw[j][:, :, :], ACT.Copy).then_inc(e_hi_ready[j], 1)

            for j in range(RING):
                split_e(0, j, USED[max(u for u in range(NU) if u % RING == j)])
            for k in range(KD):
                act.wait_ge(xT_done, 2 * KD + k + 1)
                nc.scalar.activation(xT32[:, k, :], bank[k][:, :], ACT.Copy).then_inc(xT32_ready, 1)
            for j in range(RING, EU):
                split_e(0, j, (x2_ready, NT))
            act.wait_ge(gap_ready, 1)
            nc.scalar.activation(gsum[:, :], gap[:, :], ACT.Exp).then_inc(gap_exp, 1)

            def load_rows(b):
                nc.scalar.dma_start(xg[:, :], xs[bass.ds(b * P, P), :]).then_inc(xg_loaded, 16)

            def upper_rows(b):
                act.wait_ge(xgT_done, b + 1)
                nc.scalar.activation(xgT_hi[:, :, :], bank[7][:, :].rearrange("p (k n) -> p k n", n=P), ACT.Copy).then_inc(xgT_hi_ready, 1)

            def silu(b, half):
                act.wait_ge(unit_done[2 * half], b + 1)
                nc.scalar.activation(sg[half][:, :], bank[2 * half][:, :], ACT.Silu).then_inc(silu_ready, 1)

            def upper_hidden(b, half):
                act.wait_ge(hmT_done, 2 * b + half + 1)
                nc.scalar.activation(hmT_hi[half][:, :, :], bank[4 + half][:, :].rearrange("p (k n) -> p k n", n=P),
                                     ACT.Copy).then_inc(hmT_hi_ready, 1)

            def expert_block(b, e, again=False, last=False):
                def split(j):
                    if not again and not last:
                        split_e(e + 1, j, (unit_done[j], b + 1))

                split(0)
                silu(b, 1)
                upper_hidden(b, 0)
                split(1)
                if not last:
                    upper_rows(b + 1)
                    load_rows(b + 2)
                split(2)
                upper_hidden(b, 1)
                split(3)
                split(4)
                if not last:
                    silu(b + 1, 0)
                act.wait_ge(unit_done[5], b + 1)
                act.wait_ge(y_stored, 16 * b + 1)
                nc.scalar.activation(yb[:, :], bank[6][:, :], ACT.Copy).then_inc(y_ready, 1)
                split(5)
                act.wait_ge(y_ready, b + 2)
                nc.scalar.dma_start(ys[bass.ds(b * P, P), :], yb[:, :]).then_inc(last_y_stored if last else y_stored, 16)

            act.wait_ge(slots_ready, 4)
            act.wait_ge(scattered, 16 * 2 * NT)
            load_rows(0)
            upper_rows(0)
            load_rows(1)
            silu(0, 0)
            with act.Fori(0, E - 1) as e:
                first_b, last_b = expert_blocks(act, e)
                with act.If(first_b < last_b):
                    with act.Fori(first_b, last_b) as b:
                        expert_block(b, e, again=True)
                expert_block(last_b, e)
            first_b, last_b = expert_blocks(act, E - 1)
            with act.If(first_b < last_b):
                with act.Fori(first_b, last_b) as b:
                    expert_block(b, E - 1, again=True)
            expert_block(last_b, E - 1, last=True)

        @block.vector
        def _(dve):
            steps = [0]

            def link(ins_):
                steps[0] += 1
                ins_.then_inc(dve_step, 1)
                dve.wait_ge(dve_step, steps[0])

            for par in range(2):
                nc.vector.memset(raw[par][64:P, FULL, :], 0.0).then_inc(raw_zeroed, 1)
                nc.vector.memset(sc[par][0:S, KEYS:NKT * P], 0.0).then_inc(sc_zeroed, 1)
            for t in range(NT):
                dve.wait_ge(x_loaded[t], 16)
                last = nc.vector.bn_stats(stats[:, t, :], xt[:, t, :])
            link(last)
            for t in range(NT):
                last = nc.vector.bn_aggr(mv[:, t, :], stats[:, t, :])
            link(last)
            nc.vector.tensor_scalar(rstd[:, :], mv[:, :, 1], EPS, None, ALU.add).then_inc(var_ready, 1)
            dve.wait_ge(rstd_ready, 1)
            for t in range(NT):
                nc.vector.tensor_scalar(pn[:, t, :], xt[:, t, :], mv[:, t, 0:1], rstd[:, t:t + 1],
                                        ALU.subtract, ALU.mult).then_inc(pn_ready, 1)
            dve.wait_ge(W_hi_ready, 1)
            nc.vector.tensor_tensor(W_lo[:, :, :], Wn[:, :, :], W_hi[:, :, :].bitcast(f32), ALU.subtract).then_inc(W_lo_ready, 1)
            for k in range(KD):
                dve.wait_ge(pnT_hi_ready, k + 1)
                nc.vector.tensor_tensor(pnT_lo[:, k, :], bank[k][:, :], pnT_hi[:, k, :].bitcast(f32), ALU.subtract).then_inc(pnT_lo_ready, 1)
            dve.wait_ge(b_loaded, 16)
            link(nc.vector.tensor_tensor(pn[:, :, :], pn[:, :, :], b_row[:, :].unsqueeze(1).to_broadcast([P, NT, D]), ALU.mult))
            nc.vector.tensor_reduce(pb_tile[:, :], pn[:, :, :], AX.X, ALU.add).then_inc(pb_done, 1)
            for m in range(KD):
                dve.wait_ge(pw_hi_ready, m + 1)
                nc.vector.tensor_tensor(pw_all[:, m, :, S:2 * S], bank[m][:, :].rearrange("p (b s) -> p b s", b=B),
                                        pw_all[:, m, :, 0:S].bitcast(f32), ALU.subtract).then_inc(pw_lo_ready, 1)

            def evacuate(b, c, between=()):
                for (g, ks), after in zip(groups(c), tuple(between) + (None,) * KD):
                    dve.wait_ge(t_hi, G * b + g + 1)
                    n = width(c) if len(ks) == 1 else REMP
                    nc.vector.tensor_tensor(ct_lo[c % 2][:, ks[0]:ks[-1] + 1, 0:n],
                                            t_bank(g)[:, :].rearrange("p (k n) -> p k n", k=len(ks))[:, :, 0:n],
                                            ct_hi[c % 2][:, ks[0]:ks[-1] + 1, 0:n].bitcast(f32), ALU.subtract).then_inc(t_lo, 1)
                    if after:
                        after()

            def add_scores(b, par, c):
                dve.wait_ge(s_low, NC * b + c + 1)
                if c == 0 and not (isinstance(b, int) and b < 2):
                    dve.wait_ge(pt_done, 2 * (b - 1))
                nc.vector.tensor_tensor(sc[par][0:S, 512 * c:512 * c + width(c)], SB[c % 2][0:S, 0:width(c)],
                                        sc_low[c % 2][:, 0:width(c)], ALU.add).then_inc(s_ready, 1)

            def chunk_max(b, par, c):
                dve.wait_ge(s_ready, NC * b + c + 1)
                return nc.vector.reduce_max(mx4[:, c:c + 1], sc[par][0:S, 512 * c:512 * c + width(c)], AX.X)

            def split_half(b, par):
                dve.wait_ge(nat_hi_ready, act_tiles(NKT) * b + CH // 2)
                nc.vector.tensor_tensor(nat_lo[:, 0:CH // 2, :], raw[par][:, 0:CH // 2, :],
                                        nat_hi[:, 0:CH // 2, :].bitcast(f32), ALU.subtract).then_inc(nat_lo_ready[0], 1)

            def step_to(ins_, n):
                ins_.then_inc(dve_step, 1)
                dve.wait_ge(dve_step, n)

            base = steps[0]

            def max_stage(b, par):
                n = base + 3 * b
                step_to(chunk_max(b, par, 3), n + 1)
                step_to(nc.vector.reduce_max(mx[:, 0:1], mx4[:, :], AX.X), n + 2)
                step_to(nc.vector.tensor_tensor(mx[:, 1:2], mx[:, 0:1], pb[:, bass.ds(b, 1)], ALU.add), n + 3)
                if not (isinstance(b, int) and b < 2):
                    dve.wait_ge(exp_done, b - 1)
                nc.vector.tensor_tensor(nbias[par][:, :], pb[:, bass.ds(b, 1)], mx[:, 1:2], ALU.subtract).then_inc(max_ready, 1)

            def prob_parts(b):
                for h, (t0, t1) in enumerate(PT_SPLIT):
                    dve.wait_ge(pt_hi, 2 * b + h + 1)
                    nc.vector.tensor_tensor(pT[:, t0:t1, S:2 * S], PB[h][:, 0:(t1 - t0) * S].rearrange("p (j s) -> p j s", s=S),
                                            pT[:, t0:t1, 0:S].bitcast(f32), ALU.subtract).then_inc(pt_lo, 1)

            def upper_tiles(b, par):
                c = DVE_TILES[0] // CH
                dve.wait_ge(ctx_loaded[par][c], 16 * (b // 2 + 1) if isinstance(b, int) else 16 * ((b - par) // 2 + 1))
                if not (isinstance(b, int) and b == 0):
                    dve.wait_ge(pv_done, NC * (b - 1) + c + 1)
                nc.vector.tensor_copy(nat_hi[:, DVE_TILES[0]:DVE_TILES[1], :], raw[par][:, DVE_TILES[0]:DVE_TILES[1], :]).then_inc(nat_hi_dve, 1)

            def sum_values(b):
                dve.wait_ge(pv_low_ready, b + 1)
                nc.vector.tensor_tensor(pv_low[:, :], VB[0:S, :], pv_low[:, :], ALU.add).then_inc(av_sum, 1)

            def stage(b, par, scores=True, values=True, earlier=True, ahead=True):
                n, npar = b + 1, 1 - par
                if earlier:
                    sum_values(b - 1)
                if scores:
                    evacuate(n, 1, ((lambda: (prob_parts(b), upper_tiles(b, par))) if values else None,))
                else:
                    prob_parts(b)
                    upper_tiles(b, par)
                if values:
                    if earlier:
                        dve.wait_ge(av_ready, b)
                    dve.wait_ge(exp_done, b + 1)
                    nc.vector.reciprocal(rinv[:, :], rsum[par][:, :]).then_inc(rinv_ready, 1)
                if scores:
                    add_scores(n, npar, 0)
                    evacuate(n, 2)
                    chunk_max(n, npar, 0)
                    add_scores(n, npar, 1)
                    evacuate(n, 3)
                    chunk_max(n, npar, 1)
                    split_half(n, npar)
                    add_scores(n, npar, 2)
                    chunk_max(n, npar, 2)
                    add_scores(n, npar, 3)
                    max_stage(n, npar)
                    if ahead:
                        evacuate(n + 1, 0)

            dve.wait_ge(sc_zeroed, 2)
            evacuate(0, 0)
            dve.wait_ge(pb_ready, 2)
            stage(-1, 1, values=False, earlier=False)
            stage(0, 0, earlier=False)
            with dve.Fori(0, B // 2 - 2) as i:
                stage(2 * i + 1, 1)
                stage(2 * i + 2, 0)
            stage(B - 3, 1)
            stage(B - 2, 0, ahead=False)
            stage(B - 1, 1, scores=False)
            def lower_vectors(first, last):
                dve.wait_ge(avT_hi_ready, 2 if last == NT else 1)
                nc.vector.tensor_tensor(avT_lo[:, :, first * P:last * P], avT[:, :, first * P:last * P],
                                        avT_hi[:, :, first * P:last * P].bitcast(f32), ALU.subtract).then_inc(avT_lo_ready, 1)

            lower_vectors(0, NT - 1)
            for k in range(KD):
                dve.wait_ge(WT_hi_ready, k + 1)
                nc.vector.tensor_tensor(WT_lo[:, k, :], bank[k][:, :], WT_hi[:, k, :].bitcast(f32), ALU.subtract).then_inc(WT_lo_ready, 1)
            sum_values(B - 1)
            dve.wait_ge(b_loaded, 32)
            steps[0] = base + 3 * B

            def residual(t):
                dve.wait_ge(xo_done, t + 1)
                link(nc.vector.tensor_tensor(xo[:, t, :], bank[t][:, :], b_bc[:, :], ALU.add))
                nc.vector.scalar_tensor_tensor(xt[:, t, :], xo[:, t, :], 0.0, xt[:, t, :], ALU.max, ALU.add).then_inc(x1_ready, 1)

            def tile_stats(src, t):
                link(nc.vector.bn_stats(stats[:, t, :], src[:, t, :]))
                link(nc.vector.bn_aggr(mv[:, t, :], stats[:, t, :]))
                nc.vector.tensor_scalar(rstd[:, t:t + 1], mv[:, t, 1:2], EPS, None, ALU.add).then_inc(var_ready, 1)

            def normalise(dst, src, t):
                return nc.vector.tensor_scalar(dst[:, t, :], src[:, t, :], mv[:, t, 0:1], rstd[:, t:t + 1], ALU.subtract, ALU.mult)

            def gained(src, t, count):
                dve.wait_ge(rstd_ready, count)
                link(nc.vector.scalar_tensor_tensor(xn[:, t, :], src[:, t, :], mv[:, t, 0:1], gain[:, :], ALU.subtract, ALU.mult))
                nc.vector.scalar_tensor_tensor(xn[:, t, :], xn[:, t, :], rstd[:, t:t + 1], shift[:, :], ALU.mult, ALU.add).then_inc(xn_ready, 1)

            for t in range(NT):
                residual(t)
                dve.wait_ge(x1_ready, t + 1)
                tile_stats(xt, t)
                if t == 0:
                    lower_vectors(NT - 1, NT)
            nc.vector.memset(proj2[:, :], 0.0).then_inc(proj_zero, 1)
            for t in range(NT):
                dve.wait_ge(rstd_ready, 2 + t)
                link(normalise(x1n, xt, t))
                tile_stats(x1n, t)
                if t == 0:
                    dve.wait_ge(vec_loaded, 48)
                else:
                    gained(x1n, t - 1, NT + 1 + t)
            gained(x1n, NT - 1, 2 * NT + 1)

            def split_w(u):
                dve.wait_ge(*upper(u))
                nc.vector.tensor_tensor(w_lo[u % RING][:, :, :], w_raw[u % RING][:, :, :], w_hi[u % RING][:, :, :].bitcast(f32),
                                        ALU.subtract).then_inc(w_lo_ready[u % RING], 1)

            def lower_xT(n):
                for k in range(KD):
                    dve.wait_ge(xT_hi_ready, KD * n + k + 1)
                    nc.vector.tensor_tensor(xT_lo[:, k, :], bank[k][:, :], xT_hi[:, k, :].bitcast(f32), ALU.subtract).then_inc(xT_lo_ready, 1)

            dve.wait_ge(proj_hi_ready, 1)
            nc.vector.tensor_tensor(proj2_lo[:, :], proj2[:, :], proj2_hi[:, :].bitcast(f32), ALU.subtract).then_inc(proj_lo_ready, 1)
            lower_xT(0)
            split_w(0)
            nc.vector.memset(zeros[:, :], 0.0).then_inc(zeros_ready, 1)
            nc.vector.memset(v1[:, :, :, DH:DH + 1], 1.0).then_inc(v_one, 1)

            def lower_z(n):
                dve.wait_ge(z_hi_ready, n + 1)
                nc.vector.tensor_tensor(z_lo[n % 2][:, :], bank[n % 2][:, :], z_hi[n % 2][:, :].bitcast(f32), ALU.subtract).then_inc(z_lo_ready, 1)

            def negative(n):
                dve.wait_ge(f_done, n + 1)
                nc.vector.tensor_scalar(neg[n % 2][:, :], bank[2 + n % 2][:, :], 0.0, None, ALU.min).then_inc(neg_ready, 1)

            def feature(n):
                dve.wait_ge(e_ready, n + 1)
                nc.vector.scalar_tensor_tensor(phi[n // 8][:, n % 8, :], bank[2 + n % 2][:, :], 0.0, neg[n % 2][:, :],
                                               ALU.max, ALU.add).then_inc(phi_ready, 1)

            for n in range(H):
                lower_z(n)
                if n >= 1:
                    negative(n - 1)
                if n >= 1:
                    feature(n - 1)
            negative(H - 1)
            feature(H - 1)
            dve.wait_ge(mask_ready, 1)
            NG = 4 * NT

            def masked(n):
                dve.wait_ge(a_done, n + 1)
                if n >= 2:
                    dve.wait_ge(o_done, n - 1)
                nc.vector.tensor_tensor(at[n % 2][:, :, :], bank[n % 3][:, :].rearrange("p (h q) -> p h q", h=4),
                                        mask[:, :].unsqueeze(1).to_broadcast([P, 4, P]), ALU.mult).then_inc(a_ready, 1)

            def divided(n):
                t, g, s = n // 4, n // 2 % 2, n % 2
                o = bank[6 + n % 2][:, 0:4 * (DH + 1)].rearrange("p (h d) -> p h d", d=DH + 1)
                dve.wait_ge(o_done, n + 1)
                link(nc.vector.tensor_scalar(den[:, 0, :], o[:, :, DH], 1e-6, None, ALU.add))
                link(nc.vector.reciprocal(den[:, 1, :], den[:, 0, :]))
                if n % 4 == 0 and t >= 2:
                    dve.wait_ge(oT_done, 2 * (t - 1))
                dst = heads[:, t % 2, :].rearrange("p (m s d) -> p m s d", s=2, d=DH)[:, 4 * g:4 * (g + 1), s, :]
                nc.vector.tensor_tensor(dst, o[:, :, 0:DH], den[:, 1, :].unsqueeze(2).to_broadcast([P, 4, DH]), ALU.mult).then_inc(o_ready, 1)

            def lower_oT(t):
                for half in range(2):
                    dve.wait_ge(oT_hi_ready, 2 * t + half + 1)
                    nc.vector.tensor_tensor(oT_lo[:, 4 * half:4 * (half + 1), :], bank[4 + half][:, :].rearrange("p (k n) -> p k n", n=P),
                                            oT_hi[:, 4 * half:4 * (half + 1), :].bitcast(f32), ALU.subtract).then_inc(oT_lo_ready, 1)

            def attended(t):
                dve.wait_ge(ao_done, t + 1)
                nc.vector.tensor_tensor(x1n[:, t, :], x1n[:, t, :], bank[3][:, :], ALU.add).then_inc(xa_ready, 1)

            for t in range(NT):
                for n in range(4 * t, 4 * t + 4):
                    masked(n)
                    if n % 4 >= 1:
                        divided(n - 1)
                    elif t >= 1:
                        lower_oT(t - 1)
                divided(4 * t + 3)
                if t >= 1:
                    attended(t - 1)
                    dve.wait_ge(xa_ready, t)
                    tile_stats(x1n, t - 1)
            lower_oT(NT - 1)
            dve.wait_ge(vec2_loaded, 32)
            dve.wait_ge(oT_done, 2 * NT)
            for t in range(NT - 1):
                gained(x1n, t, 2 * NT + 2 + t)
            attended(NT - 1)
            dve.wait_ge(xa_ready, NT)
            tile_stats(x1n, NT - 1)
            gained(x1n, NT - 1, 2 * NT + 5)
            lower_xT(1)
            split_w(9)
            split_w(10)
            for n in range(FF // P):
                dve.wait_ge(gelu_ready, n + 1)
                if n >= 2:
                    dve.wait_ge(dn_done, n - 1)
                nc.vector.tensor_copy(gl_hi[n % 2][:, :], gl[n % 2][:, :]).then_inc(gl_hi_ready, 1)
                dve.wait_ge(gl_hi_ready, n + 1)
                nc.vector.tensor_tensor(gl_lo[n % 2][:, :], gl[n % 2][:, :], gl_hi[n % 2][:, :].bitcast(f32), ALU.subtract).then_inc(gl_lo_ready, 1)
                if n % 4 == 3 and n < FF // P - 1:
                    split_w(11 + 2 * (n // 4))
                if n % 4 == 0 and 4 <= n < FF // P - 4:
                    split_w(10 + n // 2)
                if n in (1, 2):
                    for t in range(NT):
                        last = nc.vector.tensor_tensor(xt[:, t, :], xt[:, t, :], x1n[:, t, :] if n == 1 else b2_bc[:, :], ALU.add)
                    link(last)
            for t in range(NT):
                dve.wait_ge(*((last_dn, t + 1) if t < NT - 1 else (dn_done, FF // P)))
                nc.vector.tensor_tensor(xt[:, t, :], xt[:, t, :], bank[4 + t][:, :], ALU.add).then_inc(x2_ready, 1)

            dve.wait_ge(x2_ready, NT)
            for t in range(NT):
                last = nc.vector.bn_stats(stats[:, t, :], xt[:, t, :])
            link(last)
            for t in range(NT):
                last = nc.vector.bn_aggr(mv[:, t, :], stats[:, t, :])
            link(last)
            nc.vector.tensor_scalar(rstd[:, :], mv[:, :, 1], EPS, None, ALU.add).then_inc(var_ready, 1)
            dve.wait_ge(rstd_ready, 3 * NT + 2)
            for t in range(NT):
                normalise(xn, xt, t).then_inc(xn_ready, 1)
            dve.wait_ge(index_ready, 1)
            link(nc.vector.tensor_copy(e_idx[:, :], e_int[:, :]))
            link(nc.vector.tensor_scalar(pref[:, :], e_idx[:, :], -1.0, float(E), ALU.mult, ALU.add))
            link(nc.vector.memset(chosen[:, NT, :], 0.0))
            nc.vector.memset(yb[:, 0:256], 0.0).then_inc(y_ready, 1)
            nc.vector.memset(yb[:, 256:512], 0.0).then_inc(y_stored, 1)

            def over_tokens(a):
                return a.unsqueeze(1).to_broadcast([P, NT, E])

            def over_experts(a):
                return a.unsqueeze(2).to_broadcast([P, NT, E])

            def split_e(e, j):
                if j not in POOL_UNITS:
                    dve.wait_ge(e_hi_ready[j], turn_of(e, j))
                    nc.vector.tensor_tensor(e_lo[j][:, :, :], e_raw[j][:, :, :], e_hi[j][:, :, :].bitcast(f32),
                                            ALU.subtract).then_inc(e_lo_ready[j], 1)

            for j in range(RING):
                split_e(0, j)
            dve.wait_ge(logits_done, 1)
            for t in range(NT):
                last = nc.vector.tensor_copy(logits[:, t, :], bank[4 + t][:, 0:E])
            link(last)
            for k in range(2):
                link(nc.vector.reduce_max(best[k][:, :], logits[:, :, :], AX.X))
                link(nc.vector.tensor_tensor(scr[:, :, :], logits[:, :, :], over_experts(best[k][:, :]), ALU.is_equal))
                link(nc.vector.tensor_tensor(scr[:, :, :], scr[:, :, :], over_tokens(pref[:, :]), ALU.mult))
                link(nc.vector.reduce_max(top[:, :], scr[:, :, :], AX.X))
                link(nc.vector.tensor_tensor(pick[k][:, :, :], scr[:, :, :], over_experts(top[:, :]), ALU.is_equal))
                if k == 0:
                    link(nc.vector.scalar_tensor_tensor(logits[:, :, :], pick[0][:, :, :], -3e38, logits[:, :, :], ALU.mult, ALU.add))
            nc.vector.tensor_tensor(chosen[:, 0:NT, :], pick[0][:, :, :], pick[1][:, :, :], ALU.add).then_inc(chosen_ready, 1)
            nc.vector.tensor_tensor(gap[:, :], best[1][:, :], best[0][:, :], ALU.subtract).then_inc(gap_ready, 1)
            split_e(0, 3)
            dve.wait_ge(rank_done, 1)
            nc.vector.tensor_copy(rank[:, :, :], bank[3][:, 0:NT * E].rearrange("p (t e) -> p t e", e=E))
            link(nc.vector.tensor_copy(count[:, :], bank[3][:, NT * E:(NT + 1) * E]))
            link(nc.vector.tensor_scalar(extra[:, :], count[:, :], float(P), None, ALU.is_gt))
            for n in range(2, B * S // P):
                link(nc.vector.scalar_tensor_tensor(extra[:, :], count[:, :], float(n * P), extra[:, :], ALU.is_gt, ALU.add))
            dve.wait_ge(order_ready, 2)
            link(nc.vector.tensor_tensor(scr8[:, :, :], upto[:, :, :], extra[:, :].unsqueeze(1).to_broadcast([P, E, E]), ALU.mult))
            link(nc.vector.tensor_reduce(upto_extra[:, :], scr8[:, :, :], AX.X, ALU.add))
            link(nc.vector.tensor_tensor(upto_extra[:, :], upto_extra[:, :], e_idx[:, :], ALU.add))
            link(nc.vector.tensor_tensor(first_block[:, :], upto_extra[:, :], extra[:, :], ALU.subtract))
            link(nc.vector.scalar_tensor_tensor(rank[:, :, :], over_tokens(first_block[:, :]), float(P), rank[:, :, :], ALU.mult, ALU.add))
            for k in range(2):
                link(nc.vector.tensor_tensor(scr[:, :, :], rank[:, :, :], pick[k][:, :, :], ALU.mult))
                link(nc.vector.tensor_reduce(slotf[k][:, :], scr[:, :, :], AX.X, ALU.add))
                nc.vector.tensor_copy(slot_of[k][:, :], slotf[k][:, :]).then_inc(slots_ready, 1)
            nc.vector.tensor_copy(blocks[:, 0, :], first_block[:, :]).then_inc(slots_ready, 1)
            nc.vector.tensor_copy(blocks[:, 1, :], upto_extra[:, :]).then_inc(slots_ready, 1)
            dve.wait_ge(gap_exp, 1)
            link(nc.vector.tensor_scalar(gap[:, :], gsum[:, :], 1.0, None, ALU.add))
            link(nc.vector.reciprocal(gate[0][:, :], gap[:, :]))
            link(nc.vector.tensor_tensor(gate[1][:, :], gate[0][:, :], gsum[:, :], ALU.mult))

            def lower_rows(b):
                dve.wait_ge(xgT_hi_ready, b + 1)
                nc.vector.tensor_tensor(xgT_lo[:, :, :], bank[7][:, :].rearrange("p (k n) -> p k n", n=P), xgT_hi[:, :, :].bitcast(f32),
                                        ALU.subtract).then_inc(xgT_lo_ready, 1)

            def hidden(b, half):
                dve.wait_ge(silu_ready, 2 * b + half + 1)
                dve.wait_ge(unit_done[2 * half + 1], b + 1)
                nc.vector.tensor_tensor(hm[half][:, :], bank[2 * half + 1][:, :], sg[half][:, :], ALU.mult).then_inc(hm_ready, 1)

            def lower_hidden(b, half):
                dve.wait_ge(hmT_hi_ready, 2 * b + half + 1)
                nc.vector.tensor_tensor(hmT_lo[half][:, :, :], bank[4 + half][:, :].rearrange("p (k n) -> p k n", n=P),
                                        hmT_hi[half][:, :, :].bitcast(f32), ALU.subtract).then_inc(hmT_lo_ready, 1)

            def expert_block(b, e, again=False, last=False):
                def split(j):
                    if not again and not last:
                        split_e(e + 1, j)

                hidden(b, 0)
                split(0)
                lower_hidden(b, 0)
                hidden(b, 1)
                if not last:
                    lower_rows(b + 1)
                split(1)
                lower_hidden(b, 1)
                split(2)
                split(3)

            lower_rows(0)
            dve.wait_ge(slots_ready, 4)
            with dve.Fori(0, E - 1) as e:
                first_b, last_b = expert_blocks(dve, e)
                with dve.If(first_b < last_b):
                    with dve.Fori(first_b, last_b) as b:
                        expert_block(b, e, again=True)
                expert_block(last_b, e)
            first_b, last_b = expert_blocks(dve, E - 1)
            with dve.If(first_b < last_b):
                with dve.Fori(first_b, last_b) as b:
                    expert_block(b, E - 1, again=True)
            expert_block(last_b, E - 1, last=True)
            for t in range(NT):
                dve.wait_ge(gathered[t], 32)
                for k in range(2):
                    mm = nc.vector.scalar_tensor_tensor(xt[:, t, :], yt[k][:, t, :], gate[k][:, t:t + 1], xt[:, t, :], ALU.mult, ALU.add)
                    if k == 0:
                        link(mm)
                mm.then_inc(xo_ready, 1)

        @block.tensor
        def _(pe):
            def product(dst, left, right, first=True, last=True):
                n = len(left)
                for k, ((lh, ll), (rh, rl)) in enumerate(zip(left, right)):
                    nc.tensor.matmul(dst, lh, rh, start=first and k == 0, stop=False)
                    nc.tensor.matmul(dst, lh, rl, start=False, stop=False)
                    mm = nc.tensor.matmul(dst, ll, rh, start=False, stop=last and k == n - 1)
                return mm

            def turn(dst, src, waited):
                if waited:
                    return nc.tensor.matmul(dst, src, ident[0:S, 0:S], start=True, stop=True)
                return nc.tensor.transpose(dst, src, ident[0:S, 0:S])

            pe.wait_ge(const_ready, 1)
            pe.wait_ge(pn_ready, NT)
            for k in range(KD):
                for t in range(NT):
                    mm = nc.tensor.transpose(bank[k][:, t * P:(t + 1) * P], pn[:, t, k * P:(k + 1) * P], ident[:, :])
                mm.then_inc(pnT_done, 1)
            pe.wait_ge(W_lo_ready, 1)
            pe.wait_ge(pnT_lo_ready, KD)
            for m in range(KD):
                product(bank[m][:, :], [(W_hi[:, k, m * P:(m + 1) * P], W_lo[:, k, m * P:(m + 1) * P]) for k in range(KD)],
                        [(pnT_hi[:, k, :], pnT_lo[:, k, :]) for k in range(KD)]).then_inc(pwT_done, 1)
            pe.wait_ge(pw_lo_ready, KD)

            def transposes(b, par, c, some=slice(None)):
                pe.wait_ge(ctx_loaded[par][c], 16 * (b // 2 + 1) if isinstance(b, int) else 16 * ((b - par) // 2 + 1))
                tiles = range(CH * c, min(CH * (c + 1), NKT))
                for g, ks in groups(c)[some]:
                    before = t_before(b, g)
                    if before is not None:
                        pe.wait_ge(t_lo, before)
                    for k in ks:
                        for n, j in enumerate(tiles):
                            rows = P if j < FULL else REMP
                            at = (k - ks[0]) * P + n * P
                            mm = nc.tensor.transpose(t_bank(g)[:, at:at + rows], raw[par][0:rows, j, k * P:(k + 1) * P],
                                                     ident[0:rows, 0:rows])
                    mm.then_inc(t_done, 1)

            def scores(b, par, c):
                g_last = groups(c)[-1][0]
                pe.wait_ge(t_lo, G * b + g_last + 1)
                if c >= 2:
                    pe.wait_ge(s_ready, NC * b + c - 1)
                elif not (isinstance(b, int) and b == 0):
                    pe.wait_ge(s_ready, NC * (b - 1) + NC - 2 + c + 1)
                n = width(c) if c < NC - 1 else REMP
                for k in range(KD):
                    nc.tensor.matmul(SB[c % 2][:, 0:n], pw[par][:, k, :], ct_hi[c % 2][:, k, 0:n], start=k == 0, stop=False)
                    mm = nc.tensor.matmul(SB[c % 2][:, 0:n], pw[par][:, k, :], ct_lo[c % 2][:, k, 0:n], start=False, stop=k == KD - 1)
                mm.then_inc(qk_done, 1)

            def av_transposes(b):
                pe.wait_ge(av_ready, b + 1)
                for k in range(KD):
                    mm = turn(VB[:, k * S:(k + 1) * S], av[:, k * P:(k + 1) * P], k == 0)
                mm.then_inc(avt_done, 1)

            def prob_transposes(b, par):
                pe.wait_ge(exp_done, b + 1)
                for h, (t0, t1) in enumerate(PT_SPLIT):
                    if not (isinstance(b, int) and b == 0):
                        pe.wait_ge(pt_lo, 2 * (b - 1) + h + 1)
                    for j in range(t0, t1):
                        mm = turn(PB[h][:, (j - t0) * S:(j - t0 + 1) * S], sc[par][:, j * P:(j + 1) * P], j == t0)
                    mm.then_inc(pt_done, 1)

            def values_of(b, c):
                if c == 0 and not (isinstance(b, int) and b == 0):
                    pe.wait_ge(avt_ready, b)
                for h, (t0, t1) in enumerate(PT_SPLIT):
                    if CH * c == t0:
                        pe.wait_ge(pt_lo, 2 * b + h + 1)
                pe.wait_ge(nat_lo_ready[c], LO_STEPS[c] * (b + 1))
                for j in range(CH * c, min(CH * (c + 1), NKT)):
                    nc.tensor.matmul(VB[:, :], pT[:, j, :], nat_hi[:, j, :], start=j == 0, stop=False)
                    mm = nc.tensor.matmul(VB[:, :], pT[:, j, :], nat_lo[:, j, :], start=False, stop=j == NKT - 1)
                mm.then_inc(pv_done, 1)

            def stage(b, par, scores_too=True, values=True, earlier=True, ahead=True):
                n, npar = b + 1, 1 - par
                if values:
                    prob_transposes(b, par)
                if scores_too:
                    transposes(n, npar, 1)
                    pe.wait_ge(pw_ready, n + 1)
                    scores(n, npar, 0)
                if earlier:
                    av_transposes(b - 1)
                if scores_too:
                    transposes(n, npar, 2)
                    scores(n, npar, 1)
                if values:
                    values_of(b, 0)
                if scores_too:
                    transposes(n, npar, 3)
                    scores(n, npar, 2)
                if values:
                    values_of(b, 1)
                if scores_too:
                    scores(n, npar, 3)
                    if ahead:
                        transposes(n + 1, par, 0, slice(0, 3))
                if values:
                    values_of(b, 2)
                if scores_too and ahead:
                    transposes(n + 1, par, 0, slice(3, 4))
                if values:
                    values_of(b, 3)

            transposes(0, 0, 0)
            stage(-1, 1, values=False, earlier=False)
            stage(0, 0, earlier=False)
            with pe.Fori(0, B // 2 - 2) as i:
                stage(2 * i + 1, 1)
                stage(2 * i + 2, 0)
            stage(B - 3, 1)
            stage(B - 2, 0, ahead=False)
            prob_transposes(B - 1, 1)
            pe.wait_ge(W_loaded, 32)
            pe.wait_ge(t_lo, G * B)
            pe.wait_ge(s_ready, NC * B)
            for k in range(KD):
                for m in range(KD):
                    mm = nc.tensor.transpose(bank[k][:, m * P:(m + 1) * P], We[:, m, k * P:(k + 1) * P], ident[:, :])
                mm.then_inc(WT_done, 1)
            av_transposes(B - 2)
            for c in range(NC):
                values_of(B - 1, c)
            pe.wait_ge(WT_lo_ready, KD)
            pe.wait_ge(avT_lo_ready, 1)
            for t in range(NT):
                if t == 1:
                    av_transposes(B - 1)
                if t == NT - 1:
                    pe.wait_ge(avT_lo_ready, 2)
                product(bank[t][:, :], [(avT_hi[:, k, t * P:(t + 1) * P], avT_lo[:, k, t * P:(t + 1) * P]) for k in range(KD)],
                        [(WT_hi[:, k, :], WT_lo[:, k, :]) for k in range(KD)]).then_inc(xo_done, 1)

            def parts(u):
                return w_hi[u % RING], w_lo[u % RING]

            def transpose_xn(n):
                for t in range(NT):
                    pe.wait_ge(xn_ready, NT * n + t + 1)
                    for k in range(KD):
                        mm = nc.tensor.transpose(bank[k][:, t * P:(t + 1) * P], xn[:, t, k * P:(k + 1) * P], ident[:, :])
                        if t == NT - 1:
                            mm.then_inc(xT_done, 1)
                pe.wait_ge(xT_lo_ready, KD * (n + 1))

            xT = [(xT_hi[:, k, :], xT_lo[:, k, :]) for k in range(KD)]

            def columns(u, m):
                hi, lo = parts(u)
                return [(hi[:, k, m * P:(m + 1) * P], lo[:, k, m * P:(m + 1) * P]) for k in range(KD)]

            def rows(u):
                hi, lo = parts(u)
                return [(hi[:, k, :], lo[:, k, :]) for k in range(KD)]

            pe.wait_ge(x1_ready, NT)
            transpose_xn(0)

            def features(n):
                pe.wait_ge(z_lo_ready, n + 1)
                if n >= 2:
                    pe.wait_ge(phi_ready, n - 1)
                product(bank[2 + n % 2][:, :], [(proj2_hi[:, :], proj2_lo[:, :])], [(z_hi[n % 2][:, :], z_lo[n % 2][:, :])]).then_inc(f_done, 1)

            pe.wait_ge(proj_lo_ready, 1)
            for n in range(H):
                u = n // 4
                if n % 4 == 0:
                    pe.wait_ge(*lower(u))
                if n >= 2:
                    pe.wait_ge(z_lo_ready, n - 1)
                product(bank[n % 2][:, :], columns(u, n % 4), xT).then_inc(z_done, 1)
                if n >= 1:
                    features(n - 1)
            features(H - 1)
            for u in range(2):
                pe.wait_ge(*lower(4 + u))
                for t in range(NT):
                    n = NT * u + t
                    if n >= 2:
                        pe.wait_ge(v_ready, n - 1)
                    product(bank[4 + n % 2][:, :], [(hi[:, t * P:(t + 1) * P], lo[:, t * P:(t + 1) * P]) for hi, lo in xT],
                            rows(4 + u)).then_inc(v_done, 1)
            pe.wait_ge(v_ready, 2 * NT)
            pe.wait_ge(v_one, 1)
            pe.wait_ge(phi_ready, H)

            def weights(n):
                t, g, s = n // 4, n // 2 % 2, n % 2
                if n >= 3:
                    pe.wait_ge(a_ready, n - 2)
                half = slice(DH * s, DH * (s + 1))
                for m in range(4):
                    k, q = (phi[i][half, 4 * g + m, t * P:(t + 1) * P] for i in (1, 0))
                    mm = nc.tensor.matmul(bank[n % 3][:, m * P:(m + 1) * P], k, q, start=True, stop=True)
                mm.then_inc(a_done, 1)

            def weighted(n):
                t, g, s = n // 4, n // 2 % 2, n % 2
                pe.wait_ge(a_ready, n + 1)
                if n >= 2:
                    pe.wait_ge(o_ready, n - 1)
                for m in range(4):
                    head = 2 * (4 * g + m) + s
                    mm = nc.tensor.matmul(bank[6 + n % 2][:, m * (DH + 1):(m + 1) * (DH + 1)], at[n % 2][:, m, :], v1[:, t, head, :],
                                          start=True, stop=True)
                mm.then_inc(o_done, 1)

            def heads_transposed(t):
                pe.wait_ge(o_ready, 4 * t + 4)
                for half in range(2):
                    if t >= 1:
                        pe.wait_ge(oT_lo_ready, 2 * t - 1 + half)
                    for k in range(4):
                        at_ = (4 * half + k) * P
                        mm = nc.tensor.transpose(bank[4 + half][:, k * P:(k + 1) * P], heads[:, t % 2, at_:at_ + P], ident[:, :])
                    mm.then_inc(oT_done, 1)

            def projected(t, part):
                if part == 0:
                    pe.wait_ge(oT_lo_ready, 2 * t + 2)
                    pe.wait_ge(*lower(6))
                    pe.wait_ge(*lower(7))
                    if t >= 1:
                        pe.wait_ge(xa_ready, t)
                some = slice(2 * part, 2 * part + 2)
                mm = product(bank[3][:, :], [(oT_hi[:, k, :], oT_lo[:, k, :]) for k in range(HD // P)][some],
                             (rows(6) + rows(7))[some], part == 0, part == 3)
                if part == 3:
                    mm.then_inc(ao_done, 1)

            for t in range(NT):
                weights(4 * t)
                if t >= 1:
                    heads_transposed(t - 1)
                weights(4 * t + 1)
                if t == 0:
                    weights(2)
                for i in range(4):
                    weighted(4 * t + i)
                    if t >= 1:
                        projected(t - 1, i)
                    if i < 2 and not t == i == 0:
                        weights(4 * t + i + 2)
            heads_transposed(NT - 1)
            for part in range(4):
                projected(NT - 1, part)
            pe.wait_ge(xa_ready, NT)
            transpose_xn(1)

            def down(n):
                if n % 4 == 0:
                    pe.wait_ge(*lower(9 + 2 * (n // 4)))
                hi, lo = parts(9 + 2 * (n // 4))
                pe.wait_ge(gl_lo_ready, n + 1)
                for t in range(NT):
                    left = (gl_hi[n % 2][:, t * P:(t + 1) * P], gl_lo[n % 2][:, t * P:(t + 1) * P])
                    mm = product(bank[4 + t][:, :], [left], [(hi[:, n % 4, :], lo[:, n % 4, :])], n == 0, n == FF // P - 1)
                    if n == FF // P - 1 and t < NT - 1:
                        mm.then_inc(last_dn, 1)
                mm.then_inc(dn_done, 1)

            for n in range(FF // P):
                u = 8 + 2 * (n // 4)
                if n % 4 == 0:
                    pe.wait_ge(*lower(u))
                if n >= 2:
                    pe.wait_ge(gelu_ready, n - 1)
                product(bank[n % 2][:, :], columns(u, n % 4), xT).then_inc(up_done, 1)
                if n >= 1:
                    down(n - 1)
            down(FF // P - 1)

            pe.wait_ge(gelu_ready, FF // P)
            for t in range(NT):
                pe.wait_ge(xn_ready, 2 * NT + t + 1)
                for k in range(KD):
                    mm = nc.tensor.transpose(bank[k][:, t * P:(t + 1) * P], xn[:, t, k * P:(k + 1) * P], ident[:, :])
                    if t == NT - 1:
                        mm.then_inc(xT_done, 1)
            pe.wait_ge(router_loaded, 16)
            for k in range(KD):
                pe.wait_ge(xT32_ready, k + 1)
                for t in range(NT):
                    mm = nc.tensor.matmul(bank[4 + t][:, 0:E], xT32[:, k, t * P:(t + 1) * P], w_router[:, k, :],
                                          start=k == 0, stop=k == KD - 1)
            mm.then_inc(logits_done, 1)
            pe.wait_ge(chosen_ready, 1)
            pe.wait_ge(order_ready, 2)
            nc.tensor.matmul(bank[3][:, 0:(NT + 1) * E], before[:, :], chosen[:, :, :], start=True, stop=False)
            for m in range(NT):
                mm = nc.tensor.matmul(bank[3][:, (m + 1) * E:(NT + 1) * E], ones[:, :], chosen[:, m:m + 1, :].to_broadcast([P, NT - m, E]),
                                      start=False, stop=m == NT - 1)
            mm.then_inc(rank_done, 1)

            def rows_transposed(b):
                pe.wait_ge(xg_loaded, 16 * (b + 1))
                for k in range(KD):
                    mm = nc.tensor.transpose(bank[7][:, k * P:(k + 1) * P], xg[:, k * P:(k + 1) * P], ident[:, :])
                mm.then_inc(xgT_done, 1)

            def unit_rows(j):
                return [(e_hi[j][:, k, :], e_lo[j][:, k, :]) for k in range(KD)]

            def up(e, j):
                pe.wait_ge(e_lo_ready[j], turn_of(e, j))
                product(bank[j][:, :], [(xgT_hi[:, k, :], xgT_lo[:, k, :]) for k in range(KD)], unit_rows(j)).then_inc(unit_done[j], 1)

            def hidden_transposed(b, half):
                pe.wait_ge(hm_ready, 2 * b + half + 1)
                for k in range(4):
                    mm = nc.tensor.transpose(bank[4 + half][:, k * P:(k + 1) * P], hm[half][:, k * P:(k + 1) * P], ident[:, :])
                mm.then_inc(hmT_done, 1)

            def down_half(b, e, half):
                pe.wait_ge(e_lo_ready[4 + half], turn_of(e, 4 + half))
                pe.wait_ge(hmT_lo_ready, 2 * b + half + 1)
                product(bank[6][:, :], [(hmT_hi[half][:, k, :], hmT_lo[half][:, k, :]) for k in range(4)], unit_rows(4 + half),
                        half == 0, half == 1).then_inc(unit_done[4 + half], 1)

            def expert_block(b, e, again=False, last=False):
                up(e, 1)
                up(e, 2)
                hidden_transposed(b, 0)
                up(e, 3)
                if not last:
                    rows_transposed(b + 1)
                pe.wait_ge(y_ready, b + 1)
                down_half(b, e, 0)
                hidden_transposed(b, 1)
                if not last:
                    pe.wait_ge(xgT_lo_ready, b + 2)
                    up(e if again else e + 1, 0)
                down_half(b, e, 1)

            rows_transposed(0)
            pe.wait_ge(xgT_lo_ready, 1)
            up(0, 0)
            pe.wait_ge(slots_ready, 4)
            with pe.Fori(0, E - 1) as e:
                first_b, last_b = expert_blocks(pe, e)
                with pe.If(first_b < last_b):
                    with pe.Fori(first_b, last_b) as b:
                        expert_block(b, e, again=True)
                expert_block(last_b, e)
            first_b, last_b = expert_blocks(pe, E - 1)
            with pe.If(first_b < last_b):
                with pe.Fori(first_b, last_b) as b:
                    expert_block(b, E - 1, again=True)
            expert_block(last_b, E - 1, last=True)


def kernel(**inputs):
    import numpy as _np
    import concourse.bacc as _bacc
    from concourse import mybir as _mybir
    from concourse.bass_utils import run_bass_kernel_spmd as _run

    nc = _bacc.Bacc("TRN2", target_bir_lowering=False, num_devices=1)
    arrays, args = {}, {}
    for name in inputs:
        a = _np.ascontiguousarray(inputs[name])
        arrays[f"in_{name}_dram"] = a
        args[name] = nc.dram_tensor(f"in_{name}_dram", a.shape, _mybir.dt.from_np(a.dtype), kind="ExternalInput").ap()
    out = nc.dram_tensor("out_0_dram", inputs["x"].shape, _mybir.dt.float32, kind="ExternalOutput").ap()
    perceiver_block(nc, args, out)
    r = _run(nc, [arrays], core_ids=[0])
    return r.results[0]["out_0_dram"]
```
